# Optimizing a Trainium2 kernel written in Bass

```python
import numpy as np
import jax
import jax.numpy as jnp

def _softmax(x, axis=-1):
    return jax.nn.softmax(x, axis=axis)

def _gelu(x):
    return jax.nn.gelu(x, approximate=True)

def _silu(x):
    return jax.nn.silu(x)

def _sigmoid(x):
    return jax.nn.sigmoid(x)

def _layernorm(x, axis=-1, eps=1e-05):
    m = jnp.mean(x, axis=axis, keepdims=True)
    v = jnp.var(x, axis=axis, keepdims=True)
    return (x - m) / jnp.sqrt(v + eps)

def _scatter_add(tgt, idx, src, axis=0):
    return tgt.at[idx].add(src)

def _segment_sum(src, seg, n):
    return jax.ops.segment_sum(src, seg, n)
kernel_name = 'mk_adaln_ffn_d1_seqx_r8_2448a5'

def setup_inputs(seed: int=0):
    np.random.seed(seed)
    _w = jnp.asarray

    def _rec_inputs():
        import jax
        import jax.numpy as jnp
        _rk = jax.random.key(seed)
        x = -0.0002928 + 1 * jax.random.normal(jax.random.fold_in(_rk, 1), (32, 128, 128), jnp.float32)
        _lenS = 128 - jax.random.randint(jax.random.fold_in(_rk, 7), (32,), 0, max(1, 128 // 4) + 1, jnp.int32)
        _lenS2 = 128 - jax.random.randint(jax.random.fold_in(_rk, 8), (32,), 0, max(1, 128 // 4) + 1, jnp.int32)
        fside_BxS_0 = 0.0061147 + 1.02565 * jax.random.normal(jax.random.fold_in(_rk, 12), (32, 128), jnp.float32)
        itok_BxSxS_0_4 = jax.random.randint(jax.random.fold_in(_rk, 13), (32, 128, 128), 0, 5, jnp.int32)
        fside_BxSxS_0 = -3.24666e-05 + 0.0312493 * jax.random.normal(jax.random.fold_in(_rk, 14), (32, 128, 128), jnp.float32)
        cond_2048 = -4.62462e-05 + 0.0441849 * jax.random.normal(jax.random.fold_in(_rk, 16), (32, 256), jnp.float32)
        _validS = jnp.arange(128)[None, :] < _lenS[:, None]
        _validS2 = jnp.arange(128)[None, :] < _lenS2[:, None]
        _causal = jnp.tril(jnp.ones((128, 128), dtype=bool))
        mask_BxS_ff1 = jnp.where(jnp.ones((32, 128), dtype=bool), 1.0, 0.0).astype(jnp.float32)
        mask_BxS_ff0 = jnp.where(jnp.ones((32, 128), dtype=bool), 0.0, -1000000000.0).astype(jnp.float32)
        return (x, fside_BxS_0, itok_BxSxS_0_4, fside_BxSxS_0, cond_2048, mask_BxS_ff1, mask_BxS_ff0)
    x, fside_BxS_0, itok_BxSxS_0_4, fside_BxSxS_0, cond_2048, mask_BxS_ff1, mask_BxS_ff0 = _rec_inputs()

    def _L0_cond_setup():
        import jax, jax.numpy as jnp
        import numpy as np
        B, N, D = (4, 128, 128)
        T_ITER = 4
        E_TYPES = 4
        ALPHA = 0.2

        def _lin_w(key, out_f, in_f):
            bound = float(np.sqrt(3.0 / ((in_f + out_f) / 2.0)))
            return jax.random.uniform(key, (out_f, in_f), minval=-bound, maxval=bound, dtype=jnp.float32)

        def _lin(x, w, b):
            return x @ w.T + b

        def _qdgat_forward(ents, ent_mask, q_encoding, adj, types, init_mem, w_qin, b_qin, w_qt, b_qt, w_pl, b_pl, w_pc, b_pc, w_q, b_q, w_k, b_k, w_v, b_v, w_pk, b_pk, w_pv, b_pv, wes, w_mu, b_mu, w_cb, b_cb):
            d = ents.shape[-1]
            x_loc = ents
            x_ctx = jnp.broadcast_to(init_mem, ents.shape)
            var_drop = ent_mask[:, :, None]
            adj_pos = adj > 0
            q_base = jax.nn.elu(_lin(q_encoding, w_qin, b_qin))
            n_types = wes.shape[0] + 1
            for t in range(T_ITER):
                cmd = _lin(q_base, w_qt[t], b_qt[t])
                xc = x_ctx * var_drop
                pl = _lin(x_loc, w_pl, b_pl)
                pc = _lin(xc, w_pc, b_pc)
                x_joint = jnp.concatenate([x_loc, xc, pl * pc], axis=-1)
                q = _lin(x_joint, w_q, b_q)
                k = _lin(x_joint, w_k, b_k) * _lin(cmd, w_pk, b_pk)[:, None, :]
                v = _lin(x_joint, w_v, b_v) * _lin(cmd, w_pv, b_pv)[:, None, :]
                edge_score = jnp.zeros(adj.shape, jnp.float32)
                for i in range(n_types):
                    if types >> i & 1 == 1:
                        w1, w2 = (wes[i - 1, :d], wes[i - 1, d:])
                        s = (q @ w1)[:, :, None] + (k @ w2)[:, None, :]
                        edge_score = edge_score + jnp.where(adj == i, s, 0.0)
                e = jnp.where(edge_score > 0, edge_score, ALPHA * edge_score)
                logits = jnp.where(adj_pos, e, jnp.float32(-9000000000000000.0))
                prob = jax.nn.softmax(logits, axis=-1)
                message = jnp.einsum('bij,bjd->bid', prob, v)
                x_ctx = _lin(jnp.concatenate([xc, message], axis=-1), w_mu, b_mu)
            return _lin(jnp.concatenate([x_loc, x_ctx], axis=-1), w_cb, b_cb)
        key = jax.random.key(seed)
        ks = jax.random.split(key, 32)
        inp = {}
        inp['ents'] = jax.random.normal(ks[0], (B, N, D), jnp.float32)
        inp['ent_mask'] = jnp.ones((B, N), jnp.float32)
        inp['q_encoding'] = jax.random.normal(ks[1], (B, D), jnp.float32)
        inp['adj'] = jax.random.randint(ks[2], (B, N, N), 0, E_TYPES + 1, dtype=jnp.int32)
        inp['types'] = 30
        inp['init_mem'] = jax.random.normal(ks[3], (1, D), jnp.float32)
        inp['w_qin'] = _lin_w(ks[4], D, D)
        inp['b_qin'] = jnp.zeros((D,), jnp.float32)
        inp['w_qt'] = jnp.stack([_lin_w(ks[5 + t], D, D) for t in range(T_ITER)])
        inp['b_qt'] = jnp.zeros((T_ITER, D), jnp.float32)
        inp['w_pl'] = _lin_w(ks[9], D, D)
        inp['b_pl'] = jnp.zeros((D,), jnp.float32)
        inp['w_pc'] = _lin_w(ks[10], D, D)
        inp['b_pc'] = jnp.zeros((D,), jnp.float32)
        inp['w_q'] = _lin_w(ks[11], D, 3 * D)
        inp['b_q'] = jnp.zeros((D,), jnp.float32)
        inp['w_k'] = _lin_w(ks[12], D, 3 * D)
        inp['b_k'] = jnp.zeros((D,), jnp.float32)
        inp['w_v'] = _lin_w(ks[13], D, 3 * D)
        inp['b_v'] = jnp.zeros((D,), jnp.float32)
        inp['w_pk'] = _lin_w(ks[14], D, D)
        inp['b_pk'] = jnp.zeros((D,), jnp.float32)
        inp['w_pv'] = _lin_w(ks[15], D, D)
        inp['b_pv'] = jnp.zeros((D,), jnp.float32)
        wb = 1.414 * float(np.sqrt(6.0 / (2 * D + 1)))
        inp['wes'] = jax.random.uniform(ks[16], (E_TYPES, 2 * D), minval=-wb, maxval=wb, dtype=jnp.float32)
        inp['w_mu'] = _lin_w(ks[17], D, 2 * D)
        inp['b_mu'] = jnp.zeros((D,), jnp.float32)
        inp['w_cb'] = _lin_w(ks[18], D, 2 * D)
        inp['b_cb'] = jnp.zeros((D,), jnp.float32)
        return inp
    _L0_cond_all = _L0_cond_setup()
    _L0_cond_in = {k: v for k, v in _L0_cond_all.items() if k in ('init_mem', 'w_qin', 'b_qin', 'w_pl', 'b_pl', 'w_pc', 'b_pc', 'w_q', 'b_q', 'w_k', 'b_k', 'w_v', 'b_v', 'w_pk', 'b_pk', 'w_pv', 'b_pv', 'w_mu', 'b_mu', 'w_cb', 'b_cb')}
    del _L0_cond_all

    def _L0_ffn_setup():
        import jax, jax.numpy as jnp
        import numpy as np
        D = 128
        H = 16
        FF = 512
        E = 8
        K = 2
        EH = 128
        B, S = (2, 256)
        EPS = 1e-05

        def rmsnorm(x, w):
            v = jnp.mean(jnp.square(x), axis=-1, keepdims=True)
            return x * jax.lax.rsqrt(v + EPS) * w

        def _dense_path(x, wq, wk, wv, wo, w1, w2, w3, attn_norm_w, ff_norm_w):
            b, s, d = x.shape
            hd = d // H
            q = (x @ wq).reshape(b, s, H, hd)
            k = (x @ wk).reshape(b, s, H, hd)
            v = (x @ wv).reshape(b, s, H, hd)
            scores = jnp.einsum('bqhd,bkhd->bhqk', q, k) / np.sqrt(hd).astype(np.float32)
            causal = jnp.tril(jnp.ones((s, s), bool))
            scores = jnp.where(causal, scores, jnp.finfo(scores.dtype).min)
            attn = jax.nn.softmax(scores, axis=-1)
            o = jnp.einsum('bhqk,bkhd->bqhd', attn, v).reshape(b, s, d)
            h = x + rmsnorm(o @ wo, attn_norm_w)
            ffn = jax.nn.silu(h @ w1) * (h @ w3) @ w2
            return h + rmsnorm(ffn, ff_norm_w)

        def _sparse_path(x, router_w, ew1, ew2, ew3, moe_norm_w):
            b, s, d = x.shape
            xt = x.reshape(-1, d)
            probs = jax.nn.softmax(xt @ router_w, axis=-1)
            topw, topi = jax.lax.top_k(probs, K)
            g = jax.nn.silu(jnp.einsum('td,edh->eth', xt, ew1)) * jnp.einsum('td,edh->eth', xt, ew3)
            eo = jnp.einsum('eth,ehd->ted', g, ew2)
            sel = jnp.take_along_axis(eo, topi[:, :, None], axis=1)
            moe_out = jnp.sum(topw[:, :, None] * sel, axis=1).reshape(b, s, d)
            return rmsnorm(moe_out, moe_norm_w)
        key = jax.random.key(seed)
        ks = jax.random.split(key, 16)
        s = 0.02
        return {'x': jax.random.normal(ks[0], (B, S, D), jnp.float32), 'wq': jax.random.normal(ks[1], (D, D), jnp.float32) * s, 'wk': jax.random.normal(ks[2], (D, D), jnp.float32) * s, 'wv': jax.random.normal(ks[3], (D, D), jnp.float32) * s, 'wo': jax.random.normal(ks[4], (D, D), jnp.float32) * s, 'w1': jax.random.normal(ks[5], (D, FF), jnp.float32) * s, 'w2': jax.random.normal(ks[6], (FF, D), jnp.float32) * s, 'w3': jax.random.normal(ks[7], (D, FF), jnp.float32) * s, 'attn_norm_w': jnp.ones((D,), jnp.float32), 'ff_norm_w': jnp.ones((D,), jnp.float32), 'moe_norm_w': jnp.ones((D,), jnp.float32), 'router_w': jax.random.normal(ks[8], (D, E), jnp.float32) * s, 'ew1': jax.random.normal(ks[9], (E, D, EH), jnp.float32) * s, 'ew2': jax.random.normal(ks[10], (E, EH, D), jnp.float32) * s, 'ew3': jax.random.normal(ks[11], (E, D, EH), jnp.float32) * s}
    _L0_ffn_all = _L0_ffn_setup()
    _L0_ffn_in = {k: v for k, v in _L0_ffn_all.items() if k in ('wq', 'wk', 'wv', 'wo', 'w1', 'w2', 'w3', 'attn_norm_w', 'ff_norm_w', 'moe_norm_w', 'router_w', 'ew1', 'ew2', 'ew3')}
    del _L0_ffn_all
    return {'x': x, 'fside_BxS_0': fside_BxS_0, 'itok_BxSxS_0_4': itok_BxSxS_0_4, 'fside_BxSxS_0': fside_BxSxS_0, 'cond_2048': cond_2048, 'mask_BxS_ff1': mask_BxS_ff1, 'mask_BxS_ff0': mask_BxS_ff0, 'L0_cond_init_mem': _L0_cond_in['init_mem'], 'L0_cond_w_qin': _L0_cond_in['w_qin'], 'L0_cond_b_qin': _L0_cond_in['b_qin'], 'L0_cond_w_pl': _L0_cond_in['w_pl'], 'L0_cond_b_pl': _L0_cond_in['b_pl'], 'L0_cond_w_pc': _L0_cond_in['w_pc'], 'L0_cond_b_pc': _L0_cond_in['b_pc'], 'L0_cond_w_q': _L0_cond_in['w_q'], 'L0_cond_b_q': _L0_cond_in['b_q'], 'L0_cond_w_k': _L0_cond_in['w_k'], 'L0_cond_b_k': _L0_cond_in['b_k'], 'L0_cond_w_v': _L0_cond_in['w_v'], 'L0_cond_b_v': _L0_cond_in['b_v'], 'L0_cond_w_pk': _L0_cond_in['w_pk'], 'L0_cond_b_pk': _L0_cond_in['b_pk'], 'L0_cond_w_pv': _L0_cond_in['w_pv'], 'L0_cond_b_pv': _L0_cond_in['b_pv'], 'L0_cond_w_mu': _L0_cond_in['w_mu'], 'L0_cond_b_mu': _L0_cond_in['b_mu'], 'L0_cond_w_cb': _L0_cond_in['w_cb'], 'L0_cond_b_cb': _L0_cond_in['b_cb'], 'L0_ffn_wq': _L0_ffn_in['wq'], 'L0_ffn_wk': _L0_ffn_in['wk'], 'L0_ffn_wv': _L0_ffn_in['wv'], 'L0_ffn_wo': _L0_ffn_in['wo'], 'L0_ffn_w1': _L0_ffn_in['w1'], 'L0_ffn_w2': _L0_ffn_in['w2'], 'L0_ffn_w3': _L0_ffn_in['w3'], 'L0_ffn_attn_norm_w': _L0_ffn_in['attn_norm_w'], 'L0_ffn_ff_norm_w': _L0_ffn_in['ff_norm_w'], 'L0_ffn_moe_norm_w': _L0_ffn_in['moe_norm_w'], 'L0_ffn_router_w': _L0_ffn_in['router_w'], 'L0_ffn_ew1': _L0_ffn_in['ew1'], 'L0_ffn_ew2': _L0_ffn_in['ew2'], 'L0_ffn_ew3': _L0_ffn_in['ew3']}

def reference(x, fside_BxS_0, itok_BxSxS_0_4, fside_BxSxS_0, cond_2048, mask_BxS_ff1, mask_BxS_ff0, L0_cond_init_mem, L0_cond_w_qin, L0_cond_b_qin, L0_cond_w_pl, L0_cond_b_pl, L0_cond_w_pc, L0_cond_b_pc, L0_cond_w_q, L0_cond_b_q, L0_cond_w_k, L0_cond_b_k, L0_cond_w_v, L0_cond_b_v, L0_cond_w_pk, L0_cond_b_pk, L0_cond_w_pv, L0_cond_b_pv, L0_cond_w_mu, L0_cond_b_mu, L0_cond_w_cb, L0_cond_b_cb, L0_ffn_wq, L0_ffn_wk, L0_ffn_wv, L0_ffn_wo, L0_ffn_w1, L0_ffn_w2, L0_ffn_w3, L0_ffn_attn_norm_w, L0_ffn_ff_norm_w, L0_ffn_moe_norm_w, L0_ffn_router_w, L0_ffn_ew1, L0_ffn_ew2, L0_ffn_ew3):
    import jax
    import jax.numpy as jnp

    def _L0_cond_ref(ents, ent_mask, q_encoding, adj, types, init_mem, w_qin, b_qin, w_qt, b_qt, w_pl, b_pl, w_pc, b_pc, w_q, b_q, w_k, b_k, w_v, b_v, w_pk, b_pk, w_pv, b_pv, wes, w_mu, b_mu, w_cb, b_cb):
        import jax, jax.numpy as jnp
        import numpy as np
        B, N, D = (4, 128, 128)
        T_ITER = 4
        E_TYPES = 4
        ALPHA = 0.2

        def _lin_w(key, out_f, in_f):
            bound = float(np.sqrt(3.0 / ((in_f + out_f) / 2.0)))
            return jax.random.uniform(key, (out_f, in_f), minval=-bound, maxval=bound, dtype=jnp.float32)

        def _lin(x, w, b):
            return x @ w.T + b

        def _qdgat_forward(ents, ent_mask, q_encoding, adj, types, init_mem, w_qin, b_qin, w_qt, b_qt, w_pl, b_pl, w_pc, b_pc, w_q, b_q, w_k, b_k, w_v, b_v, w_pk, b_pk, w_pv, b_pv, wes, w_mu, b_mu, w_cb, b_cb):
            d = ents.shape[-1]
            x_loc = ents
            x_ctx = jnp.broadcast_to(init_mem, ents.shape)
            var_drop = ent_mask[:, :, None]
            adj_pos = adj > 0
            q_base = jax.nn.elu(_lin(q_encoding, w_qin, b_qin))
            n_types = wes.shape[0] + 1
            for t in range(T_ITER):
                cmd = _lin(q_base, w_qt[t], b_qt[t])
                xc = x_ctx * var_drop
                pl = _lin(x_loc, w_pl, b_pl)
                pc = _lin(xc, w_pc, b_pc)
                x_joint = jnp.concatenate([x_loc, xc, pl * pc], axis=-1)
                q = _lin(x_joint, w_q, b_q)
                k = _lin(x_joint, w_k, b_k) * _lin(cmd, w_pk, b_pk)[:, None, :]
                v = _lin(x_joint, w_v, b_v) * _lin(cmd, w_pv, b_pv)[:, None, :]
                edge_score = jnp.zeros(adj.shape, jnp.float32)
                for i in range(n_types):
                    if types >> i & 1 == 1:
                        w1, w2 = (wes[i - 1, :d], wes[i - 1, d:])
                        s = (q @ w1)[:, :, None] + (k @ w2)[:, None, :]
                        edge_score = edge_score + jnp.where(adj == i, s, 0.0)
                e = jnp.where(edge_score > 0, edge_score, ALPHA * edge_score)
                logits = jnp.where(adj_pos, e, jnp.float32(-9000000000000000.0))
                prob = jax.nn.softmax(logits, axis=-1)
                message = jnp.einsum('bij,bjd->bid', prob, v)
                x_ctx = _lin(jnp.concatenate([xc, message], axis=-1), w_mu, b_mu)
            return _lin(jnp.concatenate([x_loc, x_ctx], axis=-1), w_cb, b_cb)
        return _qdgat_forward(ents, ent_mask, q_encoding, adj, types, init_mem, w_qin, b_qin, w_qt, b_qt, w_pl, b_pl, w_pc, b_pc, w_q, b_q, w_k, b_k, w_v, b_v, w_pk, b_pk, w_pv, b_pv, wes, w_mu, b_mu, w_cb, b_cb)

    def _L0_ffn_ref(x, wq, wk, wv, wo, w1, w2, w3, attn_norm_w, ff_norm_w, moe_norm_w, router_w, ew1, ew2, ew3):
        import jax, jax.numpy as jnp
        import numpy as np
        D = 128
        H = 16
        FF = 512
        E = 8
        K = 2
        EH = 128
        B, S = (2, 256)
        EPS = 1e-05

        def rmsnorm(x, w):
            v = jnp.mean(jnp.square(x), axis=-1, keepdims=True)
            return x * jax.lax.rsqrt(v + EPS) * w

        def _dense_path(x, wq, wk, wv, wo, w1, w2, w3, attn_norm_w, ff_norm_w):
            b, s, d = x.shape
            hd = d // H
            q = (x @ wq).reshape(b, s, H, hd)
            k = (x @ wk).reshape(b, s, H, hd)
            v = (x @ wv).reshape(b, s, H, hd)
            scores = jnp.einsum('bqhd,bkhd->bhqk', q, k) / np.sqrt(hd).astype(np.float32)
            causal = jnp.tril(jnp.ones((s, s), bool))
            scores = jnp.where(causal, scores, jnp.finfo(scores.dtype).min)
            attn = jax.nn.softmax(scores, axis=-1)
            o = jnp.einsum('bhqk,bkhd->bqhd', attn, v).reshape(b, s, d)
            h = x + rmsnorm(o @ wo, attn_norm_w)
            ffn = jax.nn.silu(h @ w1) * (h @ w3) @ w2
            return h + rmsnorm(ffn, ff_norm_w)

        def _sparse_path(x, router_w, ew1, ew2, ew3, moe_norm_w):
            b, s, d = x.shape
            xt = x.reshape(-1, d)
            probs = jax.nn.softmax(xt @ router_w, axis=-1)
            topw, topi = jax.lax.top_k(probs, K)
            g = jax.nn.silu(jnp.einsum('td,edh->eth', xt, ew1)) * jnp.einsum('td,edh->eth', xt, ew3)
            eo = jnp.einsum('eth,ehd->ted', g, ew2)
            sel = jnp.take_along_axis(eo, topi[:, :, None], axis=1)
            moe_out = jnp.sum(topw[:, :, None] * sel, axis=1).reshape(b, s, d)
            return rmsnorm(moe_out, moe_norm_w)
        dense_out = _dense_path(x, wq, wk, wv, wo, w1, w2, w3, attn_norm_w, ff_norm_w)
        sparse_out = _sparse_path(x, router_w, ew1, ew2, ew3, moe_norm_w)
        return dense_out + sparse_out
    x = x + _L0_ffn_ref(_L0_cond_ref(x, mask_BxS_ff1, fside_BxS_0, itok_BxSxS_0_4, 30, L0_cond_init_mem, L0_cond_w_qin, L0_cond_b_qin, fside_BxSxS_0, mask_BxS_ff0, L0_cond_w_pl, L0_cond_b_pl, L0_cond_w_pc, L0_cond_b_pc, L0_cond_w_q, L0_cond_b_q, L0_cond_w_k, L0_cond_b_k, L0_cond_w_v, L0_cond_b_v, L0_cond_w_pk, L0_cond_b_pk, L0_cond_w_pv, L0_cond_b_pv, cond_2048, L0_cond_w_mu, L0_cond_b_mu, L0_cond_w_cb, L0_cond_b_cb), L0_ffn_wq, L0_ffn_wk, L0_ffn_wv, L0_ffn_wo, L0_ffn_w1, L0_ffn_w2, L0_ffn_w3, L0_ffn_attn_norm_w, L0_ffn_ff_norm_w, L0_ffn_moe_norm_w, L0_ffn_router_w, L0_ffn_ew1, L0_ffn_ew2, L0_ffn_ew3)
    return x

_drawn_inputs = setup_inputs


def setup_inputs(seed=0):
    import zlib

    import numpy as np

    out = dict(_drawn_inputs(seed))
    spreads = {'L0_cond_b_qin': (0.0, 0.1),
     'L0_cond_b_pl': (0.0, 0.1),
     'L0_cond_b_pc': (0.0, 0.771),
     'L0_cond_b_q': (0.0, 0.8),
     'L0_cond_b_k': (0.0, 0.8),
     'L0_cond_b_v': (0.0, 0.1),
     'L0_cond_b_pk': (0.0, 0.8),
     'L0_cond_b_pv': (0.0, 0.1),
     'L0_cond_b_mu': (0.0, 0.1),
     'L0_cond_b_cb': (0.0, 0.1),
     'L0_ffn_attn_norm_w': (1.0, 0.2),
     'L0_ffn_ff_norm_w': (1.0, 0.2),
     'L0_ffn_moe_norm_w': (1.0, 0.2)}
    factors = {'cond_2048': 3.864,
     'L0_cond_w_q': 4.274,
     'L0_cond_w_k': 5.744,
     'L0_cond_w_pk': 6.668,
     'L0_ffn_wq': 5.081,
     'L0_ffn_wk': 4.892}
    for name, (base, spread) in spreads.items():
        noise = np.random.default_rng([zlib.crc32(name.encode()), seed]).standard_normal(out[name].shape)
        drawn = base * np.exp(spread * noise) if base else spread * noise
        out[name] = jnp.asarray(drawn.astype(out[name].dtype))
    for name, factor in factors.items():
        out[name] = (out[name] * factor).astype(out[name].dtype)
    return out
```

```python
from contextlib import ExitStack

import concourse.bass as bass
from concourse import mybir

F32 = mybir.dt.float32
F32R = mybir.dt.float32r
BF16 = mybir.dt.bfloat16
U8 = mybir.dt.uint8
I32 = mybir.dt.int32
ALU = mybir.AluOpType
ACT = mybir.ActivationFunctionType
AX_X = mybir.AxisListType.X

P = 128
B = 32
GB = 4
NG = B // GB
W = GB * P
T = 4
TY = 4
H = 16
HD = P // H
E = 8
FC = 4
NC = E + FC
EPS = 1e-5
ALPHA = 0.2
MASKED = -9e15 / ALPHA
NV = P + 2 * TY
NX = P + TY + T * TY
NR = P + E

COLS = {}


def _cols():
    at = 0
    for name, width in (("pl", P), ("pc", P), ("mu1", P), ("mu2", P), ("cb1", P), ("cb2", P),
                        ("v1", P), ("v2", P), ("v3", P), ("wq", 3 * P), ("wk", 3 * P),
                        ("qin", P), ("pk", P), ("pv", P), ("qt", T * P), ("bqt", T), ("wes1", TY), ("wes2", TY),
                        ("qenc", B), ("init", 1), ("bqin", 1), ("bpl", 1), ("bpc", 1), ("bq", 1), ("bk", 1),
                        ("bpk", 1), ("bpv", 1), ("bmu", 1), ("bcb", 1),
                        ("wo", P), ("vr", NR), ("w2", FC * P), ("ew2", E * P)):
        COLS[name] = (at, at + width)
        at += width
    return at


NW = _cols()
NS = 2 * P + 2 * NC * P


COND_POINTS = [("start", 0)] + [(s, t) for t in range(T)
                                for s in ("pc", "vp", "tt", "s0", "s1", "p0", "p1", "msg", "mu")] + [("cb", 0)]
FFN_POINTS = ([("vr", 0), ("qk", 0)] + [("arrange", g) for g in range(4)] + [("gates", 0)]
              + [("spread", e) for e in range(0, E, 2)]
              + [("attend", u) for u in range(16 + 2)] + [("mix", 0), ("out_proj", 0), ("chunk", 0), ("norm_h", 0), ("chunk", 1),
              ("turn_h", 0)] + [("chunk", c) for c in range(2, NC + 2)] + [("last", 0)])


def points(cond, ffn):
    a = [("c",) + p for p in COND_POINTS] if cond else []
    b = [("f",) + p for p in FFN_POINTS] if ffn else []
    if not a or not b:
        return a + b
    out, j = [], 0
    for i, p in enumerate(a):
        out.append(p)
        while (j + 1) * len(a) <= (i + 1) * len(b):
            out.append(b[j])
            j += 1
    return out + b[j:]


TILES = (["ont", "wo", ("h1", 0), ("h3", 0), ("h1", 1), ("h3", 1), "ht"]
         + [(h, c) for c in range(2, NC) for h in ("h1", "h3")])


def tile_bank(tile):
    return 4 + TILES.index(tile) % 3


def build(nc, xT, xN, adj, msk, wts, splits, norms, rows, cst_bf, cst_f, out):
    with ExitStack() as ctx:
        def sb(name, shape, dt=F32):
            return ctx.enter_context(nc.sbuf_tensor(name, shape, dt))

        def sem(name):
            return ctx.enter_context(nc.semaphore(name))

        ps = ctx.enter_context(nc.psum_tensor("ps", [P, 8, 512], F32))

        wt = sb("wt", [P, NW])
        hi_w = sb("hi_w", [P, NS], F32R)
        lo_w = sb("lo_w", [P, NS], F32R)
        cb = sb("cb", [P, cst_bf.shape[1]], BF16)
        ident = sb("ident", [P, P])
        arr = sb("arr", [P, 4 * 4 * P], F32R)
        tri = sb("tri", [P, E, E])
        nrm = sb("nrm", [P, 3, P])
        ones_row = sb("ones_row", [1, P])
        half_pow = sb("half_pow", [P, GB])
        eps = sb("eps", [P, GB])
        key_w = sb("key_w", [P, 3, B * T * TY])
        key_b = sb("key_b", [1, B * T * TY])
        qry_w = sb("qry_w", [P, 3, TY])
        qry_b = sb("qry_b", [1, TY])
        vc = sb("vc", [P, T, B])
        kc = sb("kc", [P, T, B])
        rh = sb("rh", [P, 2, GB, 2, NV])
        rx = sb("rx", [P, GB, NX])
        rb = sb("rb", [1, GB, NX])
        qb = sb("qb", [P, B])
        qneg = sb("qneg", [P, B])
        cmd = sb("cmd", [P, T, B])

        xt = sb("xt", [P, W])
        ad = sb("ad", [P, W], I32)
        mb = sb("mb", [P, W])
        is_ty = sb("is_ty", [P, TY - 1, W], U8)
        pen = sb("pen", [P, W], BF16)
        pl = sb("pl", [P, W])
        cbx = sb("cbx", [P, W])
        xlv = sb("xlv", [P, GB, P])
        xlac = sb("xlac", [P, GB, T, 2 * TY])
        xc = sb("xc", [P, W])
        pr = sb("pr", [P, W])
        ac = sb("ac", [P, GB, 2 * TY])
        ac_r = sb("ac_r", [P, GB, 2 * TY])
        t3 = sb("t3", [P, GB, 32], BF16)
        tt = sb("tt", [P, P], BF16)
        z = sb("z", [P, GB, P])
        lk = sb("lk", [P, GB, P])
        neg_mx = sb("neg_mx", [P, GB])
        den = sb("den", [P, GB])
        carrier = sb("carrier", [1, 1])
        rden = sb("rden", [P, GB])
        pe_ = sb("pexp", [P, GB, P])
        pn = sb("pn", [P, GB, P])
        pt = sb("pt", [P, GB, P])
        v = sb("v", [P, GB, P])
        ms = sb("ms", [P, W])
        yt = sb("yt", [P, W])

        xn = sb("xn", [P, GB, P])
        yh = sb("yh", [P, W], F32R)
        yl = sb("yl", [P, W], F32R)
        yn = sb("yn", [P, GB, P])
        qk_h = sb("qk_h", [P, 2, W], F32R)
        qk_l = sb("qk_l", [P, 2, W], F32R)
        qk = sb("qk", [P, 4, 2, W], F32R)
        va = sb("va", [P, GB, H, HD + 1])
        lg = sb("lg", [P, GB, E])
        lgm = sb("lgm", [P, GB])
        lge = sb("lge", [P, GB, E])
        lgs = sb("lgs", [P, GB])
        prb = sb("prb", [P, GB, E])
        gt = sb("gt", [P, GB, E, E])
        eq = sb("eq", [P, GB, E, E])
        rank = sb("rank", [P, GB, E])
        gate = sb("gate", [P, GB, E])
        gate_r = sb("gate_r", [P, GB, E])
        g3 = sb("g3", [P, GB, 32], BF16)
        gT = sb("gT", [32, W], BF16)
        wb = sb("wb", [P, E, W])
        nmx = sb("nmx", [P, 2, 4])
        pa = sb("pa", [P, 2, 4, P])
        pat = sb("pat", [P, 2, 4, P])
        rl = sb("rl", [P, H])
        on = sb("on", [P, GB, H, HD])
        onT = sb("onT", [P, W])
        sq = sb("sq", [P, P])
        ss = sb("ss", [P, 3, GB])
        rs = sb("rs", [P, 3, GB])
        rstd = sb("rstd", [P, 3, GB])
        nh = onT
        hh = sb("hh", [P, W])
        hth = qk_h[:, 0, :]
        htl = qk_h[:, 1, :]
        th = pa[:, :, :, :].rearrange("p k g i -> p k (g i)")
        g1 = pat[:, :, :, :].rearrange("p k g i -> p k (g i)")
        g2 = sb("g2", [P, 3, W])
        gw = sb("gw", [P, 2, W])
        mo = sb("mo", [P, W])
        res, fo = mo, hh

        def w(name):
            a, b = COLS[name]
            return wt[:, a:b]

        def col(name):
            return w(name)[:, 0:1]

        def part(name, k):
            return w(name)[:, k * P:(k + 1) * P]

        idb = cb[:, 0:P]
        causal = cb[:, P:P + 512]
        o = P + 512
        sel_key = cb[:, o:o + 16 * P].rearrange("k (b y j) -> k b y j", b=GB, y=TY)
        o += 16 * P
        sel_qry = cb[:, o:o + 4 * 512].rearrange("k (b j) -> k b j", b=GB)
        o += 4 * 512
        sel_exp = cb[0:32, o:o + E * P].rearrange("k (e j) -> k e j", e=E)
        arr4 = arr[:, :].rearrange("k (s g j) -> k s g j", s=4, g=4)

        S = {}
        for name in (
            "weights_in", "splits_in", "consts_in", "xt_in", "adj_in", "mask_in", "xn_in", "out_stored",
            "setup_pe", "setup_dve", "setup_act", "setup_pool",
            "pl_ps", "cbx_ps", "xl_ps", "pc_ps", "v_ps", "turned_ac", "score_ps", "turned_p", "msg_ps", "mu_ps", "cb_ps",
            "edges_ready", "pl_sb", "xlac_sb", "xc_sb", "prod_sb", "t3_sb", "v_sb", "z_sb", "max_sb", "probs_sb",
            "msg_sb", "yt_sb", "cond_dve", "rden_sb", "cbx_sb", "xlv_sb", "tt_sb", "base_sb", "exp_sb", "pt_sb",
            "rh_next", "rx_next",
            "vr_ps", "yn_ps", "qk_ps", "arr_ps", "gT_ps", "spread_ps", "s_ps", "turned_pa", "o_ps", "onT_ps", "wo_ps",
            "ht_ps", "h1_ps", "h3_ps", "down_ps", "lg_sb", "yl_sb", "qk_lo", "arrk_sb", "lgneg_sb", "g3_sb", "nmx_sb", "on_sb",
            "hh_sb", "htl_sb", "g1_sb", "g2_sb", "mo_sb", "fo_sb", "ffn_dve", "yh_sb", "va_sb", "yn_sb", "qk_hi",
            "arrq_sb", "lge_sb", "gT_sb", "wb_sb", "pa_sb", "pat_sb", "onT_sb", "ss_sb", "hth_sb", "th_sb", "gw_sb",
            "rstd_sb", "res_sb", "ffn_pool",
        ):
            S[name] = sem(name)
        block = ctx.enter_context(nc.Block())

        def at(n, per, k):
            return n * per + k + 1

        DVE_COND, DVE_FFN = 6 + T * (4 + 2 * 1), 29

        @block.sync
        def _(sp):
            sp.dma_start(wt[:, :], wts).then_inc(S["weights_in"], 16)
            sp.dma_start(cb[:, :], cst_bf).then_inc(S["consts_in"], 16)
            sp.dma_start(ident[:, :], cst_f[:, 0:P]).then_inc(S["consts_in"], 16)
            sp.dma_start(tri[:, :, :], cst_f[:, P:P + E * E].rearrange("p (a b) -> p a b", a=E)).then_inc(S["consts_in"], 16)
            sp.dma_start(nrm[:, :, :], norms.partition_broadcast(P)).then_inc(S["consts_in"], 16)
            sp.dma_start(rb[0:1, :, 0:P], rows.rearrange("a (b j) -> a b j", b=GB)).then_inc(S["consts_in"], 16)
            sp.dma_start(xt[:, :], xT[:, 0:W]).then_inc(S["xt_in"], 16)
            sp.dma_start(ad[:, :].rearrange("p (b j) -> p b j", b=GB), adj[:, 0:GB, :]).then_inc(S["adj_in"], 16)
            sp.dma_start(mb[:, :], msk[:, 0:W].partition_broadcast(P).rearrange("p a w -> p (a w)")).then_inc(S["mask_in"], 16)
            stage = wb[:, :, :].rearrange("p e w -> p (e w)")
            for k in range(2):
                if k:
                    sp.wait_ge(S["setup_dve"], 2)
                sp.dma_start(stage[:, 0:NS // 2], splits[:, k * NS // 2:(k + 1) * NS // 2]).then_inc(S["splits_in"], 16)
            sp.wait_ge(S["setup_dve"], 4)
            sp.dma_start(stage[:, 0:16 * P], cst_f[:, P + E * E:P + E * E + 16 * P]).then_inc(S["splits_in"], 16)

            def iteration(n, cond, ffn, more):
                if ffn:
                    if not (isinstance(n, int) and n == 1):
                        sp.wait_ge(S["res_sb"], at(n - 2, 1, 0))
                    sp.dma_start(xn[:, :, :], xN[:, bass.ds((n - 1) * GB, GB), :]).then_inc(S["xn_in"], 16)
                if more:
                    sp.wait_ge(S["xl_ps"], at(n, 2, 1))
                    sp.dma_start(xt[:, :], xT[:, bass.ds((n + 1) * W, W)]).then_inc(S["xt_in"], 16)
                    sp.wait_ge(S["edges_ready"], at(n, 1, 0))
                    sp.dma_start(ad[:, :].rearrange("p (b j) -> p b j", b=GB),
                                 adj[:, bass.ds((n + 1) * GB, GB), :]).then_inc(S["adj_in"], 16)
                    sp.wait_ge(S["xc_sb"], at(n, 5, 3))
                    sp.dma_start(mb[:, :], msk[:, bass.ds((n + 1) * W, W)].partition_broadcast(P)
                                 .rearrange("p a w -> p (a w)")).then_inc(S["mask_in"], 16)
                if ffn:
                    sp.wait_ge(S["fo_sb"], at(n - 1, 1, 0))
                    sp.dma_start(out[:, bass.ds((n - 1) * GB, GB), :],
                                 fo[:, :].rearrange("p (b j) -> p b j", b=GB)).then_inc(S["out_stored"], 16)

            iterations(sp, iteration)
            sp.wait_ge(S["out_stored"], 16 * NG)

        @block.tensor
        def _(pe):
            def mm(out_, lhsT, rhs, start=True, stop=True, **kw):
                return pe.matmul(out_, lhsT, rhs, start=start, stop=stop, skip_group_check=True, **kw)

            def split3(out_, k, ah, al, start=True, sl=slice(None)):
                wh, wl = hi_w[:, k * P:(k + 1) * P], lo_w[:, k * P:(k + 1) * P]
                mm(out_, wh, ah, start=start, stop=False)
                mm(out_, wh, al, start=False, stop=False)
                return mm(out_, wl, ah, start=False, stop=True)

            pe.wait_ge(S["weights_in"], 16)
            mm(ps[:, 0, 0:B], w("qin"), w("qenc")).then_inc(S["setup_pe"], 1)
            pe.wait_ge(S["setup_dve"], 6)
            for t in range(T):
                i = mm(ps[:, 1, t * B:(t + 1) * B], part("qt", t), qb[:, :], start=(t == 0))
            i.then_inc(S["setup_pe"], 1)
            pe.wait_ge(S["setup_dve"], 7)
            cm = cmd[:, :, :].rearrange("p t b -> p (t b)")
            mm(ps[:, 2, 0:T * B], w("pk"), cm)
            mm(ps[:, 3, 0:T * B], w("pv"), cm).then_inc(S["setup_pe"], 1)
            for k in range(3):
                mm(ps[:, 4, k * TY:(k + 1) * TY], part("wq", k), w("wes1"), start=(k == 0))
            mm(ps[0:1, 5, 0:TY], w("bq"), w("wes1")).then_inc(S["setup_pe"], 1)
            pe.wait_ge(S["setup_dve"], 12)
            kw = wb[:, 0, :]
            for k in range(3):
                mm(ps[:, k, :], part("wk", k), kw)
            mm(ps[0:1, 3, :], w("bk"), kw).then_inc(S["setup_pe"], 1)
            pe.wait_ge(S["setup_pool"], 1)
            pe.wait_ge(S["setup_dve"], 20)
            pe.wait_ge(S["consts_in"], 5 * 16)

            def cond_point(n, what, t):
                first = isinstance(n, int) and n == 0
                if what == "start":
                    if not first:
                        pe.wait_ge(S["yt_sb"], at(n - 1, 1, 0))
                    pe.wait_ge(S["xt_in"], 16 * n + 16)
                    mm(ps[:, 2, :], w("pl"), xt[:, :]).then_inc(S["pl_ps"], 1)
                    mm(ps[:, 3, :], w("cb1"), xt[:, :]).then_inc(S["cbx_ps"], 1)
                    if not first:
                        pe.wait_ge(S["rx_next"], n)
                    for b in range(GB):
                        o_ = ps[:, b // 2, b % 2 * NX:(b % 2 + 1) * NX]
                        mm(o_, xt[:, b * P:(b + 1) * P], rx[:, b, :], start=(b % 2 == 0), stop=False)
                        i = mm(o_, ones_row[:, :], rb[:, b, :], start=False)
                        if b % 2:
                            i.then_inc(S["xl_ps"], 1)
                elif what == "pc":
                    if t == 0:
                        pe.wait_ge(S["pl_sb"], at(n, 1, 0))
                    pe.wait_ge(S["xc_sb"], at(n, 5, t))
                    mm(ps[:, 2, :], w("pc"), xc[:, :]).then_inc(S["pc_ps"], 1)
                    if t == 0:
                        pe.wait_ge(S["xlac_sb"], at(n, 1, 0))
                        pe.wait_ge(S["xlv_sb"], at(n, 1, 0))
                    if not first or t >= 2:
                        pe.wait_ge(S["rh_next"], 4 * n + t - 1)
                    for b in range(GB):
                        mm(ps[:, b // 2, b % 2 * NV:(b % 2 + 1) * NV], xc[:, b * P:(b + 1) * P], rh[:, 0, b, t % 2, :],
                           start=(b % 2 == 0), stop=False)
                elif what == "vp":
                    pe.wait_ge(S["prod_sb"], at(n, T, t))
                    for b in range(GB):
                        i = mm(ps[:, b // 2, b % 2 * NV:(b % 2 + 1) * NV], pr[:, b * P:(b + 1) * P], rh[:, 1, b, t % 2, :],
                               start=False)
                    i.then_inc(S["v_ps"], 1)
                elif what == "tt":
                    pe.wait_ge(S["t3_sb"], at(n, T, t))
                    if t == 0:
                        pe.wait_ge(S["cbx_sb"], at(n, 1, 0))
                    pe.transpose(ps[:, 3, 0:P // 2].bitcast(BF16), t3[:, :, :].rearrange("p b k -> p (b k)"),
                                 idb).then_inc(S["turned_ac"], 1)
                elif what in ("s0", "s1"):
                    hf = int(what[1])
                    if hf == 0:
                        pe.wait_ge(S["tt_sb"], at(n, T, t))
                        pe.wait_ge(S["v_sb"], at(n, T, t))
                        if t == 0:
                            pe.wait_ge(S["edges_ready"], at(n, 1, 0))
                    else:
                        pe.wait_ge(S["z_sb"], at(n, 2 * T, 2 * t))
                    for k in range(2):
                        b = 2 * hf + k
                        mm(ps[:, k, :], tt[:, :], sel_qry[:, b, :], start=True, stop=False)
                        mm(ps[:, k, 0:P], idb, pen[:, b * P:(b + 1) * P], start=False, stop=False)
                        for y in range(TY):
                            i = mm(ps[:, k, y * P:(y + 1) * P], sel_key[:, b, y, :], tt[:, :], start=False)
                    i.then_inc(S["score_ps"], 1)
                elif what in ("p0", "p1"):
                    hf = int(what[1])
                    pe.wait_ge(S["probs_sb"], at(n, 2 * T, 2 * t + hf))
                    for k in range(2):
                        b = 2 * hf + k
                        i = pe.transpose(ps[:, 3 - hf, k * P:(k + 1) * P], pn[:, b, :], ident[:, :])
                    i.then_inc(S["turned_p"], 1)
                elif what == "msg":
                    pe.wait_ge(S["pt_sb"], at(n, 2 * T, 2 * t + 1))
                    pe.wait_ge(S["z_sb"], at(n, 2 * T, 2 * t + 1))
                    for b in range(GB):
                        i = mm(ps[:, 0, b * P:(b + 1) * P], v[:, b, :], pt[:, b, :], start=(b == 0))
                    i.then_inc(S["msg_ps"], 1)
                elif what == "mu":
                    mm(ps[:, 1, :], w("mu1"), xc[:, :], stop=False)
                    pe.wait_ge(S["msg_sb"], at(n, T, t))
                    mm(ps[:, 1, :], w("mu2"), ms[:, :], start=False).then_inc(S["mu_ps"], 1)
                elif what == "cb":
                    pe.wait_ge(S["xc_sb"], at(n, 5, 4))
                    pe.wait_ge(S["pt_sb"], at(n, 2 * T, 2 * T - 1))
                    mm(ps[:, 2, :], w("cb2"), xc[:, :]).then_inc(S["cb_ps"], 1)

            def tile_free(f, tile):
                i = TILES.index(tile)
                if i < 2:
                    pe.wait_ge(S["pa_sb"], at(f, 64, 4 * (14 + i) + 3))
                    return
                if i == 2:
                    pe.wait_ge(S["pat_sb"], at(f, 16, 15))
                    return
                old = TILES[i - 3]
                if old == "ont":
                    pe.wait_ge(S["onT_sb"], at(f, 1, 0))
                elif old == "wo":
                    pe.wait_ge(S["hh_sb"], at(f, 1, 0))
                elif old == "ht":
                    pe.wait_ge(S["htl_sb"], at(f, 1, 0))
                elif old[0] == "h1":
                    pe.wait_ge(S["g1_sb"], at(f, NC, old[1]))
                else:
                    pe.wait_ge(S["g2_sb"], at(f, NC, old[1]))

            def down(f, c):
                if c == 0:
                    pe.wait_ge(S["on_sb"], at(f, GB, GB - 1))
                if c == E:
                    pe.wait_ge(S["mo_sb"], at(f, 1, 0))
                if c < E:
                    pe.wait_ge(S["gw_sb"], at(f, E, c))
                    a, m = gw[:, c % 2, :], part("ew2", c)
                else:
                    pe.wait_ge(S["g2_sb"], at(f, NC, c))
                    a, m = g2[:, c % 3, :], part("w2", c - E)
                for b in range(GB):
                    i = mm(ps[:, 7, b * P:(b + 1) * P], a[:, b * P:(b + 1) * P], m,
                           start=(b == 0 and c in (0, E)), stop=(c in (E - 1, NC - 1)))
                i.then_inc(S["down_ps"], 1)

            def ffn_point(n, what, u):
                f = n - 1
                first = isinstance(n, int) and n == 1
                if what == "vr":
                    pe.wait_ge(S["yt_sb"], at(f, 1, 0))
                    if not first:
                        pe.wait_ge(S["g2_sb"], at(f - 1, NC, NC - 1))
                        pe.wait_ge(S["g1_sb"], at(f - 1, NC, NC - 1))
                    for b in range(GB):
                        i = mm(ps[:, 4 + b // 2, b % 2 * NR:(b % 2 + 1) * NR], yt[:, b * P:(b + 1) * P], w("vr"),
                               start=(b % 2 == 0))
                    i.then_inc(S["vr_ps"], 1)
                    for b in range(GB):
                        i = pe.transpose(ps[:, 6, b * P:(b + 1) * P], yt[:, b * P:(b + 1) * P], ident[:, :])
                    i.then_inc(S["yn_ps"], 1)
                elif what == "qk":
                    pe.wait_ge(S["yl_sb"], at(f, 1, 0))
                    if not first:
                        pe.wait_ge(S["fo_sb"], at(f - 1, 1, 0))
                    split3(ps[:, 7, :], 0, yh[:, :], yl[:, :]).then_inc(S["qk_ps"], 1)
                    pe.wait_ge(S["yn_sb"], at(f, 1, 0))
                    split3(ps[:, 6, :], 1, yh[:, :], yl[:, :]).then_inc(S["qk_ps"], 1)
                elif what == "arrange":
                    for s in range(2):
                        bank = (4, 5)[s] if u % 2 == 0 else (7, 6)[s]
                        pe.wait_ge(S["qk_lo"], at(f, 2, 1))
                        if u == 0:
                            pe.wait_ge(S["lg_sb"], at(f, 1, 0))
                            pe.wait_ge(S["va_sb"], at(f, 2, 1))
                        elif u >= 2:
                            pe.wait_ge(S["arrk_sb" if s else "arrq_sb"], at(f, 4, u - 2))
                        mm(ps[:, bank, :], arr4[:, 2 * s, u, :], qk_h[:, s, :], stop=False)
                        mm(ps[:, bank, :], arr4[:, 2 * s + 1, u, :], qk_l[:, s, :], start=False).then_inc(S["arr_ps"], 1)
                elif what == "gates":
                    pe.wait_ge(S["g3_sb"], at(f, 1, 0))
                    pe.wait_ge(S["arrq_sb"], at(f, 4, 3))
                    for b in range(GB):
                        i = pe.transpose(ps[0:32, 7, b * 64:(b + 1) * 64].bitcast(BF16), g3[:, b, :], idb)
                    i.then_inc(S["gT_ps"], 1)
                elif what == "spread":
                    for e in (u, u + 1):
                        if e == 0:
                            pe.wait_ge(S["gT_sb"], at(f, 1, 0))
                            pe.wait_ge(S["arrq_sb"], at(f, 4, 2))
                        elif e == 1:
                            pe.wait_ge(S["arrk_sb"], at(f, 4, 2))
                        else:
                            pe.wait_ge(S["wb_sb"], at(f, E, e - 2))
                        mm(ps[:, 4 + e % 2, :], sel_exp[:, e, :], gT[:, :]).then_inc(S["spread_ps"], 1)
                elif what == "attend":
                    if u < 16:
                        b, r = divmod(u, 4)
                        if u < 2:
                            pe.wait_ge(S["wb_sb"], at(f, E, 6 + u))
                            pe.wait_ge(S["arrk_sb"], at(f, 4, 3))
                            pe.wait_ge(S["arrq_sb"], at(f, 4, 3))
                        else:
                            pe.wait_ge(S["pa_sb"], at(f, 64, 4 * (u - 2) + 3))
                        mm(ps[:, 4 + u % 2, :], idb, causal, stop=False)
                        for g in range(4):
                            i = mm(ps[:, 4 + u % 2, g * P:(g + 1) * P], qk[32 * r:32 * r + 32, g, 0, b * P:(b + 1) * P],
                                   qk[32 * r:32 * r + 32, g, 1, b * P:(b + 1) * P], start=False,
                                   tile_position=(32 * r, 0))
                        i.then_inc(S["s_ps"], 1)
                    if 1 <= u <= 16:
                        q = u - 1
                        pe.wait_ge(S["pa_sb"], at(f, 64, 4 * q + 3))
                        if q:
                            pe.wait_ge(S["pat_sb"], at(f, 16, q - 1))
                        for g in range(4):
                            i = pe.transpose(ps[:, 6, g * P:(g + 1) * P], pa[:, q % 2, g, :], ident[:, :])
                        i.then_inc(S["turned_pa"], 1)
                    if u >= 2:
                        q = u - 2
                        b, r = divmod(q, 4)
                        pe.wait_ge(S["pat_sb"], at(f, 16, q))
                        if r == 0 and b:
                            pe.wait_ge(S["on_sb"], at(f, GB, b - 1))
                        elif q == 0:
                            pe.wait_ge(S["gT_sb"], at(f, 1, 0))
                        for g in range(4):
                            h = 4 * g + r
                            i = mm(ps[:, 7, h * (HD + 1):(h + 1) * (HD + 1)], pat[:, q % 2, g, :], va[:, b, h, :],
                                   start=(r == 0 and g == 0))
                        i.then_inc(S["o_ps"], 1)
                elif what == "mix":
                    pe.wait_ge(S["on_sb"], at(f, GB, GB - 1))
                    tile_free(f, "ont")
                    for b in range(GB):
                        i = pe.transpose(ps[:, tile_bank("ont"), b * P:(b + 1) * P],
                                         on[:, b, :, :].rearrange("p h d -> p (h d)"), ident[:, :])
                    i.then_inc(S["onT_ps"], 1)
                elif what == "out_proj":
                    pe.wait_ge(S["onT_sb"], at(f, 1, 0))
                    tile_free(f, "wo")
                    for b in range(GB):
                        i = mm(ps[:, tile_bank("wo"), b * P:(b + 1) * P], onT[:, b * P:(b + 1) * P], w("wo"), start=(b == 0))
                    i.then_inc(S["wo_ps"], 1)
                elif what == "turn_h":
                    pe.wait_ge(S["hh_sb"], at(f, 1, 0))
                    tile_free(f, "ht")
                    for b in range(GB):
                        i = pe.transpose(ps[:, tile_bank("ht"), b * P:(b + 1) * P], hh[:, b * P:(b + 1) * P], ident[:, :])
                    i.then_inc(S["ht_ps"], 1)
                elif what == "chunk":
                    if u < NC:
                        if u == E:
                            pe.wait_ge(S["htl_sb"], at(f, 1, 0))
                        ah, al = (yh, yl) if u < E else (hth, htl)
                        for k, nm in enumerate(("h1", "h3")):
                            tile_free(f, (nm, u))
                            split3(ps[:, tile_bank((nm, u)), :], 2 + 2 * u + k, ah[:, :], al[:, :])\
                                .then_inc(S[nm + "_ps"], 1)
                    if u >= 2:
                        down(f, u - 2)

            iterations(pe, lambda n, cond, ffn, more: [
                (cond_point if k == "c" else ffn_point)(n, what, t) for k, what, t in points(cond, ffn)])

        @block.vector
        def _(dve):
            count = [0]

            def setup(ins):
                count[0] += 1
                ins.then_inc(S["setup_dve"], 1)
                dve.wait_ge(S["setup_dve"], count[0])

            stage = wb[:, :, :].rearrange("p e w -> p (e w)")
            for k in range(2):
                dve.wait_ge(S["splits_in"], 16 * (k + 1))
                src = stage[:, 0:NS // 2]
                sl = slice(k * NS // 2, (k + 1) * NS // 2)
                setup(dve.tensor_copy(hi_w[:, sl], src))
                setup(dve.tensor_tensor(lo_w[:, sl], src, hi_w[:, sl].bitcast(F32), ALU.subtract))
            dve.wait_ge(S["setup_pe"], 1)
            dve.wait_ge(S["weights_in"], 16)
            setup(dve.tensor_scalar(qneg[:, :], ps[:, 0, 0:B], col("bqin"), 0.0, ALU.add, ALU.min))
            dve.wait_ge(S["setup_act"], 2)
            setup(dve.scalar_tensor_tensor(out=qb[:, :], in0=qneg[:, :], scalar=-1.0, in1=qb[:, :],
                                           op0=ALU.add, op1=ALU.add))
            dve.wait_ge(S["setup_pe"], 2)
            setup(dve.tensor_tensor(cmd[:, :, :], ps[:, 1, 0:T * B].rearrange("p (t b) -> p t b", t=T),
                                    w("bqt").unsqueeze(2).to_broadcast([P, T, B]), ALU.add))
            dve.wait_ge(S["setup_pe"], 3)
            setup(dve.tensor_scalar(kc[:, :, :].rearrange("p t b -> p (t b)"), ps[:, 2, 0:T * B], col("bpk"), None, ALU.add))
            setup(dve.tensor_scalar(vc[:, :, :].rearrange("p t b -> p (t b)"), ps[:, 3, 0:T * B], col("bpv"), None, ALU.add))
            dve.wait_ge(S["setup_pe"], 4)
            dve.wait_ge(S["splits_in"], 48)
            setup(dve.tensor_copy(arr[:, :], stage[:, 0:16 * P]))
            setup(dve.tensor_copy(qry_w[:, :, :], ps[:, 4, 0:3 * TY].rearrange("p (k y) -> p k y", k=3)))
            setup(dve.tensor_tensor(wb[:, 0, :].rearrange("p (b t y) -> p b t y", b=B, t=T),
                                    kc[:, :, :].rearrange("p t b -> p b t").unsqueeze(3).to_broadcast([P, B, T, TY]),
                                    w("wes2").unsqueeze(1).unsqueeze(1).to_broadcast([P, B, T, TY]), ALU.mult))
            dve.wait_ge(S["setup_pe"], 5)
            setup(dve.tensor_copy(key_w[:, :, :], ps[:, 0:3, :]))
            setup(dve.tensor_copy(key_b[:, :], ps[0:1, 3, :]))
            setup(dve.tensor_copy(qry_b[:, :], ps[0:1, 5, 0:TY]))
            setup(dve.tensor_scalar(w("w2"), w("w2"), 0.5, None, ALU.mult))
            setup(dve.memset(ones_row[:, :], 1.0))
            setup(dve.memset(t3[:, :, :], 0.0))
            setup(dve.memset(g3[:, :, :], 0.0))
            setup(dve.memset(va[:, :, :, HD:HD + 1], 1.0))
            dve.wait_ge(S["consts_in"], 5 * 16)

            state = {}

            def link(kind, n, per, ins):
                state[kind] += 1
                ins.then_inc(S[kind], 1)
                dve.wait_ge(S[kind], n * per + state[kind])

            def cond_point(n, what, t):
                first = isinstance(n, int) and n == 0
                if what == "start":
                    state["cond_dve"] = 0
                    dve.wait_ge(S["mask_in"], 16 * n + 16)
                    dve.tensor_scalar(xc[:, :], mb[:, :], col("init"), None, ALU.mult).then_inc(S["xc_sb"], 1)
                    dve.wait_ge(S["adj_in"], 16 * n + 16)
                    if not first:
                        dve.wait_ge(S["score_ps"], at(n - 1, 2 * T, 2 * T - 1))
                    for y in range(1, TY):
                        link("cond_dve", n, DVE_COND,
                             dve.tensor_scalar(is_ty[:, y - 1, :], ad[:, :], float(y + 1), None, ALU.is_equal))
                    dve.tensor_scalar(pen[:, :], ad[:, :], 0.0, MASKED, ALU.is_le, ALU.mult).then_inc(S["edges_ready"], 1)
                    dve.wait_ge(S["pl_ps"], at(n, 1, 0))
                    dve.tensor_scalar(pl[:, :], ps[:, 2, :], col("bpl"), None, ALU.add).then_inc(S["pl_sb"], 1)
                    dve.wait_ge(S["xl_ps"], at(n, 2, 1))
                    for k in range(2):
                        bs = slice(2 * k, 2 * k + 2)
                        x = ps[:, k, 0:2 * NX].rearrange("p (b c) -> p b c", b=2)
                        link("cond_dve", n, DVE_COND, dve.tensor_copy(
                            xlac[:, bs, :, TY:2 * TY], x[:, :, P + TY:NX].rearrange("p b (t y) -> p b t y", t=T)))
                        i = dve.tensor_copy(xlac[:, bs, :, 0:TY], x[:, :, P:P + TY].unsqueeze(2).to_broadcast([P, 2, T, TY]))
                        if k == 0:
                            link("cond_dve", n, DVE_COND, i)
                    i.then_inc(S["xlac_sb"], 1)
                elif what == "pc":
                    dve.wait_ge(S["pc_ps"], at(n, T, t))
                    dve.wait_ge(S["pl_sb"], at(n, 1, 0))
                    dve.scalar_tensor_tensor(out=pr[:, :], in0=ps[:, 2, :], scalar=col("bpc"), in1=pl[:, :],
                                             op0=ALU.add, op1=ALU.mult).then_inc(S["prod_sb"], 1)
                elif what == "vp":
                    dve.wait_ge(S["v_ps"], at(n, T, t))
                    if t == 0:
                        dve.wait_ge(S["xlac_sb"], at(n, 1, 0))
                        dve.wait_ge(S["xlv_sb"], at(n, 1, 0))
                    vs = ps[:, 0:2, 0:2 * NV].rearrange("p k (b c) -> p k b c", b=2)
                    sc = vs[:, :, :, P:NV]
                    xa = xlac[:, :, t, :].rearrange("p (k b) y -> p k b y", k=2)
                    dve.tensor_tensor(ac[:, :, :].rearrange("p (k b) y -> p k b y", k=2), sc, xa, ALU.add)\
                        .then_inc(S["cond_dve"], 1)
                    state["cond_dve"] += 1
                    link("cond_dve", n, DVE_COND, dve.tensor_tensor(
                        t3[:, :, 0:8].rearrange("p (k b) y -> p k b y", k=2), sc, xa, ALU.add))
                    dve.tensor_tensor(ac_r[:, :, :], ac[:, :, :], t3[:, :, 0:8], ALU.subtract).then_inc(S["cond_dve"], 1)
                    state["cond_dve"] += 1
                    link("cond_dve", n, DVE_COND,
                         dve.tensor_tensor(t3[:, :, 8:16], ac[:, :, :], t3[:, :, 0:8], ALU.subtract))
                    dve.tensor_tensor(t3[:, :, 16:24], ac_r[:, :, :], t3[:, :, 8:16], ALU.subtract).then_inc(S["t3_sb"], 1)
                    dve.tensor_tensor(v[:, :, :].rearrange("p (k b) d -> p k b d", k=2), vs[:, :, :, 0:P],
                                      xlv[:, :, :].rearrange("p (k b) d -> p k b d", k=2), ALU.add).then_inc(S["v_sb"], 1)
                elif what in ("s0", "s1"):
                    hf = int(what[1])
                    k = 2 * t + hf
                    bs = slice(2 * hf, 2 * hf + 2)
                    dve.wait_ge(S["base_sb"], at(n, 2 * T, k))
                    if t == 0 and hf == 0:
                        dve.wait_ge(S["edges_ready"], at(n, 1, 0))
                    dve.memset(carrier[:, :], 0.0)
                    dve.drain()
                    for y in range(1, TY):
                        i = dve.copy_predicated(z[:, bs, :],
                                                is_ty[:, y - 1, 2 * hf * P:(2 * hf + 2) * P].rearrange("p (b j) -> p b j", b=2),
                                                ps[:, 0:2, y * P:(y + 1) * P])
                        if y < TY - 1:
                            dve.drain()
                    i.then_inc(S["z_sb"], 1)
                    dve.wait_ge(S["z_sb"], at(n, 2 * T, k))
                    link("cond_dve", n, DVE_COND, dve.scalar_tensor_tensor(
                        out=lk[:, bs, :], in0=z[:, bs, :], scalar=ALPHA, in1=z[:, bs, :], op0=ALU.mult, op1=ALU.max))
                    dve.tensor_reduce(neg_mx[:, bs], lk[:, bs, :], AX_X, ALU.max, negate=True).then_inc(S["max_sb"], 1)
                elif what in ("p0", "p1"):
                    hf = int(what[1])
                    k = 2 * t + hf
                    bs = slice(2 * hf, 2 * hf + 2)
                    dve.wait_ge(S["exp_sb"], at(n, 4 * T, 2 * k + 1))
                    dve.reciprocal(rden[:, bs], den[:, bs]).then_inc(S["rden_sb"], 1)
                    dve.wait_ge(S["rden_sb"], at(n, 2 * T, k))
                    dve.tensor_tensor(pn[:, bs, :], pe_[:, bs, :], rden[:, bs].unsqueeze(2).to_broadcast([P, 2, P]),
                                      ALU.mult).then_inc(S["probs_sb"], 1)
                elif what == "msg":
                    dve.wait_ge(S["msg_ps"], at(n, T, t))
                    dve.tensor_tensor(ms[:, :].rearrange("p (b i) -> p b i", b=GB),
                                      ps[:, 0, :].rearrange("p (b i) -> p b i", b=GB),
                                      vc[:, t, bass.ds(n * GB, GB)].unsqueeze(2).to_broadcast([P, GB, P]),
                                      ALU.mult).then_inc(S["msg_sb"], 1)
                elif what == "mu":
                    dve.wait_ge(S["mu_ps"], at(n, T, t))
                    if t < T - 1:
                        dve.scalar_tensor_tensor(out=xc[:, :], in0=ps[:, 1, :], scalar=col("bmu"), in1=mb[:, :],
                                                 op0=ALU.add, op1=ALU.mult).then_inc(S["xc_sb"], 1)
                    else:
                        dve.tensor_scalar(xc[:, :], ps[:, 1, :], col("bmu"), None, ALU.add).then_inc(S["xc_sb"], 1)
                elif what == "cb":
                    dve.wait_ge(S["cb_ps"], at(n, 1, 0))
                    if not first:
                        dve.wait_ge(S["yn_ps"], at(n - 1, 1, 0))
                        dve.wait_ge(S["yl_sb"], at(n - 1, 1, 0))
                    dve.tensor_tensor(yt[:, :], ps[:, 2, :], cbx[:, :], ALU.add).then_inc(S["yt_sb"], 1)
                    assert state["cond_dve"] == DVE_COND, state["cond_dve"]

            SETUP = 20
            assert count[0] == SETUP, count[0]

            def gates(f):
                def l(ins):
                    link("ffn_dve", f, DVE_FFN, ins)

                def over(x):
                    return x.unsqueeze(2).to_broadcast([P, GB, E])
                dve.wait_ge(S["lge_sb"], at(f, 1, 0))
                l(dve.tensor_reduce(lgs[:, :], lge[:, :, :], AX_X, ALU.add))
                l(dve.reciprocal(lgs[:, :], lgs[:, :]))
                l(dve.tensor_tensor(prb[:, :, :], lge[:, :, :], over(lgs[:, :]), ALU.mult))
                mine = prb[:, :, :].unsqueeze(3).to_broadcast([P, GB, E, E])
                other = prb[:, :, :].unsqueeze(2).to_broadcast([P, GB, E, E])
                l(dve.tensor_tensor(gt[:, :, :, :], other, mine, ALU.is_gt))
                l(dve.tensor_tensor(eq[:, :, :, :], other, mine, ALU.is_equal))
                l(dve.tensor_tensor(eq[:, :, :, :], eq[:, :, :, :],
                                    tri[:, :, :].unsqueeze(1).to_broadcast([P, GB, E, E]), ALU.mult))
                l(dve.tensor_tensor(gt[:, :, :, :], gt[:, :, :, :], eq[:, :, :, :], ALU.add))
                l(dve.tensor_reduce(rank[:, :, :], gt[:, :, :, :], AX_X, ALU.add))
                l(dve.tensor_scalar(rank[:, :, :], rank[:, :, :], 1.5, 0.5, ALU.is_lt, ALU.mult))
                l(dve.tensor_tensor(gate[:, :, :], rank[:, :, :], prb[:, :, :], ALU.mult))
                l(dve.tensor_copy(g3[:, :, 0:E], gate[:, :, :]))
                l(dve.tensor_tensor(gate_r[:, :, :], gate[:, :, :], g3[:, :, 0:E], ALU.subtract))
                l(dve.tensor_copy(g3[:, :, E:2 * E], gate_r[:, :, :]))
                dve.tensor_tensor(g3[:, :, 2 * E:3 * E], gate_r[:, :, :], g3[:, :, E:2 * E], ALU.subtract)\
                    .then_inc(S["g3_sb"], 1)

            def normed(f, k, src, dst):
                dve.wait_ge(S["rstd_sb"], at(f, 3, k))
                for b in range(GB):
                    i = dve.scalar_tensor_tensor(out=dst[:, b * P:(b + 1) * P], in0=src[:, b * P:(b + 1) * P],
                                                 scalar=rstd[:, k, b:b + 1], in1=nrm[:, k, :],
                                                 op0=ALU.mult, op1=ALU.mult)
                    if b < GB - 1:
                        i.then_inc(S["ffn_dve"], 1)
                        state["ffn_dve"] += 1
                return i

            def gated(f, c):
                dve.wait_ge(S["th_sb"], at(f, NC, c))
                dve.scalar_tensor_tensor(out=g1[:, c % 2, :], in0=th[:, c % 2, :], scalar=1.0,
                                         in1=ps[:, tile_bank(("h1", c)), :], op0=ALU.add, op1=ALU.mult)\
                    .then_inc(S["g1_sb"], 1)
                dve.wait_ge(S["h3_ps"], at(f, NC, c))
                dve.wait_ge(S["g1_sb"], at(f, NC, c))
                if 3 <= c < E + 3:
                    dve.wait_ge(S["gw_sb"], at(f, E, c - 3))
                elif c >= E + 3:
                    dve.wait_ge(S["down_ps"], at(f, NC, c - 3))
                dve.tensor_tensor(g2[:, c % 3, :], g1[:, c % 2, :], ps[:, tile_bank(("h3", c)), :], ALU.mult)\
                    .then_inc(S["g2_sb"], 1)

            def ffn_point(n, what, u):
                f = n - 1
                first = isinstance(n, int) and n == 1
                if what == "vr":
                    state["ffn_dve"] = 0
                    dve.wait_ge(S["vr_ps"], at(f, 1, 0))
                    dve.tensor_copy(lg[:, :, :].rearrange("p (k b) e -> p k b e", k=2),
                                    ps[:, 4:6, 0:2 * NR].rearrange("p k (b c) -> p k b c", b=2)[:, :, :, P:NR])\
                        .then_inc(S["lg_sb"], 1)
                    dve.wait_ge(S["yh_sb"], at(f, 1, 0))
                    dve.tensor_tensor(yl[:, :], yt[:, :], yh[:, :].bitcast(F32), ALU.subtract).then_inc(S["yl_sb"], 1)
                    dve.wait_ge(S["lg_sb"], at(f, 1, 0))
                    link("ffn_dve", f, DVE_FFN, dve.tensor_reduce(lgm[:, :], lg[:, :, :], AX_X, ALU.max))
                    dve.tensor_tensor(lg[:, :, :], lg[:, :, :], lgm[:, :].unsqueeze(2).to_broadcast([P, GB, E]),
                                      ALU.subtract).then_inc(S["lgneg_sb"], 1)
                elif what == "qk":
                    for s in range(2):
                        dve.wait_ge(S["qk_hi"], at(f, 2, s))
                        bank = (7, 6)[s]
                        if s == 0:
                            i = dve.scalar_tensor_tensor(out=qk_l[:, 0, :], in0=ps[:, bank, :], scalar=HD ** -0.5,
                                                         in1=qk_h[:, 0, :].bitcast(F32), op0=ALU.mult, op1=ALU.subtract)
                        else:
                            i = dve.tensor_tensor(qk_l[:, 1, :], ps[:, bank, :], qk_h[:, 1, :].bitcast(F32), ALU.subtract)
                        i.then_inc(S["qk_lo"], 1)
                    gates(f)
                elif what == "arrange":
                    dve.wait_ge(S["arr_ps"], at(f, 8, 2 * u + 1))
                    dve.tensor_copy(qk[:, u, 1, :], ps[:, 5 if u % 2 == 0 else 6, :]).then_inc(S["arrk_sb"], 1)
                elif what == "attend":
                    if u < 16:
                        dve.wait_ge(S["s_ps"], at(f, 16, u))
                        if u >= 2:
                            dve.wait_ge(S["pa_sb"], at(f, 64, 4 * (u - 2) + 3))
                        dve.tensor_reduce(nmx[:, u % 2, :], ps[:, 4 + u % 2, :].rearrange("p (g j) -> p g j", g=4),
                                          AX_X, ALU.max, negate=True).then_inc(S["nmx_sb"], 1)
                    if u >= 5 and (u - 5) % 4 == 0:
                        b = (u - 5) // 4
                        dve.wait_ge(S["o_ps"], at(f, 16, 4 * b + 3))
                        x = ps[:, 7, 0:H * (HD + 1)].rearrange("p (h d) -> p h d", h=H)
                        link("ffn_dve", f, DVE_FFN, dve.reciprocal(rl[:, :].unsqueeze(2), x[:, :, HD:HD + 1]))
                        dve.tensor_tensor(on[:, b, :, :], x[:, :, 0:HD], rl[:, :].unsqueeze(2).to_broadcast([P, H, HD]),
                                          ALU.mult).then_inc(S["on_sb"], 1)
                elif what == "norm_h":
                    i = normed(f, 0, ps[:, tile_bank("wo"), :], nh)
                    link("ffn_dve", f, DVE_FFN, i)
                    dve.wait_ge(S["yn_sb"], at(f, 1, 0))
                    if not first:
                        dve.wait_ge(S["out_stored"], 16 * (n - 1))
                    dve.tensor_tensor(hh[:, :], nh[:, :], yn[:, :, :].rearrange("p b d -> p (b d)"), ALU.add)\
                        .then_inc(S["hh_sb"], 1)
                elif what == "turn_h":
                    dve.wait_ge(S["hth_sb"], at(f, 1, 0))
                    dve.tensor_tensor(htl[:, :], ps[:, tile_bank("ht"), :], hth[:, :].bitcast(F32), ALU.subtract)\
                        .then_inc(S["htl_sb"], 1)
                elif what == "chunk":
                    if u < NC:
                        gated(f, u)
                    if u == E + 1:
                        normed(f, 1, ps[:, 7, :], mo).then_inc(S["mo_sb"], 1)
                elif what == "last":
                    i = normed(f, 2, ps[:, 7, :], nh)
                    link("ffn_dve", f, DVE_FFN, i)
                    dve.wait_ge(S["res_sb"], at(f, 1, 0))
                    dve.tensor_tensor(fo[:, :], nh[:, :], res[:, :], ALU.add).then_inc(S["fo_sb"], 1)
                    assert state["ffn_dve"] == DVE_FFN, state["ffn_dve"]

            iterations(dve, lambda n, cond, ffn, more: [
                (cond_point if k == "c" else ffn_point)(n, what, t) for k, what, t in points(cond, ffn)])

        @block.scalar
        def _(act):
            act.wait_ge(S["setup_dve"], 5)
            act.activation(qneg[:, :], qneg[:, :], ACT.Exp).then_inc(S["setup_act"], 1)
            act.wait_ge(S["setup_pe"], 1)
            act.activation(qb[:, :], ps[:, 0, 0:B], ACT.Relu, bias=col("bqin")).then_inc(S["setup_act"], 1)

            def cond_point(n, what, t):
                first = isinstance(n, int) and n == 0
                if what == "start":
                    act.wait_ge(S["cbx_ps"], at(n, 1, 0))
                    if not first:
                        act.wait_ge(S["yt_sb"], at(n - 1, 1, 0))
                    act.activation(cbx[:, :], ps[:, 3, :], ACT.Identity, bias=col("bcb")).then_inc(S["cbx_sb"], 1)
                    act.wait_ge(S["xlac_sb"], at(n, 1, 0))
                    act.activation(xlv[:, :, :].rearrange("p (k b) d -> p k b d", k=2),
                                   ps[:, 0:2, 0:2 * NX].rearrange("p k (b c) -> p k b c", b=2)[:, :, :, 0:P],
                                   ACT.Copy).then_inc(S["xlv_sb"], 1)
                elif what == "tt":
                    act.wait_ge(S["turned_ac"], at(n, T, t))
                    act.activation(tt[:, :], ps[:, 3, 0:P // 2].bitcast(BF16), ACT.Copy).then_inc(S["tt_sb"], 1)
                elif what in ("s0", "s1"):
                    hf = int(what[1])
                    k = 2 * t + hf
                    act.wait_ge(S["score_ps"], at(n, 2 * T, k))
                    act.activation(z[:, 2 * hf:2 * hf + 2, :], ps[:, 0:2, 0:P], ACT.Copy).then_inc(S["base_sb"], 1)
                elif what in ("p0", "p1"):
                    hf = int(what[1])
                    k = 2 * t + hf
                    act.wait_ge(S["max_sb"], at(n, 2 * T, k))
                    for b in (2 * hf, 2 * hf + 1):
                        act.activation(pe_[:, b, :], lk[:, b, :], ACT.Exp, bias=neg_mx[:, b:b + 1],
                                       accum_out=den[:, b:b + 1]).then_inc(S["exp_sb"], 1)
                    act.wait_ge(S["turned_p"], at(n, 2 * T, k))
                    act.activation(pt[:, 2 * hf:2 * hf + 2, :].rearrange("p b i -> p (b i)"), ps[:, 3 - hf, 0:2 * P],
                                   ACT.Copy).then_inc(S["pt_sb"], 1)

            def squares(f, k, src):
                for b in range(GB):
                    act.activation(sq[:, :], src[:, b * P:(b + 1) * P], ACT.Square, scale=P ** -0.5,
                                   accum_out=ss[:, k, b:b + 1]).then_inc(S["ss_sb"], 1)
                    act.wait_ge(S["ss_sb"], at(f, 3 * GB, k * GB + b))

            def ffn_point(n, what, u):
                f = n - 1
                first = isinstance(n, int) and n == 1
                if what == "vr":
                    act.wait_ge(S["yt_sb"], at(f, 1, 0))
                    act.activation(yh[:, :], yt[:, :], ACT.Copy).then_inc(S["yh_sb"], 1)
                    act.wait_ge(S["lg_sb"], at(f, 1, 0))
                    for k in range(2):
                        act.activation(va[:, 2 * k:2 * k + 2, :, 0:HD],
                                       ps[:, 4 + k, 0:2 * NR].rearrange("p (b c) -> p b c", b=2)[:, :, 0:P]
                                       .rearrange("p b (h d) -> p b h d", h=H), ACT.Copy).then_inc(S["va_sb"], 1)
                    act.wait_ge(S["yn_ps"], at(f, 1, 0))
                    act.activation(yn[:, :, :].rearrange("p b d -> p (b d)"), ps[:, 6, :], ACT.Copy).then_inc(S["yn_sb"], 1)
                elif what == "qk":
                    for s in range(2):
                        act.wait_ge(S["qk_ps"], at(f, 2, s))
                        act.activation(qk_h[:, s, :], ps[:, (7, 6)[s], :], ACT.Copy,
                                       scale=(HD ** -0.5, 1.0)[s]).then_inc(S["qk_hi"], 1)
                    act.wait_ge(S["lgneg_sb"], at(f, 1, 0))
                    act.activation(lge[:, :, :], lg[:, :, :], ACT.Exp).then_inc(S["lge_sb"], 1)
                elif what == "arrange":
                    act.wait_ge(S["arr_ps"], at(f, 8, 2 * u))
                    act.activation(qk[:, u, 0, :], ps[:, 4 if u % 2 == 0 else 7, :], ACT.Copy).then_inc(S["arrq_sb"], 1)
                elif what == "gates":
                    act.wait_ge(S["gT_ps"], at(f, 1, 0))
                    act.activation(gT[:, :], ps[0:32, 7, 0:W // 2].bitcast(BF16), ACT.Copy).then_inc(S["gT_sb"], 1)
                elif what == "spread":
                    for e in (u, u + 1):
                        act.wait_ge(S["spread_ps"], at(f, E, e))
                        act.activation(wb[:, e, :], ps[:, 4 + e % 2, :], ACT.Copy).then_inc(S["wb_sb"], 1)
                elif what == "attend":
                    if u < 16:
                        act.wait_ge(S["nmx_sb"], at(f, 16, u))
                        if u >= 2:
                            act.wait_ge(S["turned_pa"], at(f, 16, u - 2))
                        for g in range(4):
                            act.activation(pa[:, u % 2, g, :], ps[:, 4 + u % 2, g * P:(g + 1) * P], ACT.Exp,
                                           bias=nmx[:, u % 2, g:g + 1]).then_inc(S["pa_sb"], 1)
                    if 1 <= u <= 16:
                        q = u - 1
                        act.wait_ge(S["turned_pa"], at(f, 16, q))
                        if q >= 2:
                            act.wait_ge(S["o_ps"], at(f, 16, q - 2))
                        act.activation(pat[:, q % 2, :, :].rearrange("p g i -> p (g i)"), ps[:, 6, :], ACT.Copy)\
                            .then_inc(S["pat_sb"], 1)
                elif what == "mix":
                    act.wait_ge(S["onT_ps"], at(f, 1, 0))
                    act.activation(onT[:, :], ps[:, tile_bank("ont"), :], ACT.Copy).then_inc(S["onT_sb"], 1)
                elif what == "out_proj":
                    act.wait_ge(S["wo_ps"], at(f, 1, 0))
                    squares(f, 0, ps[:, tile_bank("wo"), :])
                elif what == "turn_h":
                    act.wait_ge(S["ht_ps"], at(f, 1, 0))
                    act.activation(hth[:, :], ps[:, tile_bank("ht"), :], ACT.Copy).then_inc(S["hth_sb"], 1)
                elif what == "chunk":
                    if u < NC:
                        act.wait_ge(S["h1_ps"], at(f, NC, u))
                        if u >= 2:
                            act.wait_ge(S["g1_sb"], at(f, NC, u - 2))
                        act.activation(th[:, u % 2, :], ps[:, tile_bank(("h1", u)), :], ACT.Tanh, scale=0.5)\
                            .then_inc(S["th_sb"], 1)
                    if u == E + 1:
                        act.wait_ge(S["down_ps"], at(f, NC, E - 1))
                        squares(f, 1, ps[:, 7, :])
                elif what == "last":
                    act.wait_ge(S["down_ps"], at(f, NC, NC - 1))
                    squares(f, 2, ps[:, 7, :])

            iterations(act, lambda n, cond, ffn, more: [
                (cond_point if k == "c" else ffn_point)(n, what, t) for k, what, t in points(cond, ffn)])

        @block.gpsimd
        def _(pool):
            kw5 = key_w[:, :, :].rearrange("p k (b t y) -> p k b t y", b=B, t=T)
            kb4 = key_b[:, :].rearrange("p (b t y) -> p b t y", b=B, t=T)

            def keys(n, t):
                for k in range(2):
                    i = pool.tensor_copy(rh[:, k, :, t % 2, P + TY:NV], kw5[:, 1 + k, bass.ds(n * GB, GB), t, :])
                return i

            def keys_x(n):
                x = key_w[:, 0, bass.ds(n * GB * T * TY, GB * T * TY)].rearrange("p (b c) -> p b c", b=GB)
                y = key_b[:, bass.ds(n * GB * T * TY, GB * T * TY)].rearrange("p (b c) -> p b c", b=GB)
                pool.tensor_copy(rx[:, :, P + TY:NX], x)
                return pool.tensor_copy(rb[:, :, P + TY:NX], y)

            pool.wait_ge(S["weights_in"], 16)
            pool.wait_ge(S["consts_in"], 5 * 16)
            pool.wait_ge(S["setup_dve"], 15)
            for k in range(2):
                for b in range(GB):
                    pool.tensor_copy(rh[:, k, b, :, 0:P], w(("v2", "v3")[k]).unsqueeze(1).to_broadcast([P, 2, P]))
                    pool.tensor_copy(rh[:, k, b, :, P:P + TY], qry_w[:, 1 + k, :].unsqueeze(1).to_broadcast([P, 2, TY]))
            pool.tensor_copy(rx[:, :, 0:P], w("v1").unsqueeze(1).to_broadcast([P, GB, P]))
            pool.tensor_copy(rx[:, :, P:P + TY], qry_w[:, 0, :].unsqueeze(1).to_broadcast([P, GB, TY]))
            pool.tensor_copy(rb[:, :, P:P + TY], qry_b[:, :].unsqueeze(1).to_broadcast([1, GB, TY]))
            for t in range(2):
                keys(0, t)
            pool.memset(half_pow[:, :], -0.5)
            pool.memset(eps[:, :], EPS)
            keys_x(0).then_inc(S["setup_pool"], 1)
            pool.wait_ge(S["setup_pool"], 1)

            def cond_point(n, what, t, more):
                if what == "pc" and t == 0 and more:
                    pool.wait_ge(S["xl_ps"], at(n, 2, 1))
                    keys_x(n + 1).then_inc(S["rx_next"], 1)
                if what == "tt" and (more or t < 2):
                    pool.wait_ge(S["v_ps"], at(n, T, t))
                    keys(n + (t + 2) // T, (t + 2) % T).then_inc(S["rh_next"], 1)

            def rstd_of(f, k):
                pool.wait_ge(S["ss_sb"], at(f, 3 * GB, k * GB + GB - 1))
                pool.tensor_tensor(rs[:, k, :], ss[:, k, :], eps[:, :], ALU.add).then_inc(S["ffn_pool"], 1)
                pool.wait_ge(S["ffn_pool"], at(f, 4, (0, 1, 3)[k]))
                pool.tensor_tensor(rstd[:, k, :], rs[:, k, :], half_pow[:, :], ALU.pow).then_inc(S["rstd_sb"], 1)

            def weighted(f, e):
                pool.wait_ge(S["g2_sb"], at(f, NC, e))
                if e == 0:
                    pool.wait_ge(S["wb_sb"], at(f, E, E - 1))
                if e >= 2:
                    pool.wait_ge(S["down_ps"], at(f, NC, e - 2))
                pool.tensor_tensor(gw[:, e % 2, :], g2[:, e % 3, :], wb[:, e, :], ALU.mult).then_inc(S["gw_sb"], 1)

            def ffn_point(n, what, u):
                f = n - 1
                first = isinstance(n, int) and n == 1
                if what == "out_proj":
                    rstd_of(f, 0)
                elif what == "chunk":
                    if u < E:
                        weighted(f, u)
                    if u == E + 1:
                        rstd_of(f, 1)
                elif what == "last":
                    rstd_of(f, 2)
                if what == "chunk" and u == E + 2:
                    pool.wait_ge(S["mo_sb"], at(f, 1, 0))
                    pool.wait_ge(S["hh_sb"], at(f, 1, 0))
                    pool.wait_ge(S["ffn_dve"], f * DVE_FFN + DVE_FFN - 4)
                    pool.tensor_tensor(res[:, :], hh[:, :], mo[:, :], ALU.add).then_inc(S["ffn_pool"], 1)
                    pool.wait_ge(S["xn_in"], 16 * n)
                    pool.wait_ge(S["ffn_pool"], at(f, 4, 2))
                    pool.tensor_tensor(res[:, :], res[:, :], xn[:, :, :].rearrange("p b d -> p (b d)"), ALU.add)\
                        .then_inc(S["res_sb"], 1)

            def iteration(n, cond, ffn, more):
                for k, what, t in points(cond, ffn):
                    if k == "f":
                        ffn_point(n, what, t)
                    else:
                        cond_point(n, what, t, more)

            iterations(pool, iteration)


def iterations(eng, body):
    body(0, True, False, True)
    body(1, True, True, True)
    with eng.Fori(2, NG - 1) as n:
        body(n, True, True, True)
    body(NG - 1, True, True, False)
    body(NG, False, True, False)


def _constants():
    import numpy as np
    bf = np.zeros((P, P + 512 + 16 * P + 4 * 512 + E * P), np.float32)
    bf[:, 0:P] = np.eye(P)
    ahead = np.triu(np.ones((P, P), np.float32), 1) * -1e30
    bf[:, P:P + 512] = np.tile(ahead, (1, 4))
    o = P + 512
    key = np.zeros((P, GB, TY, P), np.float32)
    qry = np.zeros((P, GB, TY, P), np.float32)
    for b in range(GB):
        for y in range(TY):
            for part in range(3):
                key[32 * b + 8 * part + TY + y, b, y, :] = 1
                qry[32 * b + 8 * part + y, b, y, :] = 1
    bf[:, o:o + 16 * P] = key.reshape(P, -1)
    o += 16 * P
    bf[:, o:o + 4 * 512] = qry.reshape(P, -1)
    o += 4 * 512
    for e in range(E):
        for part in range(3):
            bf[E * part + e, o + e * P:o + (e + 1) * P] = 1
    arr = np.zeros((P, 4, 4, P), np.float32)
    high = {0: (0, 1), 2: (0, 2)}
    for s in (0, 2):
        for g in range(4):
            for r in range(4):
                for copy in range(4):
                    which = s if copy in high[s] else s + 1
                    for d in range(HD):
                        arr[(4 * g + r) * HD + d, which, g, 32 * r + copy * HD + d] = 1
    tri = np.zeros((P, E, E), np.float32)
    tri[:, :, :] = np.tril(np.ones((E, E)), -1)
    f = np.concatenate([np.eye(P, dtype=np.float32), tri.reshape(P, -1), arr.reshape(P, -1)], 1)
    return bf, f.astype(np.float32)


def kernel(**inputs):
    import numpy as np
    import ml_dtypes
    import concourse.bacc as _bacc
    from concourse.bass_utils import run_bass_kernel_spmd as _run

    a = {k: np.asarray(v) for k, v in inputs.items()}
    c = lambda k: a["L0_cond_" + k]
    f = lambda k: a["L0_ffn_" + k]
    column = lambda v: v.reshape(P, 1)
    wT = {}
    wT["pl"], wT["pc"] = c("w_pl").T, c("w_pc").T
    wT["mu1"], wT["mu2"] = c("w_mu").T[:P], c("w_mu").T[P:]
    wT["cb1"], wT["cb2"] = c("w_cb").T[:P], c("w_cb").T[P:]
    for k in range(3):
        wT[f"v{k + 1}"] = c("w_v").T[k * P:(k + 1) * P]
    wT["wq"], wT["wk"] = c("w_q"), c("w_k")
    wT["qin"], wT["pk"], wT["pv"] = c("w_qin").T, c("w_pk").T, c("w_pv").T
    wT["qt"] = np.concatenate([a["fside_BxSxS_0"][t].T for t in range(T)], 1)
    wT["bqt"] = a["mask_BxS_ff0"][:T].T
    wT["wes1"], wT["wes2"] = a["cond_2048"][:TY, :P].T, a["cond_2048"][:TY, P:].T
    wT["qenc"] = a["fside_BxS_0"].T
    wT["init"] = column(c("init_mem"))
    for k in ("qin", "pl", "pc", "q", "k", "pk", "pv", "mu", "cb"):
        wT["b" + k] = column(c("b_" + k))
    wT["wo"] = f("wo")
    wT["vr"] = np.concatenate([f("wv"), f("router_w")], 1)
    wT["w2"] = np.concatenate([f("w2")[k * P:(k + 1) * P] for k in range(FC)], 1)
    wT["ew2"] = np.concatenate([f("ew2")[e] for e in range(E)], 1)
    for k, (lo, hi) in COLS.items():
        assert wT[k].shape == (P, hi - lo), (k, wT[k].shape)
    wts = np.concatenate([wT[k] for k in COLS], 1)
    sp = [f("wq"), f("wk")]
    for e in range(E):
        sp += [f("ew1")[e], f("ew3")[e]]
    for k in range(FC):
        sp += [f("w1")[:, k * P:(k + 1) * P], f("w3")[:, k * P:(k + 1) * P]]
    splits = np.concatenate(sp, 1)
    bf, cf = _constants()
    arrays = {
        "xT": a["x"].transpose(2, 0, 1).reshape(P, B * P),
        "xN": a["x"].transpose(1, 0, 2),
        "adj": a["itok_BxSxS_0_4"].astype(np.int32).transpose(1, 0, 2),
        "msk": a["mask_BxS_ff1"].reshape(1, B * P),
        "wts": wts, "splits": splits,
        "norms": np.stack([f("attn_norm_w"), f("moe_norm_w"), f("ff_norm_w")]),
        "rows": np.tile(c("b_v").reshape(1, P), (1, GB)),
        "cst_bf": bf.astype(ml_dtypes.bfloat16), "cst_f": cf,
    }
    arrays = {k + "_dram": np.ascontiguousarray(v) for k, v in arrays.items()}
    nc = _bacc.Bacc("TRN2", target_bir_lowering=False, num_devices=1)
    args = [nc.dram_tensor(k, v.shape, mybir.dt.from_np(v.dtype), kind="ExternalInput").ap() for k, v in arrays.items()]
    out = nc.dram_tensor("out_dram", (P, B, P), F32, kind="ExternalOutput").ap()
    build(nc, *args, out)
    r = _run(nc, [arrays], core_ids=[0])
    return np.ascontiguousarray(r.results[0]["out_dram"].transpose(1, 0, 2))
```

```python
from contextlib import ExitStack

import concourse.bass as bass
from concourse import mybir

F32 = mybir.dt.float32
F32R = mybir.dt.float32r
BF16 = mybir.dt.bfloat16
U8 = mybir.dt.uint8
I32 = mybir.dt.int32
ALU = mybir.AluOpType
ACT = mybir.ActivationFunctionType
AX_X = mybir.AxisListType.X

P = 128
B = 32
GB = 4
NG = B // GB
W = GB * P
T = 4
TY = 4
H = 16
HD = P // H
E = 8
FC = 4
NC = E + FC
EPS = 1e-5
ALPHA = 0.2
MASKED = -9e15 / ALPHA
NV = P + 2 * TY
NX = P + TY + T * TY
NR = P + E

def _cols(cols, widths):
    at = 0
    for name, width in widths:
        cols[name] = (at, at + width)
        at += width
    return at


SETUP_COLS, COLS = {}, {}
NSET = _cols(SETUP_COLS, (
    ("qin", P), ("bqin", 1), ("qenc", B), ("qt", T * P), ("bqt", T), ("pk", P), ("pv", P), ("bpk", 1), ("bpv", 1),
    ("wes1", TY), ("wes2", TY), ("bq", 1), ("bk", 1), ("wq", 3 * P), ("wk", 3 * P), ("v1", P), ("v2", P), ("v3", P)))
NW = _cols(COLS, (
    ("pl", P), ("pc", P), ("mu1", P), ("mu2", P), ("cb1", P), ("cb2", P), ("init", 1), ("bpl", 1), ("bpc", 1),
    ("bmu", 1), ("bcb", 1), ("bv", 1), ("wo", P), ("vr", NR), ("w2", FC * P), ("ew2", E * P)))
NS = 2 * P + 2 * NC * P


ORDER = """
        | vr.0 turn_y.0
start.0 | q.0 k.0
pc.0    | choose.0 arrange.0 arrange.1
vp.0    | arrange.2 arrange.3
tt.0    | gates.0
s0.0    | spread.0 spread.1 spread.2 spread.3 spread.4
z0.0    |
s1.0    | spread.5 spread.6 spread.7 scores.0
z1.0    | exps.0 scores.1
p0.0    | exps.1 turn.0 scores.2
pt0.0   | exps.2 turn.1 scores.3
p1.0    | exps.3 values.0
pt1.0   | turn.2 scores.4
msg.0   | exps.4 values.1 scores.5
mu.0    | turn.3 exps.5 values.2 scores.6
pc.1    | turn.4 exps.6
vp.1    | values.3 turn.5
tt.1    | scores.7 exps.7 values.4 turn.6
s0.1    | scores.8 exps.8 values.5
z0.1    | scores.9 turn.7
s1.1    | exps.9 values.6
p0.1    | turn.8 scores.10
z1.1    | exps.10 turn.9 values.7 scores.11 exps.11 values.8 turn.10
pt0.1   |
p1.1    |
pt1.1   | scores.12 exps.12 values.9 scores.13 turn.11 exps.13
msg.1   | values.10
mu.1    | turn.12 scores.14 exps.14
pc.2    | values.11 turn.13 scores.15 exps.15 values.12
vp.2    | turn.14 values.13
tt.2    | turn.15 values.14 mix.0 values.15
s0.2    | out_proj.0
s1.2    |
z0.2    | h1.0 norm_h.0 h3.0 h1.1 g1.0 h3.1
z1.2    | g2.0 turn_h.0
p0.2    | g1.1 g2.1 h1.2 g1.2 h3.2 g2.2
pt0.2   | down.0
p1.2    | h1.3 g1.3
msg.2   | h3.3 g2.3 down.1
mu.2    |
pt1.2   | h1.4 g1.4 h3.4 g2.4 h1.5 down.2
pc.3    | g1.5 h3.5
vp.3    | g2.5 down.3 h1.6
tt.3    | g1.6 h3.6 g2.6
s0.3    | down.4 h1.7
z0.3    | g1.7 h3.7 g2.7 down.5
s1.3    | h1.8 g1.8
p0.3    | h3.8
z1.3    | g2.8 down.6
pt0.3   | h1.9 g1.9 h3.9 down.7
p1.3    | norm_m.0 g2.9 h1.10
pt1.3   | g1.10 h3.10
msg.3   | g2.10 down.8 h1.11 g1.11
mu.3    | h3.11 g2.11 down.9 down.10 down.11
cb.0    | last.0
"""


def points(cond, ffn):
    out = []
    for line in ORDER.strip("\n").splitlines():
        c, f = line.split("|")
        for stage, name in [("c", x) for x in c.split()] + [("f", x) for x in f.split()]:
            if cond if stage == "c" else ffn:
                what, index = name.split(".")
                out.append((stage, what, int(index)))
    return out


TILES = (["invT", "wo", ("h1", 0), ("h3", 0), ("h1", 1), ("h3", 1), "ht"]
         + [(h, c) for c in range(2, NC) for h in ("h1", "h3")])


def tile_bank(tile):
    return 4 + TILES.index(tile) % 3


def build(nc, xT, xN, adj, msk, setup_w, wts, splits, norms, cst_bf, cst_f, out):
    with ExitStack() as ctx:
        def sb(name, shape, dt=F32):
            return ctx.enter_context(nc.sbuf_tensor(name, shape, dt))

        def sem(name):
            return ctx.enter_context(nc.semaphore(name))

        ps = ctx.enter_context(nc.psum_tensor("ps", [P, 8, 512], F32))

        wt = sb("wt", [P, NW])
        hi_w = sb("hi_w", [P, NS], F32R)
        lo_w = sb("lo_w", [P, NS], F32R)
        cb = sb("cb", [P, cst_bf.shape[1]], BF16)
        ident = sb("ident", [P, P])
        arr = sb("arr", [P, 4 * 4 * P], F32R)
        tri = sb("tri", [P, E, E])
        nrm = sb("nrm", [P, 3, P])
        half_pow = sb("half_pow", [P, GB])
        eps = sb("eps", [P, GB])
        ones = sb("ones", [P, 4])
        key_w = sb("key_w", [P, 3, B * T * TY])
        key_b = sb("key_b", [P, B * T * TY])
        qry_w = sb("qry_w", [P, 3, TY])
        qry_b = sb("qry_b", [P, TY])
        vc = sb("vc", [P, T, B])
        kc = sb("kc", [P, T, B])
        rh = sb("rh", [P, 2, GB, 2, NV])
        rx = sb("rx", [P, GB, NX])
        qb = sb("qb", [P, B])
        qneg = sb("qneg", [P, B])
        cmd = sb("cmd", [P, T, B])

        xt = sb("xt", [P, W])
        ad = sb("ad", [P, W], I32)
        mb = sb("mb", [P, W])
        is_ty = sb("is_ty", [P, TY - 1, W], U8)
        pen = sb("pen", [P, W], BF16)
        pl = sb("pl", [P, W])
        cbx = sb("cbx", [P, W])
        xlv = sb("xlv", [P, GB, P])
        xlac = sb("xlac", [P, GB, T, 2 * TY])
        xc = sb("xc", [P, W])
        pr = sb("pr", [P, W])
        ac = sb("ac", [P, GB, 2 * TY])
        ac_r = sb("ac_r", [P, GB, 2 * TY])
        t3 = sb("t3", [P, GB, 32], BF16)
        tt = sb("tt", [P, P], BF16)
        z = sb("z", [P, GB, P])
        lk = sb("lk", [P, GB, P])
        neg_mx = sb("neg_mx", [P, GB])
        den = sb("den", [P, GB])
        carrier = sb("carrier", [1, 1])
        rden = sb("rden", [P, GB])
        pe_ = sb("pexp", [P, GB, P])
        pn = sb("pn", [P, GB, P])
        pt = sb("pt", [P, GB, P])
        v = sb("v", [P, GB, P])
        ms = sb("ms", [P, W])
        yt = sb("yt", [P, W])

        xn = sb("xn", [P, GB, P])
        yh = sb("yh", [P, W], F32R)
        yl = sb("yl", [P, W], F32R)
        yn = sb("yn", [P, GB, P])
        qk_h = sb("qk_h", [P, 2, W], F32R)
        qk_l = sb("qk_l", [P, 2, W], F32R)
        qk = sb("qk", [P, 4, 2, W], F32R)
        va = sb("va", [P, GB, H, HD])
        va_pad = sb("va_pad", [P, H * (P + HD)])
        lg = sb("lg", [P, GB, E])
        lgm = sb("lgm", [P, GB])
        lge = sb("lge", [P, GB, E])
        lgs = sb("lgs", [P, GB])
        prb = sb("prb", [P, GB, E])
        gt = sb("gt", [P, GB, E, E])
        eq = sb("eq", [P, GB, E, E])
        rank = sb("rank", [P, GB, E])
        gate = sb("gate", [P, GB, E])
        gate_r = sb("gate_r", [P, GB, E])
        g3 = sb("g3", [P, GB, 32], BF16)
        gT = sb("gT", [32, W], BF16)
        wb = sb("wb", [P, E, W])
        nmx = sb("nmx", [P, 2, 4])
        pa = sb("pa", [P, 2, 4, P])
        pat = sb("pat", [P, 2, 4, P])
        sums = sb("sums", [P, GB, H])
        inv = sb("inv", [P, GB, H, HD])
        onT = sb("onT", [P, W])
        sq = sb("sq", [P, P])
        ss = sb("ss", [P, 3, GB])
        rs = sb("rs", [P, 3, GB])
        rstd = sb("rstd", [P, 3, GB])
        nh = onT
        hh = sb("hh", [P, W])
        hth = qk_h[:, 0, :]
        htl = qk_h[:, 1, :]
        th = pa[:, :, :, :].rearrange("p k g i -> p k (g i)")
        g1 = pat[:, :, :, :].rearrange("p k g i -> p k (g i)")
        gg = sb("gg", [P, 5, W])
        g2, gw = gg[:, 0:3, :], gg[:, 3:5, :]
        ws = gg[:, :, :].rearrange("p k w -> p (k w)")[:, 0:NSET]
        mo = sb("mo", [P, W])
        res, fo = mo, hh

        wb_flat = wb[:, :, :].rearrange("p e w -> p (e w)")
        arr_in = [x[:, :, :, :].rearrange("p k g i -> p (k g i)") for x in (pa, pat)]

        def w(name):
            if name in SETUP_COLS:
                a, b = SETUP_COLS[name]
                return ws[:, a:b]
            a, b = COLS[name]
            return wt[:, a:b]

        def col(name):
            return w(name)[:, 0:1]

        def part(name, k):
            return w(name)[:, k * P:(k + 1) * P]

        idb = cb[:, 0:P]
        causal = cb[:, P:P + 512]
        o = P + 512
        sel_key = cb[:, o:o + 16 * P].rearrange("k (b y j) -> k b y j", b=GB, y=TY)
        o += 16 * P
        sel_qry = cb[:, o:o + 4 * 512].rearrange("k (b j) -> k b j", b=GB)
        o += 4 * 512
        sel_exp = cb[0:32, o:o + E * P].rearrange("k (e j) -> k e j", e=E)
        arr4 = arr[:, :].rearrange("k (s g j) -> k s g j", s=4, g=4)

        S = {}
        for name in (
            "query_in", "setup_in", "weights_in", "splits_in", "late_in", "xt_in", "adj_in", "mask_in", "xn_in", "out_stored",
            "setup_pe", "setup_dve", "setup_act", "setup_pool", "split_hi", "split_lo",
            "pl_ps", "cbx_ps", "xl_ps", "pc_ps", "v_ps", "turned_ac", "score_ps", "turned_p", "msg_ps", "mu_ps", "cb_ps",
            "edges_ready", "pl_sb", "xlac_sb", "xc_sb", "prod_sb", "t3_sb", "v_sb", "z_sb", "max_sb", "probs_sb",
            "msg_sb", "yt_sb", "cond_dve", "rden_sb", "cbx_sb", "xlv_sb", "tt_sb", "base_sb", "exp_sb", "pt_sb",
            "rh_next", "rx_next",
            "vr_ps", "yn_ps", "qk_ps", "arr_ps", "gT_ps", "spread_ps", "s_ps", "turned_pa", "o_ps", "invT_ps", "wo_ps",
            "ht_ps", "h1_ps", "h3_ps", "down_ps", "lg_sb", "yl_sb", "qk_lo", "arrk_sb", "lgneg_sb", "g3_sb", "nmx_sb", "inv_sb", "invT_sb", "va_pad_sb",
            "hh_sb", "htl_sb", "g1_sb", "g2_sb", "mo_sb", "fo_sb", "ffn_dve", "yh_sb", "va_sb", "yn_sb", "qk_hi",
            "arrq_sb", "lge_sb", "gT_sb", "wb_sb", "pa_sb", "pat_sb", "onT_sb", "ss_sb", "hth_sb", "th_sb", "gw_sb",
            "rstd_sb", "res_sb", "ffn_pool",
        ):
            S[name] = sem(name)
        block = ctx.enter_context(nc.Block())

        def at(n, per, k):
            return n * per + k + 1

        def step(name):
            return 1 + ("t3", "g3", "va_pad", "qneg", "qb", "cmd", "kc", "kw", "vc", "qry_w", "qry_b",
                        "rh0", "rhq0", "rh1", "rhq1", "rx", "rxq", "key_w", "key_b", "w2").index(name)

        bias_q, bias_k = pn[:, 0, :], pn[:, 1, :]

        DVE_COND, DVE_FFN = 6 + T * (4 + 2 * 1), 25

        @block.sync
        def _(sp):
            cut = SETUP_COLS["qt"][0]
            sp.dma_start(ws[:, 0:cut], setup_w[:, 0:cut]).then_inc(S["query_in"], 16)
            sp.dma_start(ws[:, cut:NSET], setup_w[:, cut:NSET]).then_inc(S["setup_in"], 16)
            sp.dma_start(xt[:, :], xT[:, 0:W]).then_inc(S["xt_in"], 16)
            sp.dma_start(mb[:, :], msk[:, 0:W].partition_broadcast(P).rearrange("p a w -> p (a w)")).then_inc(S["mask_in"], 16)
            sp.dma_start(ad[:, :].rearrange("p (b j) -> p b j", b=GB), adj[:, 0:GB, :]).then_inc(S["adj_in"], 16)
            cut = COLS["wo"][0]
            sp.dma_start(wt[:, 0:cut], wts[:, 0:cut]).then_inc(S["weights_in"], 16)
            sp.dma_start(cb[:, :], cst_bf).then_inc(S["weights_in"], 16)
            sp.dma_start(ident[:, :], cst_f[:, 0:P]).then_inc(S["weights_in"], 16)
            sp.dma_start(wb_flat[:, W:W + NS], splits).then_inc(S["splits_in"], 16)
            for k in range(2):
                sp.dma_start(arr_in[k], cst_f[:, P + E * E + k * 8 * P:P + E * E + (k + 1) * 8 * P])\
                    .then_inc(S["splits_in"], 16)
            sp.dma_start(wt[:, cut:NW], wts[:, cut:NW]).then_inc(S["late_in"], 16)
            sp.dma_start(tri[:, :, :], cst_f[:, P:P + E * E].rearrange("p (a b) -> p a b", a=E)).then_inc(S["late_in"], 16)
            sp.dma_start(nrm[:, :, :], norms.partition_broadcast(P)).then_inc(S["late_in"], 16)

            def iteration(n, cond, ffn, more):
                if ffn:
                    if not (isinstance(n, int) and n == 1):
                        sp.wait_ge(S["res_sb"], at(n - 2, 1, 0))
                    sp.dma_start(xn[:, :, :], xN[:, bass.ds((n - 1) * GB, GB), :]).then_inc(S["xn_in"], 16)
                if more:
                    sp.wait_ge(S["xl_ps"], at(n, 2, 1))
                    sp.dma_start(xt[:, :], xT[:, bass.ds((n + 1) * W, W)]).then_inc(S["xt_in"], 16)
                    sp.wait_ge(S["edges_ready"], at(n, 1, 0))
                    sp.dma_start(ad[:, :].rearrange("p (b j) -> p b j", b=GB),
                                 adj[:, bass.ds((n + 1) * GB, GB), :]).then_inc(S["adj_in"], 16)
                    sp.wait_ge(S["xc_sb"], at(n, 5, 3))
                    sp.dma_start(mb[:, :], msk[:, bass.ds((n + 1) * W, W)].partition_broadcast(P)
                                 .rearrange("p a w -> p (a w)")).then_inc(S["mask_in"], 16)
                if ffn:
                    sp.wait_ge(S["fo_sb"], at(n - 1, 1, 0))
                    sp.dma_start(out[:, bass.ds((n - 1) * GB, GB), :],
                                 fo[:, :].rearrange("p (b j) -> p b j", b=GB)).then_inc(S["out_stored"], 16)

            iterations(sp, iteration)
            sp.wait_ge(S["out_stored"], 16 * NG)

        @block.tensor
        def _(pe):
            def mm(out_, lhsT, rhs, start=True, stop=True, **kw):
                return pe.matmul(out_, lhsT, rhs, start=start, stop=stop, skip_group_check=True, **kw)

            def split3(out_, k, ah, al, start=True, sl=slice(None)):
                wh, wl = hi_w[:, k * P:(k + 1) * P], lo_w[:, k * P:(k + 1) * P]
                mm(out_, wh, ah, start=start, stop=False)
                mm(out_, wh, al, start=False, stop=False)
                return mm(out_, wl, ah, start=False, stop=True)

            pe.wait_ge(S["query_in"], 16)
            mm(ps[:, 0, 0:B], w("qin"), w("qenc")).then_inc(S["setup_pe"], 1)
            pe.wait_ge(S["setup_in"], 16)
            pe.wait_ge(S["setup_dve"], step("qb"))
            for t in range(T):
                i = mm(ps[:, 1, t * B:(t + 1) * B], part("qt", t), qb[:, :], start=(t == 0))
            i.then_inc(S["setup_pe"], 1)
            pe.wait_ge(S["setup_dve"], step("cmd"))
            cm = cmd[:, :, :].rearrange("p t b -> p (t b)")
            mm(ps[:, 2, 0:T * B], w("pk"), cm)
            mm(ps[:, 3, 0:T * B], w("pv"), cm).then_inc(S["setup_pe"], 1)
            pe.wait_ge(S["setup_pool"], 1)
            for k in range(3):
                mm(ps[:, 1, P + k * TY:P + (k + 1) * TY], part("wq", k), w("wes1"), start=(k == 0))
            mm(ps[:, 1, P + 3 * TY:P + 4 * TY], bias_q, w("wes1"), start=False).then_inc(S["setup_pe"], 1)
            pe.wait_ge(S["setup_dve"], step("kw"))
            kw = wb[:, 0, :]
            for k in range(3):
                mm(ps[:, 4 + k, :], part("wk", k), kw).then_inc(S["setup_pe"], 1)
            mm(ps[:, 7, :], bias_k, kw).then_inc(S["setup_pe"], 1)
            pe.wait_ge(S["setup_dve"], step("qry_b"))
            pe.wait_ge(S["weights_in"], 3 * 16)

            def cond_point(n, what, t):
                first = isinstance(n, int) and n == 0
                if what == "start":
                    if not first:
                        pe.wait_ge(S["yt_sb"], at(n - 1, 1, 0))
                    pe.wait_ge(S["xt_in"], 16 * n + 16)
                    mm(ps[:, 2, :], w("pl"), xt[:, :]).then_inc(S["pl_ps"], 1)
                    mm(ps[:, 3, :], w("cb1"), xt[:, :]).then_inc(S["cbx_ps"], 1)
                    if first:
                        pe.wait_ge(S["setup_dve"], step("key_b"))
                        pe.wait_ge(S["setup_pool"], 2)
                    else:
                        pe.wait_ge(S["rx_next"], n)
                    for b in range(GB):
                        o_ = ps[:, b // 2, b % 2 * NX:(b % 2 + 1) * NX]
                        i = mm(o_, xt[:, b * P:(b + 1) * P], rx[:, b, :], start=(b % 2 == 0))
                        if b % 2:
                            i.then_inc(S["xl_ps"], 1)
                elif what == "pc":
                    if t == 0:
                        pe.wait_ge(S["pl_sb"], at(n, 1, 0))
                    pe.wait_ge(S["xc_sb"], at(n, 5, t))
                    mm(ps[:, 2, :], w("pc"), xc[:, :]).then_inc(S["pc_ps"], 1)
                    if t == 0:
                        pe.wait_ge(S["xlac_sb"], at(n, 1, 0))
                        pe.wait_ge(S["xlv_sb"], at(n, 1, 0))
                    if not first or t >= 2:
                        pe.wait_ge(S["rh_next"], 4 * n + t - 1)
                    for b in range(GB):
                        mm(ps[:, b // 2, b % 2 * NV:(b % 2 + 1) * NV], xc[:, b * P:(b + 1) * P], rh[:, 0, b, t % 2, :],
                           start=(b % 2 == 0), stop=False)
                elif what == "vp":
                    pe.wait_ge(S["prod_sb"], at(n, T, t))
                    for b in range(GB):
                        i = mm(ps[:, b // 2, b % 2 * NV:(b % 2 + 1) * NV], pr[:, b * P:(b + 1) * P], rh[:, 1, b, t % 2, :],
                               start=False)
                    i.then_inc(S["v_ps"], 1)
                elif what == "tt":
                    pe.wait_ge(S["t3_sb"], at(n, T, t))
                    if t == 0:
                        pe.wait_ge(S["cbx_sb"], at(n, 1, 0))
                    pe.transpose(ps[:, 3, 0:P // 2].bitcast(BF16), t3[:, :, :].rearrange("p b k -> p (b k)"),
                                 idb).then_inc(S["turned_ac"], 1)
                elif what in ("s0", "s1"):
                    hf = int(what[1])
                    if hf == 0:
                        pe.wait_ge(S["tt_sb"], at(n, T, t))
                        pe.wait_ge(S["v_sb"], at(n, T, t))
                        if t == 0:
                            pe.wait_ge(S["edges_ready"], at(n, 1, 0))
                    else:
                        pe.wait_ge(S["z_sb"], at(n, 2 * T, 2 * t))
                    for k in range(2):
                        b = 2 * hf + k
                        mm(ps[:, k, :], tt[:, :], sel_qry[:, b, :], start=True, stop=False)
                        mm(ps[:, k, 0:P], idb, pen[:, b * P:(b + 1) * P], start=False, stop=False)
                        for y in range(TY):
                            i = mm(ps[:, k, y * P:(y + 1) * P], sel_key[:, b, y, :], tt[:, :], start=False)
                    i.then_inc(S["score_ps"], 1)
                elif what in ("p0", "p1"):
                    hf = int(what[1])
                    pe.wait_ge(S["probs_sb"], at(n, 2 * T, 2 * t + hf))
                    for k in range(2):
                        b = 2 * hf + k
                        i = pe.transpose(ps[:, 3 - hf, k * P:(k + 1) * P], pn[:, b, :], ident[:, :])
                    i.then_inc(S["turned_p"], 1)
                elif what == "msg":
                    pe.wait_ge(S["pt_sb"], at(n, 2 * T, 2 * t + 1))
                    pe.wait_ge(S["z_sb"], at(n, 2 * T, 2 * t + 1))
                    for b in range(GB):
                        i = mm(ps[:, 0, b * P:(b + 1) * P], v[:, b, :], pt[:, b, :], start=(b == 0))
                    i.then_inc(S["msg_ps"], 1)
                elif what == "mu":
                    mm(ps[:, 1, :], w("mu1"), xc[:, :], stop=False)
                    pe.wait_ge(S["msg_sb"], at(n, T, t))
                    mm(ps[:, 1, :], w("mu2"), ms[:, :], start=False).then_inc(S["mu_ps"], 1)
                elif what == "cb":
                    pe.wait_ge(S["xc_sb"], at(n, 5, 4))
                    pe.wait_ge(S["pt_sb"], at(n, 2 * T, 2 * T - 1))
                    mm(ps[:, 2, :], w("cb2"), xc[:, :]).then_inc(S["cb_ps"], 1)

            def tile_free(f, tile):
                i = TILES.index(tile)
                if i < 2:
                    pe.wait_ge(S["pa_sb"], at(f, 64, 4 * (14 + i) + 3))
                    return
                if i == 2:
                    pe.wait_ge(S["pat_sb"], at(f, 16, 15))
                    return
                old = TILES[i - 3]
                if old == "invT":
                    pe.wait_ge(S["invT_sb"], at(f, 1, 0))
                elif old == "wo":
                    pe.wait_ge(S["hh_sb"], at(f, 1, 0))
                elif old == "ht":
                    pe.wait_ge(S["htl_sb"], at(f, 1, 0))
                elif old[0] == "h1":
                    pe.wait_ge(S["g1_sb"], at(f, NC, old[1]))
                else:
                    pe.wait_ge(S["g2_sb"], at(f, NC, old[1]))

            def down(f, c):
                if c == 0:
                    pe.wait_ge(S["onT_sb"], at(f, 1, 0))
                if c == E:
                    pe.wait_ge(S["mo_sb"], at(f, 1, 0))
                if c < E:
                    pe.wait_ge(S["gw_sb"], at(f, E, c))
                    a, m = gw[:, c % 2, :], part("ew2", c)
                else:
                    pe.wait_ge(S["g2_sb"], at(f, NC, c))
                    a, m = g2[:, c % 3, :], part("w2", c - E)
                for b in range(GB):
                    i = mm(ps[:, 7, b * P:(b + 1) * P], a[:, b * P:(b + 1) * P], m,
                           start=(b == 0 and c in (0, E)), stop=(c in (E - 1, NC - 1)))
                i.then_inc(S["down_ps"], 1)

            def ffn_point(n, what, u):
                f = n - 1
                first = isinstance(n, int) and n == 1
                if what == "vr":
                    pe.wait_ge(S["yt_sb"], at(f, 1, 0))
                    if first:
                        pe.wait_ge(S["late_in"], 3 * 16)
                    else:
                        pe.wait_ge(S["g2_sb"], at(f - 1, NC, NC - 1))
                        pe.wait_ge(S["g1_sb"], at(f - 1, NC, NC - 1))
                    for b in range(GB):
                        i = mm(ps[:, 4 + b // 2, b % 2 * NR:(b % 2 + 1) * NR], yt[:, b * P:(b + 1) * P], w("vr"),
                               start=(b % 2 == 0))
                    i.then_inc(S["vr_ps"], 1)
                elif what == "turn_y":
                    for b in range(GB):
                        i = pe.transpose(ps[:, 6, b * P:(b + 1) * P], yt[:, b * P:(b + 1) * P], ident[:, :])
                    i.then_inc(S["yn_ps"], 1)
                elif what == "q":
                    pe.wait_ge(S["yl_sb"], at(f, 1, 0))
                    if first:
                        pe.wait_ge(S["split_lo"], 2)
                    else:
                        pe.wait_ge(S["fo_sb"], at(f - 1, 1, 0))
                    split3(ps[:, 7, :], 0, yh[:, :], yl[:, :]).then_inc(S["qk_ps"], 1)
                elif what == "k":
                    pe.wait_ge(S["yn_sb"], at(f, 1, 0))
                    split3(ps[:, 6, :], 1, yh[:, :], yl[:, :]).then_inc(S["qk_ps"], 1)
                elif what == "arrange":
                    for s in range(2):
                        bank = (4, 5)[s] if u % 2 == 0 else (7, 6)[s]
                        pe.wait_ge(S["qk_lo"], at(f, 2, 1))
                        if u == 0:
                            pe.wait_ge(S["lg_sb"], at(f, 1, 0))
                            pe.wait_ge(S["va_sb"], at(f, 2, 1))
                            if first:
                                pe.wait_ge(S["split_hi"], 3)
                        elif u >= 2:
                            pe.wait_ge(S["arrk_sb" if s else "arrq_sb"], at(f, 4, u - 2))
                        mm(ps[:, bank, :], arr4[:, 2 * s, u, :], qk_h[:, s, :], stop=False)
                        mm(ps[:, bank, :], arr4[:, 2 * s + 1, u, :], qk_l[:, s, :], start=False).then_inc(S["arr_ps"], 1)
                elif what == "gates":
                    pe.wait_ge(S["g3_sb"], at(f, 1, 0))
                    pe.wait_ge(S["arrq_sb"], at(f, 4, 3))
                    for b in range(GB):
                        i = pe.transpose(ps[0:32, 7, b * 64:(b + 1) * 64].bitcast(BF16), g3[:, b, :], idb)
                    i.then_inc(S["gT_ps"], 1)
                elif what == "spread":
                    if u == 0:
                        pe.wait_ge(S["gT_sb"], at(f, 1, 0))
                        pe.wait_ge(S["arrq_sb"], at(f, 4, 2))
                    elif u == 1:
                        pe.wait_ge(S["arrk_sb"], at(f, 4, 2))
                    else:
                        pe.wait_ge(S["wb_sb"], at(f, E, u - 2))
                    mm(ps[:, 4 + u % 2, :], sel_exp[:, u, :], gT[:, :]).then_inc(S["spread_ps"], 1)
                elif what == "scores":
                    b, r = divmod(u, 4)
                    if u < 2:
                        pe.wait_ge(S["wb_sb"], at(f, E, 6 + u))
                        pe.wait_ge(S["arrk_sb"], at(f, 4, 3))
                        pe.wait_ge(S["arrq_sb"], at(f, 4, 3))
                    else:
                        pe.wait_ge(S["pa_sb"], at(f, 64, 4 * (u - 2) + 3))
                    mm(ps[:, 4 + u % 2, :], idb, causal, stop=False)
                    for g in range(4):
                        i = mm(ps[:, 4 + u % 2, g * P:(g + 1) * P], qk[32 * r:32 * r + 32, g, 0, b * P:(b + 1) * P],
                               qk[32 * r:32 * r + 32, g, 1, b * P:(b + 1) * P], start=False,
                               tile_position=(32 * r, 0))
                    i.then_inc(S["s_ps"], 1)
                elif what == "values":
                    b, r = divmod(u, 4)
                    pe.wait_ge(S["pat_sb"], at(f, 16, u))
                    pe.wait_ge(S["va_pad_sb"], at(f, 16, u))
                    if u == 0:
                        pe.wait_ge(S["gT_sb"], at(f, 1, 0))
                    for g in range(4):
                        h = 4 * g + r
                        i = mm(ps[:, 7, b * P:(b + 1) * P], va_pad[:, h * P:(h + 1) * P], pat[:, u % 2, g, :],
                               start=(u == 0 and g == 0))
                    i.then_inc(S["o_ps"], 1)
                elif what == "turn":
                    pe.wait_ge(S["pa_sb"], at(f, 64, 4 * u + 3))
                    if u:
                        pe.wait_ge(S["pat_sb"], at(f, 16, u - 1))
                    for g in range(4):
                        i = pe.transpose(ps[:, 6, g * P:(g + 1) * P], pa[:, u % 2, g, :], ident[:, :])
                    i.then_inc(S["turned_pa"], 1)
                elif what == "mix":
                    pe.wait_ge(S["inv_sb"], at(f, GB, GB - 1))
                    tile_free(f, "invT")
                    for b in range(GB):
                        i = pe.transpose(ps[:, tile_bank("invT"), b * P:(b + 1) * P],
                                         inv[:, b, :, :].rearrange("p h d -> p (h d)"), ident[:, :])
                    i.then_inc(S["invT_ps"], 1)
                elif what == "out_proj":
                    pe.wait_ge(S["onT_sb"], at(f, 1, 0))
                    tile_free(f, "wo")
                    for b in range(GB):
                        i = mm(ps[:, tile_bank("wo"), b * P:(b + 1) * P], onT[:, b * P:(b + 1) * P], w("wo"), start=(b == 0))
                    i.then_inc(S["wo_ps"], 1)
                elif what == "turn_h":
                    pe.wait_ge(S["hh_sb"], at(f, 1, 0))
                    tile_free(f, "ht")
                    for b in range(GB):
                        i = pe.transpose(ps[:, tile_bank("ht"), b * P:(b + 1) * P], hh[:, b * P:(b + 1) * P], ident[:, :])
                    i.then_inc(S["ht_ps"], 1)
                elif what in ("h1", "h3"):
                    if u == E:
                        pe.wait_ge(S["htl_sb"], at(f, 1, 0))
                    ah, al = (yh, yl) if u < E else (hth, htl)
                    tile_free(f, (what, u))
                    split3(ps[:, tile_bank((what, u)), :], 2 + 2 * u + (what == "h3"), ah[:, :], al[:, :])\
                        .then_inc(S[what + "_ps"], 1)
                elif what == "down":
                    down(f, u)

            iterations(pe, lambda n, cond, ffn, more: [
                (cond_point if k == "c" else ffn_point)(n, what, t) for k, what, t in points(cond, ffn)])

        @block.vector
        def _(dve):
            count = [0]

            def setup(name, ins):
                count[0] += 1
                assert step(name) == count[0]
                ins.then_inc(S["setup_dve"], 1)
                dve.wait_ge(S["setup_dve"], count[0])

            setup("t3", dve.memset(t3[:, :, :], 0.0))
            setup("g3", dve.memset(g3[:, :, :], 0.0))
            setup("va_pad", dve.memset(va_pad[:, :], 0.0))
            dve.wait_ge(S["setup_pe"], 1)
            dve.wait_ge(S["query_in"], 16)
            dve.wait_ge(S["setup_in"], 16)
            setup("qneg", dve.tensor_scalar(qneg[:, :], ps[:, 0, 0:B], col("bqin"), 0.0, ALU.add, ALU.min))
            dve.wait_ge(S["setup_act"], 2)
            setup("qb", dve.scalar_tensor_tensor(out=qb[:, :], in0=qneg[:, :], scalar=-1.0, in1=qb[:, :],
                                                 op0=ALU.add, op1=ALU.add))
            dve.wait_ge(S["setup_pe"], 2)
            setup("cmd", dve.tensor_tensor(cmd[:, :, :], ps[:, 1, 0:T * B].rearrange("p (t b) -> p t b", t=T),
                                           w("bqt").unsqueeze(2).to_broadcast([P, T, B]), ALU.add))
            dve.wait_ge(S["setup_pe"], 3)
            setup("kc", dve.tensor_scalar(kc[:, :, :].rearrange("p t b -> p (t b)"), ps[:, 2, 0:T * B], col("bpk"), None,
                                          ALU.add))
            setup("kw", dve.tensor_tensor(wb[:, 0, :].rearrange("p (b t y) -> p b t y", b=B, t=T),
                                          kc[:, :, :].rearrange("p t b -> p b t").unsqueeze(3).to_broadcast([P, B, T, TY]),
                                          w("wes2").unsqueeze(1).unsqueeze(1).to_broadcast([P, B, T, TY]), ALU.mult))
            setup("vc", dve.tensor_scalar(vc[:, :, :].rearrange("p t b -> p (t b)"), ps[:, 3, 0:T * B], col("bpv"), None,
                                          ALU.add))
            dve.wait_ge(S["setup_pe"], 4)
            setup("qry_w", dve.tensor_copy(qry_w[:, :, :], ps[:, 1, P:P + 3 * TY].rearrange("p (k y) -> p k y", k=3)))
            setup("qry_b", dve.tensor_copy(qry_b[:, :], ps[:, 1, P + 3 * TY:P + 4 * TY]))
            for k in range(2):
                x = rh[:, k, :, :, :].rearrange("p b r c -> p (b r) c")
                setup(f"rh{k}", dve.tensor_copy(x[:, :, 0:P], w(("v2", "v3")[k]).unsqueeze(1).to_broadcast([P, 2 * GB, P])))
                setup(f"rhq{k}", dve.tensor_copy(x[:, :, P:P + TY],
                                                 qry_w[:, 1 + k, :].unsqueeze(1).to_broadcast([P, 2 * GB, TY])))
            setup("rx", dve.tensor_copy(rx[:, :, 0:P], w("v1").unsqueeze(1).to_broadcast([P, GB, P])))
            setup("rxq", dve.tensor_copy(rx[:, :, P:P + TY], qry_w[:, 0, :].unsqueeze(1).to_broadcast([P, GB, TY])))
            dve.wait_ge(S["setup_pe"], 6)
            setup("key_w", dve.tensor_copy(key_w[:, 1, :], ps[:, 5, :]))
            dve.wait_ge(S["setup_pe"], 8)
            setup("key_b", dve.tensor_copy(key_b[:, :], ps[:, 7, :]))
            dve.wait_ge(S["weights_in"], 3 * 16)

            state = {}

            def link(kind, n, per, ins):
                state[kind] += 1
                ins.then_inc(S[kind], 1)
                dve.wait_ge(S[kind], n * per + state[kind])

            def cond_point(n, what, t):
                first = isinstance(n, int) and n == 0
                if what == "start":
                    state["cond_dve"] = 0
                    dve.wait_ge(S["mask_in"], 16 * n + 16)
                    dve.tensor_scalar(xc[:, :], mb[:, :], col("init"), None, ALU.mult).then_inc(S["xc_sb"], 1)
                    dve.wait_ge(S["adj_in"], 16 * n + 16)
                    if not first:
                        dve.wait_ge(S["score_ps"], at(n - 1, 2 * T, 2 * T - 1))
                    for y in range(1, TY):
                        link("cond_dve", n, DVE_COND,
                             dve.tensor_scalar(is_ty[:, y - 1, :], ad[:, :], float(y + 1), None, ALU.is_equal))
                    dve.tensor_scalar(pen[:, :], ad[:, :], 0.0, MASKED, ALU.is_le, ALU.mult).then_inc(S["edges_ready"], 1)
                    dve.wait_ge(S["pl_ps"], at(n, 1, 0))
                    dve.tensor_scalar(pl[:, :], ps[:, 2, :], col("bpl"), None, ALU.add).then_inc(S["pl_sb"], 1)
                    dve.wait_ge(S["xl_ps"], at(n, 2, 1))
                    for k in range(2):
                        bs = slice(2 * k, 2 * k + 2)
                        x = ps[:, k, 0:2 * NX].rearrange("p (b c) -> p b c", b=2)
                        link("cond_dve", n, DVE_COND, dve.tensor_tensor(
                            xlac[:, bs, :, TY:2 * TY], x[:, :, P + TY:NX].rearrange("p b (t y) -> p b t y", t=T),
                            key_b[:, bass.ds((n * GB + 2 * k) * T * TY, 2 * T * TY)]
                            .rearrange("p (b t y) -> p b t y", b=2, t=T), ALU.add))
                        i = dve.tensor_tensor(xlac[:, bs, :, 0:TY], x[:, :, P:P + TY].unsqueeze(2).to_broadcast([P, 2, T, TY]),
                                              qry_b[:, :].unsqueeze(1).unsqueeze(1).to_broadcast([P, 2, T, TY]), ALU.add)
                        if k == 0:
                            link("cond_dve", n, DVE_COND, i)
                    i.then_inc(S["xlac_sb"], 1)
                elif what == "pc":
                    dve.wait_ge(S["pc_ps"], at(n, T, t))
                    dve.wait_ge(S["pl_sb"], at(n, 1, 0))
                    dve.scalar_tensor_tensor(out=pr[:, :], in0=ps[:, 2, :], scalar=col("bpc"), in1=pl[:, :],
                                             op0=ALU.add, op1=ALU.mult).then_inc(S["prod_sb"], 1)
                elif what == "vp":
                    dve.wait_ge(S["v_ps"], at(n, T, t))
                    if t == 0:
                        dve.wait_ge(S["xlac_sb"], at(n, 1, 0))
                        dve.wait_ge(S["xlv_sb"], at(n, 1, 0))
                    vs = ps[:, 0:2, 0:2 * NV].rearrange("p k (b c) -> p k b c", b=2)
                    sc = vs[:, :, :, P:NV]
                    xa = xlac[:, :, t, :].rearrange("p (k b) y -> p k b y", k=2)
                    dve.tensor_tensor(ac[:, :, :].rearrange("p (k b) y -> p k b y", k=2), sc, xa, ALU.add)\
                        .then_inc(S["cond_dve"], 1)
                    state["cond_dve"] += 1
                    link("cond_dve", n, DVE_COND, dve.tensor_tensor(
                        t3[:, :, 0:8].rearrange("p (k b) y -> p k b y", k=2), sc, xa, ALU.add))
                    dve.tensor_tensor(ac_r[:, :, :], ac[:, :, :], t3[:, :, 0:8], ALU.subtract).then_inc(S["cond_dve"], 1)
                    state["cond_dve"] += 1
                    link("cond_dve", n, DVE_COND,
                         dve.tensor_tensor(t3[:, :, 8:16], ac[:, :, :], t3[:, :, 0:8], ALU.subtract))
                    dve.tensor_tensor(t3[:, :, 16:24], ac_r[:, :, :], t3[:, :, 8:16], ALU.subtract).then_inc(S["t3_sb"], 1)
                    dve.tensor_tensor(v[:, :, :].rearrange("p (k b) d -> p k b d", k=2), vs[:, :, :, 0:P],
                                      xlv[:, :, :].rearrange("p (k b) d -> p k b d", k=2), ALU.add).then_inc(S["v_sb"], 1)
                elif what in ("z0", "z1"):
                    hf = int(what[1])
                    k = 2 * t + hf
                    bs = slice(2 * hf, 2 * hf + 2)
                    dve.wait_ge(S["base_sb"], at(n, 2 * T, k))
                    if t == 0 and hf == 0:
                        dve.wait_ge(S["edges_ready"], at(n, 1, 0))
                    dve.memset(carrier[:, :], 0.0)
                    dve.drain()
                    for y in range(1, TY):
                        i = dve.copy_predicated(z[:, bs, :],
                                                is_ty[:, y - 1, 2 * hf * P:(2 * hf + 2) * P].rearrange("p (b j) -> p b j", b=2),
                                                ps[:, 0:2, y * P:(y + 1) * P])
                        if y < TY - 1:
                            dve.drain()
                    i.then_inc(S["z_sb"], 1)
                    dve.wait_ge(S["z_sb"], at(n, 2 * T, k))
                    link("cond_dve", n, DVE_COND, dve.scalar_tensor_tensor(
                        out=lk[:, bs, :], in0=z[:, bs, :], scalar=ALPHA, in1=z[:, bs, :], op0=ALU.mult, op1=ALU.max))
                    dve.tensor_reduce(neg_mx[:, bs], lk[:, bs, :], AX_X, ALU.max, negate=True).then_inc(S["max_sb"], 1)
                elif what in ("p0", "p1"):
                    hf = int(what[1])
                    k = 2 * t + hf
                    bs = slice(2 * hf, 2 * hf + 2)
                    dve.wait_ge(S["exp_sb"], at(n, 4 * T, 2 * k + 1))
                    dve.reciprocal(rden[:, bs], den[:, bs]).then_inc(S["rden_sb"], 1)
                    dve.wait_ge(S["rden_sb"], at(n, 2 * T, k))
                    dve.tensor_tensor(pn[:, bs, :], pe_[:, bs, :], rden[:, bs].unsqueeze(2).to_broadcast([P, 2, P]),
                                      ALU.mult).then_inc(S["probs_sb"], 1)
                elif what == "msg":
                    dve.wait_ge(S["msg_ps"], at(n, T, t))
                    dve.scalar_tensor_tensor(out=ms[:, :].rearrange("p (b i) -> p b i", b=GB),
                                             in0=ps[:, 0, :].rearrange("p (b i) -> p b i", b=GB), scalar=col("bv"),
                                             in1=vc[:, t, bass.ds(n * GB, GB)].unsqueeze(2).to_broadcast([P, GB, P]),
                                             op0=ALU.add, op1=ALU.mult).then_inc(S["msg_sb"], 1)
                elif what == "mu":
                    dve.wait_ge(S["mu_ps"], at(n, T, t))
                    if t < T - 1:
                        dve.scalar_tensor_tensor(out=xc[:, :], in0=ps[:, 1, :], scalar=col("bmu"), in1=mb[:, :],
                                                 op0=ALU.add, op1=ALU.mult).then_inc(S["xc_sb"], 1)
                    else:
                        dve.tensor_scalar(xc[:, :], ps[:, 1, :], col("bmu"), None, ALU.add).then_inc(S["xc_sb"], 1)
                    if first and t == 0:
                        dve.wait_ge(S["late_in"], 3 * 16)
                        setup("w2", dve.tensor_scalar(w("w2"), w("w2"), 0.5, None, ALU.mult))
                elif what == "cb":
                    dve.wait_ge(S["cb_ps"], at(n, 1, 0))
                    if not first:
                        dve.wait_ge(S["yn_ps"], at(n - 1, 1, 0))
                        dve.wait_ge(S["yl_sb"], at(n - 1, 1, 0))
                    dve.tensor_tensor(yt[:, :], ps[:, 2, :], cbx[:, :], ALU.add).then_inc(S["yt_sb"], 1)
                    assert state["cond_dve"] == DVE_COND, state["cond_dve"]

            def gates(f):
                def l(ins):
                    link("ffn_dve", f, DVE_FFN, ins)

                def over(x):
                    return x.unsqueeze(2).to_broadcast([P, GB, E])
                dve.wait_ge(S["lge_sb"], at(f, 1, 0))
                l(dve.tensor_reduce(lgs[:, :], lge[:, :, :], AX_X, ALU.add))
                l(dve.reciprocal(lgs[:, :], lgs[:, :]))
                l(dve.tensor_tensor(prb[:, :, :], lge[:, :, :], over(lgs[:, :]), ALU.mult))
                mine = prb[:, :, :].unsqueeze(3).to_broadcast([P, GB, E, E])
                other = prb[:, :, :].unsqueeze(2).to_broadcast([P, GB, E, E])
                l(dve.tensor_tensor(gt[:, :, :, :], other, mine, ALU.is_gt))
                l(dve.tensor_tensor(eq[:, :, :, :], other, mine, ALU.is_equal))
                l(dve.tensor_tensor(eq[:, :, :, :], eq[:, :, :, :],
                                    tri[:, :, :].unsqueeze(1).to_broadcast([P, GB, E, E]), ALU.mult))
                l(dve.tensor_tensor(gt[:, :, :, :], gt[:, :, :, :], eq[:, :, :, :], ALU.add))
                l(dve.tensor_reduce(rank[:, :, :], gt[:, :, :, :], AX_X, ALU.add))
                l(dve.tensor_scalar(rank[:, :, :], rank[:, :, :], 1.5, 0.5, ALU.is_lt, ALU.mult))
                l(dve.tensor_tensor(gate[:, :, :], rank[:, :, :], prb[:, :, :], ALU.mult))
                l(dve.tensor_copy(g3[:, :, 0:E], gate[:, :, :]))
                l(dve.tensor_tensor(gate_r[:, :, :], gate[:, :, :], g3[:, :, 0:E], ALU.subtract))
                l(dve.tensor_copy(g3[:, :, E:2 * E], gate_r[:, :, :]))
                dve.tensor_tensor(g3[:, :, 2 * E:3 * E], gate_r[:, :, :], g3[:, :, E:2 * E], ALU.subtract)\
                    .then_inc(S["g3_sb"], 1)

            def normed(f, k, src, dst):
                dve.wait_ge(S["rstd_sb"], at(f, 3, k))
                for b in range(GB):
                    i = dve.scalar_tensor_tensor(out=dst[:, b * P:(b + 1) * P], in0=src[:, b * P:(b + 1) * P],
                                                 scalar=rstd[:, k, b:b + 1], in1=nrm[:, k, :],
                                                 op0=ALU.mult, op1=ALU.mult)
                    if b < GB - 1:
                        i.then_inc(S["ffn_dve"], 1)
                        state["ffn_dve"] += 1
                return i

            def gated(f, c, k):
                if k == 1:
                    dve.wait_ge(S["th_sb"], at(f, NC, c))
                    dve.scalar_tensor_tensor(out=g1[:, c % 2, :], in0=th[:, c % 2, :], scalar=1.0,
                                             in1=ps[:, tile_bank(("h1", c)), :], op0=ALU.add, op1=ALU.mult)\
                        .then_inc(S["g1_sb"], 1)
                    return
                dve.wait_ge(S["h3_ps"], at(f, NC, c))
                dve.wait_ge(S["g1_sb"], at(f, NC, c))
                if 3 <= c < E + 3:
                    dve.wait_ge(S["gw_sb"], at(f, E, c - 3))
                elif c >= E + 3:
                    dve.wait_ge(S["down_ps"], at(f, NC, c - 3))
                dve.tensor_tensor(g2[:, c % 3, :], g1[:, c % 2, :], ps[:, tile_bank(("h3", c)), :], ALU.mult)\
                    .then_inc(S["g2_sb"], 1)

            def ffn_point(n, what, u):
                f = n - 1
                first = isinstance(n, int) and n == 1
                if what == "vr":
                    state["ffn_dve"] = 0
                    dve.wait_ge(S["vr_ps"], at(f, 1, 0))
                    dve.tensor_copy(lg[:, :, :].rearrange("p (k b) e -> p k b e", k=2),
                                    ps[:, 4:6, 0:2 * NR].rearrange("p k (b c) -> p k b c", b=2)[:, :, :, P:NR])\
                        .then_inc(S["lg_sb"], 1)
                    dve.wait_ge(S["yh_sb"], at(f, 1, 0))
                    dve.tensor_tensor(yl[:, :], yt[:, :], yh[:, :].bitcast(F32), ALU.subtract).then_inc(S["yl_sb"], 1)
                    dve.wait_ge(S["lg_sb"], at(f, 1, 0))
                    link("ffn_dve", f, DVE_FFN, dve.tensor_reduce(lgm[:, :], lg[:, :, :], AX_X, ALU.max))
                    dve.tensor_tensor(lg[:, :, :], lg[:, :, :], lgm[:, :].unsqueeze(2).to_broadcast([P, GB, E]),
                                      ALU.subtract).then_inc(S["lgneg_sb"], 1)
                elif what == "q":
                    dve.wait_ge(S["qk_hi"], at(f, 2, 0))
                    dve.scalar_tensor_tensor(out=qk_l[:, 0, :], in0=ps[:, 7, :], scalar=HD ** -0.5,
                                             in1=qk_h[:, 0, :].bitcast(F32), op0=ALU.mult, op1=ALU.subtract)\
                        .then_inc(S["qk_lo"], 1)
                elif what == "k":
                    dve.wait_ge(S["qk_hi"], at(f, 2, 1))
                    dve.tensor_tensor(qk_l[:, 1, :], ps[:, 6, :], qk_h[:, 1, :].bitcast(F32), ALU.subtract)\
                        .then_inc(S["qk_lo"], 1)
                elif what == "choose":
                    gates(f)
                elif what == "arrange":
                    dve.wait_ge(S["arr_ps"], at(f, 8, 2 * u + 1))
                    dve.tensor_copy(qk[:, u, 1, :], ps[:, 5 if u % 2 == 0 else 6, :]).then_inc(S["arrk_sb"], 1)
                elif what == "exps":
                    dve.wait_ge(S["s_ps"], at(f, 16, u))
                    if u >= 2:
                        dve.wait_ge(S["pa_sb"], at(f, 64, 4 * (u - 2) + 3))
                    dve.tensor_reduce(nmx[:, u % 2, :], ps[:, 4 + u % 2, :].rearrange("p (g j) -> p g j", g=4),
                                      AX_X, ALU.max, negate=True).then_inc(S["nmx_sb"], 1)
                elif what == "turn":
                    if u % 4 == 3:
                        b = u // 4
                        dve.wait_ge(S["pa_sb"], at(f, 64, 16 * b + 15))
                        dve.reciprocal(inv[:, b, :, :], sums[:, b, :].unsqueeze(2).to_broadcast([P, H, HD]))\
                            .then_inc(S["inv_sb"], 1)
                elif what == "mix":
                    dve.wait_ge(S["o_ps"], at(f, 16, 15))
                    dve.wait_ge(S["invT_sb"], at(f, 1, 0))
                    dve.tensor_tensor(onT[:, :], ps[:, 7, :], onT[:, :], ALU.mult).then_inc(S["onT_sb"], 1)
                elif what == "norm_h":
                    i = normed(f, 0, ps[:, tile_bank("wo"), :], nh)
                    link("ffn_dve", f, DVE_FFN, i)
                    dve.wait_ge(S["yn_sb"], at(f, 1, 0))
                    if not first:
                        dve.wait_ge(S["out_stored"], 16 * (n - 1))
                    dve.tensor_tensor(hh[:, :], nh[:, :], yn[:, :, :].rearrange("p b d -> p (b d)"), ALU.add)\
                        .then_inc(S["hh_sb"], 1)
                elif what == "turn_h":
                    dve.wait_ge(S["hth_sb"], at(f, 1, 0))
                    dve.tensor_tensor(htl[:, :], ps[:, tile_bank("ht"), :], hth[:, :].bitcast(F32), ALU.subtract)\
                        .then_inc(S["htl_sb"], 1)
                elif what in ("g1", "g2"):
                    gated(f, u, int(what[1]))
                elif what == "norm_m":
                    normed(f, 1, ps[:, 7, :], mo).then_inc(S["mo_sb"], 1)
                elif what == "last":
                    i = normed(f, 2, ps[:, 7, :], nh)
                    link("ffn_dve", f, DVE_FFN, i)
                    dve.wait_ge(S["res_sb"], at(f, 1, 0))
                    dve.tensor_tensor(fo[:, :], nh[:, :], res[:, :], ALU.add).then_inc(S["fo_sb"], 1)
                    assert state["ffn_dve"] == DVE_FFN, state["ffn_dve"]

            iterations(dve, lambda n, cond, ffn, more: [
                (cond_point if k == "c" else ffn_point)(n, what, t) for k, what, t in points(cond, ffn)])

        @block.scalar
        def _(act):
            act.wait_ge(S["setup_dve"], step("qneg"))
            act.activation(qneg[:, :], qneg[:, :], ACT.Exp).then_inc(S["setup_act"], 1)
            act.wait_ge(S["setup_pe"], 1)
            act.activation(qb[:, :], ps[:, 0, 0:B], ACT.Relu, bias=col("bqin")).then_inc(S["setup_act"], 1)
            for k in (0, 2):
                act.wait_ge(S["setup_pe"], 5 + k)
                act.activation(key_w[:, k, :], ps[:, 4 + k, :], ACT.Copy).then_inc(S["setup_act"], 1)

            def cond_point(n, what, t):
                first = isinstance(n, int) and n == 0
                if what == "start":
                    act.wait_ge(S["cbx_ps"], at(n, 1, 0))
                    if not first:
                        act.wait_ge(S["yt_sb"], at(n - 1, 1, 0))
                    act.activation(cbx[:, :], ps[:, 3, :], ACT.Identity, bias=col("bcb")).then_inc(S["cbx_sb"], 1)
                    act.wait_ge(S["xlac_sb"], at(n, 1, 0))
                    act.activation(xlv[:, :, :].rearrange("p (k b) d -> p k b d", k=2),
                                   ps[:, 0:2, 0:2 * NX].rearrange("p k (b c) -> p k b c", b=2)[:, :, :, 0:P],
                                   ACT.Copy).then_inc(S["xlv_sb"], 1)
                elif what == "tt":
                    act.wait_ge(S["turned_ac"], at(n, T, t))
                    act.activation(tt[:, :], ps[:, 3, 0:P // 2].bitcast(BF16), ACT.Copy).then_inc(S["tt_sb"], 1)
                elif what in ("s0", "s1"):
                    hf = int(what[1])
                    k = 2 * t + hf
                    act.wait_ge(S["score_ps"], at(n, 2 * T, k))
                    act.activation(z[:, 2 * hf:2 * hf + 2, :], ps[:, 0:2, 0:P], ACT.Copy).then_inc(S["base_sb"], 1)
                elif what in ("z0", "z1"):
                    hf = int(what[1])
                    k = 2 * t + hf
                    act.wait_ge(S["max_sb"], at(n, 2 * T, k))
                    for b in (2 * hf, 2 * hf + 1):
                        act.activation(pe_[:, b, :], lk[:, b, :], ACT.Exp, bias=neg_mx[:, b:b + 1],
                                       accum_out=den[:, b:b + 1]).then_inc(S["exp_sb"], 1)
                elif what in ("pt0", "pt1"):
                    hf = int(what[2])
                    k = 2 * t + hf
                    act.wait_ge(S["turned_p"], at(n, 2 * T, k))
                    act.activation(pt[:, 2 * hf:2 * hf + 2, :].rearrange("p b i -> p (b i)"), ps[:, 3 - hf, 0:2 * P],
                                   ACT.Copy).then_inc(S["pt_sb"], 1)

                elif what == "mu" and first and t < 3:
                    act.wait_ge(S["splits_in"], 48)
                    if t < 2:
                        sl = slice(t * NS // 2, (t + 1) * NS // 2)
                        i = act.activation(hi_w[:, sl], wb_flat[:, W:W + NS][:, sl], ACT.Copy)
                    else:
                        act.activation(arr[:, 0:8 * P], arr_in[0], ACT.Copy)
                        i = act.activation(arr[:, 8 * P:], arr_in[1], ACT.Copy)
                    i.then_inc(S["split_hi"], 1)

            def squares(f, k, src):
                for b in range(GB):
                    act.activation(sq[:, :], src[:, b * P:(b + 1) * P], ACT.Square, scale=P ** -0.5,
                                   accum_out=ss[:, k, b:b + 1]).then_inc(S["ss_sb"], 1)
                    act.wait_ge(S["ss_sb"], at(f, 3 * GB, k * GB + b))

            def ffn_point(n, what, u):
                f = n - 1
                first = isinstance(n, int) and n == 1
                if what == "vr":
                    act.wait_ge(S["yt_sb"], at(f, 1, 0))
                    act.activation(yh[:, :], yt[:, :], ACT.Copy).then_inc(S["yh_sb"], 1)
                    act.wait_ge(S["lg_sb"], at(f, 1, 0))
                    for k in range(2):
                        act.activation(va[:, 2 * k:2 * k + 2, :, 0:HD],
                                       ps[:, 4 + k, 0:2 * NR].rearrange("p (b c) -> p b c", b=2)[:, :, 0:P]
                                       .rearrange("p b (h d) -> p b h d", h=H), ACT.Copy).then_inc(S["va_sb"], 1)
                elif what == "turn_y":
                    act.wait_ge(S["yn_ps"], at(f, 1, 0))
                    act.activation(yn[:, :, :].rearrange("p b d -> p (b d)"), ps[:, 6, :], ACT.Copy).then_inc(S["yn_sb"], 1)
                elif what in ("q", "k"):
                    s = ("q", "k").index(what)
                    act.wait_ge(S["qk_ps"], at(f, 2, s))
                    act.activation(qk_h[:, s, :], ps[:, (7, 6)[s], :], ACT.Copy,
                                   scale=(HD ** -0.5, 1.0)[s]).then_inc(S["qk_hi"], 1)
                elif what == "choose":
                    act.wait_ge(S["lgneg_sb"], at(f, 1, 0))
                    act.activation(lge[:, :, :], lg[:, :, :], ACT.Exp).then_inc(S["lge_sb"], 1)
                elif what == "arrange":
                    act.wait_ge(S["arr_ps"], at(f, 8, 2 * u))
                    act.activation(qk[:, u, 0, :], ps[:, 4 if u % 2 == 0 else 7, :], ACT.Copy).then_inc(S["arrq_sb"], 1)
                elif what == "gates":
                    act.wait_ge(S["gT_ps"], at(f, 1, 0))
                    act.activation(gT[:, :], ps[0:32, 7, 0:W // 2].bitcast(BF16), ACT.Copy).then_inc(S["gT_sb"], 1)
                elif what == "spread":
                    act.wait_ge(S["spread_ps"], at(f, E, u))
                    act.activation(wb[:, u, :], ps[:, 4 + u % 2, :], ACT.Copy).then_inc(S["wb_sb"], 1)
                elif what == "exps":
                    act.wait_ge(S["nmx_sb"], at(f, 16, u))
                    if u >= 2:
                        act.wait_ge(S["turned_pa"], at(f, 16, u - 2))
                    if u == 0 and not first:
                        act.wait_ge(S["inv_sb"], at(f - 1, GB, GB - 1))
                    for g in range(4):
                        h = 4 * g + u % 4
                        act.activation(pa[:, u % 2, g, :], ps[:, 4 + u % 2, g * P:(g + 1) * P], ACT.Exp,
                                       bias=nmx[:, u % 2, g:g + 1], accum_out=sums[:, u // 4, h:h + 1])\
                            .then_inc(S["pa_sb"], 1)
                elif what == "turn":
                    act.wait_ge(S["turned_pa"], at(f, 16, u))
                    if u >= 2:
                        act.wait_ge(S["o_ps"], at(f, 16, u - 2))
                    act.activation(pat[:, u % 2, :, :].rearrange("p g i -> p (g i)"), ps[:, 6, :], ACT.Copy)\
                        .then_inc(S["pat_sb"], 1)
                elif what == "mix":
                    act.wait_ge(S["invT_ps"], at(f, 1, 0))
                    act.activation(onT[:, :], ps[:, tile_bank("invT"), :], ACT.Copy).then_inc(S["invT_sb"], 1)
                elif what == "out_proj":
                    act.wait_ge(S["wo_ps"], at(f, 1, 0))
                    squares(f, 0, ps[:, tile_bank("wo"), :])
                elif what == "turn_h":
                    act.wait_ge(S["ht_ps"], at(f, 1, 0))
                    act.activation(hth[:, :], ps[:, tile_bank("ht"), :], ACT.Copy).then_inc(S["hth_sb"], 1)
                elif what == "g1":
                    act.wait_ge(S["h1_ps"], at(f, NC, u))
                    if u >= 2:
                        act.wait_ge(S["g1_sb"], at(f, NC, u - 2))
                    act.activation(th[:, u % 2, :], ps[:, tile_bank(("h1", u)), :], ACT.Tanh, scale=0.5)\
                        .then_inc(S["th_sb"], 1)
                elif what == "norm_m":
                    act.wait_ge(S["down_ps"], at(f, NC, E - 1))
                    squares(f, 1, ps[:, 7, :])
                elif what == "last":
                    act.wait_ge(S["down_ps"], at(f, NC, NC - 1))
                    squares(f, 2, ps[:, 7, :])

            iterations(act, lambda n, cond, ffn, more: [
                (cond_point if k == "c" else ffn_point)(n, what, t) for k, what, t in points(cond, ffn)])

        @block.gpsimd
        def _(pool):
            kw5 = key_w[:, :, :].rearrange("p k (b t y) -> p k b t y", b=B, t=T)

            def keys(n, t):
                for k in range(2):
                    i = pool.tensor_copy(rh[:, k, :, t % 2, P + TY:NV], kw5[:, 1 + k, bass.ds(n * GB, GB), t, :])
                return i

            def keys_x(n):
                x = key_w[:, 0, bass.ds(n * GB * T * TY, GB * T * TY)].rearrange("p (b c) -> p b c", b=GB)
                return pool.tensor_copy(rx[:, :, P + TY:NX], x)

            pool.memset(half_pow[:, :], -0.5)
            pool.memset(eps[:, :], EPS)
            pool.memset(ones[:, :], 1.0)
            pool.wait_ge(S["setup_in"], 16)
            pool.tensor_copy(bias_q, w("bq").to_broadcast([P, P]))
            pool.tensor_copy(bias_k, w("bk").to_broadcast([P, P])).then_inc(S["setup_pool"], 1)
            pool.wait_ge(S["setup_dve"], step("key_w"))
            pool.wait_ge(S["setup_act"], 4)
            keys_x(0)
            for t in range(2):
                i = keys(0, t)
            i.then_inc(S["setup_pool"], 1)
            pool.wait_ge(S["setup_pool"], 2)

            def cond_point(n, what, t, more):
                if what == "pc" and t == 0 and more:
                    pool.wait_ge(S["xl_ps"], at(n, 2, 1))
                    keys_x(n + 1).then_inc(S["rx_next"], 1)
                if what == "tt" and (more or t < 2):
                    pool.wait_ge(S["v_ps"], at(n, T, t))
                    keys(n + (t + 2) // T, (t + 2) % T).then_inc(S["rh_next"], 1)

                if what == "mu" and more and isinstance(n, int) and n == 0 and t < 2:
                    pool.wait_ge(S["split_hi"], t + 1)
                    sl = slice(t * NS // 2, (t + 1) * NS // 2)
                    pool.tensor_tensor(lo_w[:, sl], wb_flat[:, W:W + NS][:, sl], hi_w[:, sl].bitcast(F32), ALU.subtract)\
                        .then_inc(S["split_lo"], 1)

            def rstd_of(f, k):
                pool.wait_ge(S["ss_sb"], at(f, 3 * GB, k * GB + GB - 1))
                pool.tensor_tensor(rs[:, k, :], ss[:, k, :], eps[:, :], ALU.add).then_inc(S["ffn_pool"], 1)
                pool.wait_ge(S["ffn_pool"], at(f, 4, (0, 1, 3)[k]))
                pool.tensor_tensor(rstd[:, k, :], rs[:, k, :], half_pow[:, :], ALU.pow).then_inc(S["rstd_sb"], 1)

            def weighted(f, e):
                pool.wait_ge(S["g2_sb"], at(f, NC, e))
                if e == 0:
                    pool.wait_ge(S["wb_sb"], at(f, E, E - 1))
                if e >= 2:
                    pool.wait_ge(S["down_ps"], at(f, NC, e - 2))
                pool.tensor_tensor(gw[:, e % 2, :], g2[:, e % 3, :], wb[:, e, :], ALU.mult).then_inc(S["gw_sb"], 1)

            def pad(f, q):
                b, r = divmod(q, 4)
                x = va[:, b, :, :].rearrange("p (g r) d -> p g r d", g=4)[:, :, r, :]
                pool.tensor_tensor(va_pad[:, :].rearrange("p (g r c) -> p g r c", g=4, r=4)[:, :, r, 0:HD], x,
                                   ones[:, :].unsqueeze(2).to_broadcast([P, 4, HD]), ALU.mult)\
                    .then_inc(S["va_pad_sb"], 1)

            def ffn_point(n, what, u):
                f = n - 1
                first = isinstance(n, int) and n == 1
                if what == "arrange":
                    pool.wait_ge(S["va_sb"], at(f, 2, 1))
                    if not first:
                        pool.wait_ge(S["o_ps"], at(f - 1, 16, 12 + u))
                    pad(f, u)
                elif what == "values" and u < 12:
                    pool.wait_ge(S["o_ps"], at(f, 16, u))
                    pad(f, u + 4)
                if what == "out_proj":
                    rstd_of(f, 0)
                elif what == "g2":
                    if u < E:
                        weighted(f, u)
                elif what == "norm_m":
                    rstd_of(f, 1)
                elif what == "last":
                    rstd_of(f, 2)
                if what == "norm_m":
                    pool.wait_ge(S["mo_sb"], at(f, 1, 0))
                    pool.wait_ge(S["hh_sb"], at(f, 1, 0))
                    pool.wait_ge(S["ffn_dve"], f * DVE_FFN + DVE_FFN - 4)
                    pool.tensor_tensor(res[:, :], hh[:, :], mo[:, :], ALU.add).then_inc(S["ffn_pool"], 1)
                    pool.wait_ge(S["xn_in"], 16 * n)
                    pool.wait_ge(S["ffn_pool"], at(f, 4, 2))
                    pool.tensor_tensor(res[:, :], res[:, :], xn[:, :, :].rearrange("p b d -> p (b d)"), ALU.add)\
                        .then_inc(S["res_sb"], 1)

            def iteration(n, cond, ffn, more):
                for k, what, t in points(cond, ffn):
                    if k == "f":
                        ffn_point(n, what, t)
                    else:
                        cond_point(n, what, t, more)

            iterations(pool, iteration)


def iterations(eng, body):
    body(0, True, False, True)
    body(1, True, True, True)
    with eng.Fori(2, NG - 1) as n:
        body(n, True, True, True)
    body(NG - 1, True, True, False)
    body(NG, False, True, False)


def _constants():
    import numpy as np
    bf = np.zeros((P, P + 512 + 16 * P + 4 * 512 + E * P), np.float32)
    bf[:, 0:P] = np.eye(P)
    ahead = np.triu(np.ones((P, P), np.float32), 1) * -1e30
    bf[:, P:P + 512] = np.tile(ahead, (1, 4))
    o = P + 512
    key = np.zeros((P, GB, TY, P), np.float32)
    qry = np.zeros((P, GB, TY, P), np.float32)
    for b in range(GB):
        for y in range(TY):
            for part in range(3):
                key[32 * b + 8 * part + TY + y, b, y, :] = 1
                qry[32 * b + 8 * part + y, b, y, :] = 1
    bf[:, o:o + 16 * P] = key.reshape(P, -1)
    o += 16 * P
    bf[:, o:o + 4 * 512] = qry.reshape(P, -1)
    o += 4 * 512
    for e in range(E):
        for part in range(3):
            bf[E * part + e, o + e * P:o + (e + 1) * P] = 1
    arr = np.zeros((P, 4, 4, P), np.float32)
    high = {0: (0, 1), 2: (0, 2)}
    for s in (0, 2):
        for g in range(4):
            for r in range(4):
                for copy in range(4):
                    which = s if copy in high[s] else s + 1
                    for d in range(HD):
                        arr[(4 * g + r) * HD + d, which, g, 32 * r + copy * HD + d] = 1
    tri = np.zeros((P, E, E), np.float32)
    tri[:, :, :] = np.tril(np.ones((E, E)), -1)
    f = np.concatenate([np.eye(P, dtype=np.float32), tri.reshape(P, -1), arr.reshape(P, -1)], 1)
    return bf, f.astype(np.float32)


def kernel(**inputs):
    import numpy as np
    import ml_dtypes
    import concourse.bacc as _bacc
    from concourse.bass_utils import run_bass_kernel_spmd as _run

    a = {k: np.asarray(v) for k, v in inputs.items()}
    c = lambda k: a["L0_cond_" + k]
    f = lambda k: a["L0_ffn_" + k]
    column = lambda v: v.reshape(P, 1)
    wT = {}
    wT["pl"], wT["pc"] = c("w_pl").T, c("w_pc").T
    wT["mu1"], wT["mu2"] = c("w_mu").T[:P], c("w_mu").T[P:]
    wT["cb1"], wT["cb2"] = c("w_cb").T[:P], c("w_cb").T[P:]
    for k in range(3):
        wT[f"v{k + 1}"] = c("w_v").T[k * P:(k + 1) * P]
    wT["wq"], wT["wk"] = c("w_q"), c("w_k")
    wT["qin"], wT["pk"], wT["pv"] = c("w_qin").T, c("w_pk").T, c("w_pv").T
    wT["qt"] = np.concatenate([a["fside_BxSxS_0"][t].T for t in range(T)], 1)
    wT["bqt"] = a["mask_BxS_ff0"][:T].T
    wT["wes1"], wT["wes2"] = a["cond_2048"][:TY, :P].T, a["cond_2048"][:TY, P:].T
    wT["qenc"] = a["fside_BxS_0"].T
    wT["init"] = column(c("init_mem"))
    for k in ("qin", "pl", "pc", "q", "k", "v", "pk", "pv", "mu", "cb"):
        wT["b" + k] = column(c("b_" + k))
    wT["wo"] = f("wo")
    wT["vr"] = np.concatenate([f("wv"), f("router_w")], 1)
    wT["w2"] = np.concatenate([f("w2")[k * P:(k + 1) * P] for k in range(FC)], 1)
    wT["ew2"] = np.concatenate([f("ew2")[e] for e in range(E)], 1)
    for k, (lo, hi) in list(COLS.items()) + list(SETUP_COLS.items()):
        assert wT[k].shape == (P, hi - lo), (k, wT[k].shape)
    sp = [f("wq"), f("wk")]
    for e in range(E):
        sp += [f("ew1")[e], f("ew3")[e]]
    for k in range(FC):
        sp += [f("w1")[:, k * P:(k + 1) * P], f("w3")[:, k * P:(k + 1) * P]]
    splits = np.concatenate(sp, 1)
    bf, cf = _constants()
    arrays = {
        "xT": a["x"].transpose(2, 0, 1).reshape(P, B * P),
        "xN": a["x"].transpose(1, 0, 2),
        "adj": a["itok_BxSxS_0_4"].astype(np.int32).transpose(1, 0, 2),
        "msk": a["mask_BxS_ff1"].reshape(1, B * P),
        "setup_w": np.concatenate([wT[k] for k in SETUP_COLS], 1), "wts": np.concatenate([wT[k] for k in COLS], 1), "splits": splits,
        "norms": np.stack([f("attn_norm_w"), f("moe_norm_w"), f("ff_norm_w")]),
        "cst_bf": bf.astype(ml_dtypes.bfloat16), "cst_f": cf,
    }
    arrays = {k + "_dram": np.ascontiguousarray(v) for k, v in arrays.items()}
    nc = _bacc.Bacc("TRN2", target_bir_lowering=False, num_devices=1)
    args = [nc.dram_tensor(k, v.shape, mybir.dt.from_np(v.dtype), kind="ExternalInput").ap() for k, v in arrays.items()]
    out = nc.dram_tensor("out_dram", (P, B, P), F32, kind="ExternalOutput").ap()
    build(nc, *args, out)
    r = _run(nc, [arrays], core_ids=[0])
    return np.ascontiguousarray(r.results[0]["out_dram"].transpose(1, 0, 2))
```

```python
from contextlib import ExitStack

import concourse.bass as bass
from concourse import mybir

F32 = mybir.dt.float32
F32R = mybir.dt.float32r
BF16 = mybir.dt.bfloat16
U8 = mybir.dt.uint8
I32 = mybir.dt.int32
ALU = mybir.AluOpType
ACT = mybir.ActivationFunctionType
AX_X = mybir.AxisListType.X

P = 128
B = 32
GB = 4
NG = B // GB
W = GB * P
T = 4
TY = 4
H = 16
HD = P // H
E = 8
FC = 4
NC = E + FC
EPS = 1e-5
ALPHA = 0.2
MASKED = -9e15 / ALPHA
NV = P + 2 * TY
NX = P + TY + T * TY
NR = P + E

def _cols(cols, widths):
    at = 0
    for name, width in widths:
        cols[name] = (at, at + width)
        at += width
    return at


SETUP_COLS, COLS = {}, {}
NSET = _cols(SETUP_COLS, (
    ("qin", P), ("bqin", 1), ("qenc", B), ("qt", T * P), ("bqt", T), ("pk", P), ("pv", P), ("bpk", 1), ("bpv", 1),
    ("wes1", TY), ("wes2", TY), ("bq", 1), ("bk", 1), ("wq", 3 * P), ("wk", 3 * P), ("v1", P), ("v2", P), ("v3", P)))
NW = _cols(COLS, (
    ("pl", P), ("pc", P), ("mu1", P), ("mu2", P), ("cb1", P), ("cb2", P), ("init", 1), ("bpl", 1), ("bpc", 1),
    ("bmu", 1), ("bcb", 1), ("bv", 1), ("wo", P), ("vr", NR), ("w2", FC * P), ("ew2", E * P)))
NS = 2 * P + 2 * NC * P


ORDER = """
        | lg.0 vr.0
xl.0    | va.0
start.0 | turn_y.0
edges.0 | q.0
pc.0    |
pr.0    | pad.0 q_sb.0 k_sb.0 arr.0 k.0
sc.0    | arrange.0
vp.0    |
vv.0    | pad.1 arrange.1 arr.1
tt.0    | arr.2 arr.3 arrange.2
z0.0    |
s0.0    | arrange.3
s1.0    | pad.2 scores.0 scores.1 max.0
z1.0    | max.1 exps.0
e0.0    |
e1.0    |
n0.0    | turn.0
n1.0    | exps.1 pat.0 scores.2
p0.0    |
p1.0    | exps.2 max.2 scores.3 max.3 choose.0
pt0.0   | turn.1 pad.3 exps.3 values.0
ms.0    |
pt1.0   | pat.1 pat.2 scores.4 pad_next.0 turn.2 values.1 max.4
msg.0   | turn.3 values.2
xc.0    | exps.4
mu.0    | scores.5 scores.6 pat.3 max.5 exps.5 pat.4
pc.1    | pad_next.1 max.6 pad_next.2
pr.1    | turn.4
vp.1    | exps.6 values.3
sc.1    | turn.5
vv.1    | pat.5 scores.7 inv.0
tt.1    | scores.8 turn.6
s0.1    | pad_next.3 exps.7 values.4 values.5 pat.6 pad_next.4 exps.8 max.7 max.8 scores.9
e0.1    |
z0.1    | turn.7 pad_next.5 pad_next.6
s1.1    | pad_next.7 inv.1 max.9 max.10 pat.7 scores.10 exps.9 pat.8 values.6 turn.8 exps.10
n0.1    |
p0.1    |
z1.1    |
e1.1    | pad_next.8 pat.9 exps.11 values.7
n1.1    | max.11
pt0.1   | scores.11 turn.9
p1.1    | values.8 pad_next.9 max.12
pt1.1   | turn.10 scores.12 scores.13 values.9 pat.10 exps.12
msg.1   | pat.11
ms.1    |
mu.1    | turn.11
xc.1    | exps.13 values.10 inv.2 max.13
pc.2    | pat.12 turn.12 pad_next.10 exps.14 pad_next.11
pr.2    | scores.14 scores.15 max.14 max.15 pat.13 values.11 turn.13
vp.2    | values.12 exps.15
sc.2    | turn.14
tt.2    | pat.14 pat.15 values.13 values.14 inv.3 turn.15 gates.0
vv.2    | onT.0 mix.0 values.15
s0.2    |
s1.2    | sq_a.0
z0.2    | h3.0 out_proj.0 spread.0 h1.0 gw.0 h1.1 h3.1
z1.2    | th.0
e0.2    | spread.1 g1.0 gate.0
n0.2    | h1.2 g2.0 norm_h.0
p0.2    | g1.1 th.1 th.2 gw.1 gate.1 g2.1
e1.2    | g1.2 g2.2 h3.2 down.0 spread.2
n1.2    | gate.2 g1.3 h1.3 th.3 gw.2
p1.2    | g2.3 h3.3
pt0.2   | gate.3 spread.3 down.1
pt1.2   | turn_h.0 h_parts.0 h1.4 th.4
ms.2    | g1.4
msg.2   |
xc.2    | spread.4 gw.3
mu.2    | gw.4 gate.4 g2.4 h3.4 down.2 h1.5 th.5 g1.5 h3.5
pc.3    | spread.5 gate.5
pr.3    | g2.5 gw.5
vp.3    |
sc.3    | down.3
vv.3    |
tt.3    | g1.6 th.6 spread.6 gw.6 h1.6 h3.6
s0.3    | gate.6 th.7 down.4 g2.6
z0.3    | h1.7 h3.7 down.5 gw.7 spread.7
e0.3    | gate.7 g1.7
s1.3    | th.8 g2.7
n0.3    |
z1.3    | h1.8 g1.8 h3.8
p0.3    | down.6 g2.8
n1.3    | th.9
e1.3    | h1.9 down.7 sq_m.0 g1.9 norm_m.0 g2.9 h3.9
p1.3    | h1.10
pt0.3   | g1.10
msg.3   |
ms.3    |
pt1.3   | res.0 th.10 th.11 h3.10 down.8 g2.10 h1.11 g1.11
mu.3    | down.9 h3.11 sq_f.0
xc.3    | down.10 g2.11 down.11
yt.0    |
cb.0    | last.0
"""


def points(cond, ffn):
    out = []
    for line in ORDER.strip("\n").splitlines():
        c, f = line.split("|")
        for stage, name in [("c", x) for x in c.split()] + [("f", x) for x in f.split()]:
            if cond if stage == "c" else ffn:
                what, index = name.split(".")
                out.append((stage, what, int(index)))
    return out


TILES = (["invT", "gT"] + [(h, c) for c in range(4) for h in ("h1", "h3", "gate")] + ["ht"]
         + [(h, c) for c in range(4, E) for h in ("h1", "h3", "gate")]
         + [(h, c) for c in range(E, NC) for h in ("h1", "h3")])



def tile_bank(tile):
    return 4 + TILES.index(tile) % 3


def build(nc, xT, xN, adj, msk, setup_w, wts, splits, norms, cst_bf, cst_f, out):
    with ExitStack() as ctx:
        def sb(name, shape, dt=F32):
            return ctx.enter_context(nc.sbuf_tensor(name, shape, dt))

        def sem(name):
            return ctx.enter_context(nc.semaphore(name))

        ps = ctx.enter_context(nc.psum_tensor("ps", [P, 8, 512], F32))

        wt = sb("wt", [P, NW])
        hi_w = sb("hi_w", [P, NS], F32R)
        lo_w = sb("lo_w", [P, NS], F32R)
        cb = sb("cb", [P, cst_bf.shape[1]], BF16)
        ident = sb("ident", [P, P])
        arr = sb("arr", [P, 4 * 4 * P], F32R)
        tri = sb("tri", [P, E, E])
        nrm = sb("nrm", [P, 3, P])
        half_pow = sb("half_pow", [P, GB])
        eps = sb("eps", [P, GB])
        ones = sb("ones", [P, 4])
        key_w = sb("key_w", [P, 3, B * T * TY])
        key_b = sb("key_b", [P, B * T * TY])
        qry_w = sb("qry_w", [P, 3, TY])
        qry_b = sb("qry_b", [P, TY])
        vc = sb("vc", [P, T, B])
        kc = sb("kc", [P, T, B])
        rh = sb("rh", [P, 2, GB, 2, NV])
        rx = sb("rx", [P, GB, NX])
        qb = sb("qb", [P, B])
        qneg = sb("qneg", [P, B])
        cmd = sb("cmd", [P, T, B])

        xt = sb("xt", [P, W])
        ad = sb("ad", [P, W], I32)
        mb = sb("mb", [P, W])
        is_ty = sb("is_ty", [P, TY - 1, W], U8)
        pen = sb("pen", [P, W], BF16)
        pl = sb("pl", [P, W])
        cbx = sb("cbx", [P, W])
        xlv = sb("xlv", [P, GB, P])
        xlac = sb("xlac", [P, GB, T, 2 * TY])
        xc = sb("xc", [P, W])
        pr = sb("pr", [P, W])
        ac = sb("ac", [P, GB, 2 * TY])
        ac_r = sb("ac_r", [P, GB, 2 * TY])
        t3 = sb("t3", [P, GB, 32], BF16)
        tt = sb("tt", [P, P], BF16)
        z = sb("z", [P, GB, P])
        lk = sb("lk", [P, GB, P])
        neg_mx = sb("neg_mx", [P, GB])
        den = sb("den", [P, GB])
        carrier = sb("carrier", [1, 1])
        rden = sb("rden", [P, GB])
        pe_ = sb("pexp", [P, GB, P])
        pn = sb("pn", [P, GB, P])
        pt = sb("pt", [P, GB, P])
        v = sb("v", [P, GB, P])
        ms = sb("ms", [P, W])
        yt = sb("yt", [P, W])

        xn = sb("xn", [P, GB, P])
        yh = sb("yh", [P, W], F32R)
        yl = sb("yl", [P, W], F32R)
        yn = sb("yn", [P, GB, P])
        qk_h = sb("qk_h", [P, 2, W], F32R)
        qk_l = sb("qk_l", [P, 2, W], F32R)
        qk = sb("qk", [P, 4, 2, W], F32R)
        va = sb("va", [P, GB, H, HD])
        va_pad = sb("va_pad", [P, H * (P + HD)])
        lg = sb("lg", [P, GB, E])
        lgm = sb("lgm", [P, GB])
        lge = sb("lge", [P, GB, E])
        lgs = sb("lgs", [P, GB])
        prb = sb("prb", [P, GB, E])
        gt = sb("gt", [P, GB, E, E])
        eq = sb("eq", [P, GB, E, E])
        rank = sb("rank", [P, GB, E])
        gate = sb("gate", [P, GB, E])
        gate_r = sb("gate_r", [P, GB, E])
        g3 = sb("g3", [P, GB, 32], BF16)
        gT = sb("gT", [32, W], BF16)
        gate_w = sb("gate_w", [P, E, W])
        stage = gate_w[:, :, :].rearrange("p e w -> p (e w)")
        nmx = sb("nmx", [P, 2, 4])
        pa = sb("pa", [P, 2, 4, P])
        pat = sb("pat", [P, 2, 4, P])
        sums = sb("sums", [P, GB, H])
        inv = sb("inv", [P, GB, H, HD])
        onT = sb("onT", [P, W])
        sq = sb("sq", [P, P])
        ss = sb("ss", [P, 3, GB])
        rs = sb("rs", [P, 3, GB])
        rstd = sb("rstd", [P, 3, GB])
        nh = onT
        hh = sb("hh", [P, W])
        hth = qk_h[:, 0, :]
        htl = qk_h[:, 1, :]
        th = pa[:, :, :, :].rearrange("p k g i -> p k (g i)")
        g1 = pat[:, :, :, :].rearrange("p k g i -> p k (g i)")
        gg = sb("gg", [P, 5, W])
        g2, gw = gg[:, 0:3, :], gg[:, 3:5, :]
        ws = gg[:, :, :].rearrange("p k w -> p (k w)")[:, 0:NSET]
        mo = sb("mo", [P, W])
        res, fo = mo, hh

        arr_in = [x[:, :, :, :].rearrange("p k g i -> p (k g i)") for x in (pa, pat)]

        def w(name):
            if name in SETUP_COLS:
                a, b = SETUP_COLS[name]
                return ws[:, a:b]
            a, b = COLS[name]
            return wt[:, a:b]

        def col(name):
            return w(name)[:, 0:1]

        def part(name, k):
            return w(name)[:, k * P:(k + 1) * P]

        idb = cb[:, 0:P]
        causal = cb[:, P:P + 512]
        o = P + 512
        sel_key = cb[:, o:o + 16 * P].rearrange("k (b y j) -> k b y j", b=GB, y=TY)
        o += 16 * P
        sel_qry = cb[:, o:o + 4 * 512].rearrange("k (b j) -> k b j", b=GB)
        o += 4 * 512
        sel_exp = cb[0:32, o:o + E * P].rearrange("k (e j) -> k e j", e=E)
        arr4 = arr[:, :].rearrange("k (s g j) -> k s g j", s=4, g=4)

        S = {}
        for name in (
            "query_in", "setup_in", "weights_in", "splits_in", "late_in", "xt_in", "adj_in", "mask_in", "xn_in", "out_stored",
            "setup_pe", "setup_dve", "setup_act", "setup_pool", "split_hi", "split_lo",
            "pl_ps", "cbx_ps", "xl_ps", "pc_ps", "v_ps", "turned_ac", "score_ps", "turned_p", "msg_ps", "mu_ps", "cb_ps",
            "edges_ready", "pl_sb", "xlac_sb", "xc_sb", "prod_sb", "t3_sb", "v_sb", "z_sb", "max_sb", "probs_sb",
            "msg_sb", "yt_sb", "cond_dve", "rden_sb", "cbx_sb", "xlv_sb", "tt_sb", "base_sb", "exp_sb", "pt_sb",
            "rh_next", "rx_next",
            "vr_ps", "yn_ps", "qk_ps", "arr_ps", "gT_ps", "spread_ps", "s_ps", "turned_pa", "o_ps", "invT_ps", "wo_ps",
            "ht_ps", "h1_ps", "h3_ps", "down_ps", "lg_sb", "yl_sb", "qk_lo", "arrk_sb", "lgneg_sb", "g3_sb", "nmx_sb",
            "inv_sb", "invT_sb", "va_pad_sb",
            "hh_sb", "htl_sb", "g1_sb", "g2_sb", "mo_sb", "fo_sb", "ffn_dve", "yh_sb", "va_sb", "yn_sb", "qk_hi",
            "arrq_sb", "lge_sb", "gT_sb", "gate_sb", "pa_sb", "pat_sb", "onT_sb", "ss_sb", "hth_sb", "th_sb", "gw_sb",
            "rstd_sb", "res_sb", "ffn_pool",
        ):
            S[name] = sem(name)
        block = ctx.enter_context(nc.Block())

        def at(n, per, k):
            return n * per + k + 1

        def step(name):
            return 1 + ("t3", "g3", "va_pad", "qneg", "qb", "cmd", "kc", "kw", "vc", "qry_w", "qry_b",
                        "rh0", "rhq0", "rh1", "rhq1", "rx", "rxq", "key_w", "key_b", "w2").index(name)

        bias_q, bias_k = pn[:, 0, :], pn[:, 1, :]

        DVE_COND, DVE_FFN = 6 + T * (4 + 2 * 1), 22

        @block.sync
        def _(sp):
            cut = SETUP_COLS["qt"][0]
            sp.dma_start(ws[:, 0:cut], setup_w[:, 0:cut]).then_inc(S["query_in"], 16)
            sp.dma_start(ws[:, cut:NSET], setup_w[:, cut:NSET]).then_inc(S["setup_in"], 16)
            sp.dma_start(xt[:, :], xT[:, 0:W]).then_inc(S["xt_in"], 16)
            sp.dma_start(mb[:, :], msk[:, 0:W].partition_broadcast(P).rearrange("p a w -> p (a w)")).then_inc(S["mask_in"], 16)
            sp.dma_start(ad[:, :].rearrange("p (b j) -> p b j", b=GB), adj[:, 0:GB, :]).then_inc(S["adj_in"], 16)
            cut = COLS["wo"][0]
            sp.dma_start(wt[:, 0:cut], wts[:, 0:cut]).then_inc(S["weights_in"], 16)
            sp.dma_start(cb[:, :], cst_bf).then_inc(S["weights_in"], 16)
            sp.dma_start(ident[:, :], cst_f[:, 0:P]).then_inc(S["weights_in"], 16)
            sp.dma_start(stage[:, W:W + NS], splits).then_inc(S["splits_in"], 16)
            for k in range(2):
                sp.dma_start(arr_in[k], cst_f[:, P + E * E + k * 8 * P:P + E * E + (k + 1) * 8 * P])\
                    .then_inc(S["splits_in"], 16)
            sp.dma_start(wt[:, cut:NW], wts[:, cut:NW]).then_inc(S["late_in"], 16)
            sp.dma_start(tri[:, :, :], cst_f[:, P:P + E * E].rearrange("p (a b) -> p a b", a=E)).then_inc(S["late_in"], 16)
            sp.dma_start(nrm[:, :, :], norms.partition_broadcast(P)).then_inc(S["late_in"], 16)

            def iteration(n, cond, ffn, more):
                if ffn:
                    if not (isinstance(n, int) and n == 1):
                        sp.wait_ge(S["res_sb"], at(n - 2, 1, 0))
                    sp.dma_start(xn[:, :, :], xN[:, bass.ds((n - 1) * GB, GB), :]).then_inc(S["xn_in"], 16)
                if more:
                    sp.wait_ge(S["xl_ps"], at(n, 2, 1))
                    sp.dma_start(xt[:, :], xT[:, bass.ds((n + 1) * W, W)]).then_inc(S["xt_in"], 16)
                    sp.wait_ge(S["edges_ready"], at(n, 1, 0))
                    sp.dma_start(ad[:, :].rearrange("p (b j) -> p b j", b=GB),
                                 adj[:, bass.ds((n + 1) * GB, GB), :]).then_inc(S["adj_in"], 16)
                    sp.wait_ge(S["xc_sb"], at(n, 5, 3))
                    sp.dma_start(mb[:, :], msk[:, bass.ds((n + 1) * W, W)].partition_broadcast(P)
                                 .rearrange("p a w -> p (a w)")).then_inc(S["mask_in"], 16)
                if ffn:
                    sp.wait_ge(S["fo_sb"], at(n - 1, 1, 0))
                    sp.dma_start(out[:, bass.ds((n - 1) * GB, GB), :],
                                 fo[:, :].rearrange("p (b j) -> p b j", b=GB)).then_inc(S["out_stored"], 16)

            iterations(sp, iteration)
            sp.wait_ge(S["out_stored"], 16 * NG)

        @block.tensor
        def _(pe):
            def mm(out_, lhsT, rhs, start=True, stop=True, **kw):
                return pe.matmul(out_, lhsT, rhs, start=start, stop=stop, skip_group_check=True, **kw)

            def split3(out_, k, ah, al):
                wh, wl = hi_w[:, k * P:(k + 1) * P], lo_w[:, k * P:(k + 1) * P]
                mm(out_, wh, ah, stop=False)
                mm(out_, wh, al, start=False, stop=False)
                return mm(out_, wl, ah, start=False)

            pe.wait_ge(S["query_in"], 16)
            mm(ps[:, 0, 0:B], w("qin"), w("qenc")).then_inc(S["setup_pe"], 1)
            pe.wait_ge(S["setup_in"], 16)
            pe.wait_ge(S["setup_dve"], step("qb"))
            for t in range(T):
                i = mm(ps[:, 1, t * B:(t + 1) * B], part("qt", t), qb[:, :], start=(t == 0))
            i.then_inc(S["setup_pe"], 1)
            pe.wait_ge(S["setup_dve"], step("cmd"))
            cm = cmd[:, :, :].rearrange("p t b -> p (t b)")
            mm(ps[:, 2, 0:T * B], w("pk"), cm)
            mm(ps[:, 3, 0:T * B], w("pv"), cm).then_inc(S["setup_pe"], 1)
            pe.wait_ge(S["setup_pool"], 1)
            for k in range(3):
                mm(ps[:, 1, P + k * TY:P + (k + 1) * TY], part("wq", k), w("wes1"), start=(k == 0))
            mm(ps[:, 1, P + 3 * TY:P + 4 * TY], bias_q, w("wes1"), start=False).then_inc(S["setup_pe"], 1)
            pe.wait_ge(S["setup_dve"], step("kw"))
            kw = stage[:, 0:W]
            for k in range(3):
                mm(ps[:, 4 + k, :], part("wk", k), kw).then_inc(S["setup_pe"], 1)
            mm(ps[:, 7, :], bias_k, kw).then_inc(S["setup_pe"], 1)
            pe.wait_ge(S["setup_dve"], step("qry_b"))
            pe.wait_ge(S["weights_in"], 3 * 16)

            def cond_point(n, what, t):
                first = isinstance(n, int) and n == 0
                if what == "start":
                    if not first:
                        pe.wait_ge(S["yt_sb"], at(n - 1, 1, 0))
                    pe.wait_ge(S["xt_in"], 16 * n + 16)
                    mm(ps[:, 2, :], w("pl"), xt[:, :]).then_inc(S["pl_ps"], 1)
                    mm(ps[:, 3, :], w("cb1"), xt[:, :]).then_inc(S["cbx_ps"], 1)
                    if first:
                        pe.wait_ge(S["setup_dve"], step("key_b"))
                        pe.wait_ge(S["setup_pool"], 2)
                    else:
                        pe.wait_ge(S["rx_next"], n)
                    for b in range(GB):
                        o_ = ps[:, b // 2, b % 2 * NX:(b % 2 + 1) * NX]
                        i = mm(o_, xt[:, b * P:(b + 1) * P], rx[:, b, :], start=(b % 2 == 0))
                        if b % 2:
                            i.then_inc(S["xl_ps"], 1)
                elif what == "pc":
                    if t == 0:
                        pe.wait_ge(S["pl_sb"], at(n, 1, 0))
                    pe.wait_ge(S["xc_sb"], at(n, 5, t))
                    mm(ps[:, 2, :], w("pc"), xc[:, :]).then_inc(S["pc_ps"], 1)
                    if t == 0:
                        pe.wait_ge(S["xlac_sb"], at(n, 1, 0))
                        pe.wait_ge(S["xlv_sb"], at(n, 1, 0))
                    if not first or t >= 2:
                        pe.wait_ge(S["rh_next"], 4 * n + t - 1)
                    for b in range(GB):
                        mm(ps[:, b // 2, b % 2 * NV:(b % 2 + 1) * NV], xc[:, b * P:(b + 1) * P], rh[:, 0, b, t % 2, :],
                           start=(b % 2 == 0), stop=False)
                elif what == "vp":
                    pe.wait_ge(S["prod_sb"], at(n, T, t))
                    for b in range(GB):
                        i = mm(ps[:, b // 2, b % 2 * NV:(b % 2 + 1) * NV], pr[:, b * P:(b + 1) * P], rh[:, 1, b, t % 2, :],
                               start=False)
                    i.then_inc(S["v_ps"], 1)
                elif what == "tt":
                    pe.wait_ge(S["t3_sb"], at(n, T, t))
                    if t == 0:
                        pe.wait_ge(S["cbx_sb"], at(n, 1, 0))
                    pe.transpose(ps[:, 3, 0:P // 2].bitcast(BF16), t3[:, :, :].rearrange("p b k -> p (b k)"),
                                 idb).then_inc(S["turned_ac"], 1)
                elif what in ("s0", "s1"):
                    hf = int(what[1])
                    if hf == 0:
                        pe.wait_ge(S["tt_sb"], at(n, T, t))
                        pe.wait_ge(S["v_sb"], at(n, T, t))
                        if t == 0:
                            pe.wait_ge(S["edges_ready"], at(n, 1, 0))
                    for k in range(2):
                        b = 2 * hf + k
                        mm(ps[:, b, :], tt[:, :], sel_qry[:, b, :], start=True, stop=False)
                        mm(ps[:, b, 0:P], idb, pen[:, b * P:(b + 1) * P], start=False, stop=False)
                        for y in range(TY):
                            i = mm(ps[:, b, y * P:(y + 1) * P], sel_key[:, b, y, :], tt[:, :], start=False)
                    i.then_inc(S["score_ps"], 1)
                elif what in ("p0", "p1"):
                    hf = int(what[1])
                    pe.wait_ge(S["probs_sb"], at(n, 2 * T, 2 * t + hf))
                    for k in range(2):
                        b = 2 * hf + k
                        i = pe.transpose(ps[:, 2 * hf, k * P:(k + 1) * P], pn[:, b, :], ident[:, :])
                    i.then_inc(S["turned_p"], 1)
                elif what == "msg":
                    pe.wait_ge(S["pt_sb"], at(n, 2 * T, 2 * t + 1))
                    pe.wait_ge(S["z_sb"], at(n, 2 * T, 2 * t + 1))
                    for b in range(GB):
                        i = mm(ps[:, 3, b * P:(b + 1) * P], v[:, b, :], pt[:, b, :], start=(b == 0))
                    i.then_inc(S["msg_ps"], 1)
                elif what == "mu":
                    mm(ps[:, 1, :], w("mu1"), xc[:, :], stop=False)
                    pe.wait_ge(S["msg_sb"], at(n, T, t))
                    mm(ps[:, 1, :], w("mu2"), ms[:, :], start=False).then_inc(S["mu_ps"], 1)
                elif what == "cb":
                    pe.wait_ge(S["xc_sb"], at(n, 5, 4))
                    pe.wait_ge(S["pt_sb"], at(n, 2 * T, 2 * T - 1))
                    mm(ps[:, 2, :], w("cb2"), xc[:, :]).then_inc(S["cb_ps"], 1)

            def tile_free(f, tile):
                i = TILES.index(tile)
                if i < 2:
                    pe.wait_ge(S["pa_sb"], at(f, 64, 4 * (14 + i) + 3))
                    return
                if i == 2:
                    pe.wait_ge(S["pat_sb"], at(f, 16, 15))
                    return
                old = TILES[i - 3]
                if old == "invT":
                    pe.wait_ge(S["invT_sb"], at(f, 1, 0))
                elif old == "gT":
                    pe.wait_ge(S["gT_sb"], at(f, 1, 0))
                elif old[0] == "gate":
                    pe.wait_ge(S["gate_sb"], at(f, E, old[1]))
                elif old == "ht":
                    pe.wait_ge(S["htl_sb"], at(f, 1, 0))
                elif old[0] == "h1":
                    pe.wait_ge(S["g1_sb"], at(f, NC, old[1]))
                else:
                    pe.wait_ge(S["g2_sb"], at(f, NC, old[1]))

            def down(f, c):
                if c == 0:
                    pe.wait_ge(S["hh_sb"], at(f, 1, 0))
                if c == E:
                    pe.wait_ge(S["mo_sb"], at(f, GB, GB - 1))
                if c < E:
                    pe.wait_ge(S["gw_sb"], at(f, E, c))
                    a, m = gw[:, c % 2, :], part("ew2", c)
                else:
                    pe.wait_ge(S["g2_sb"], at(f, NC, c))
                    a, m = g2[:, c % 3, :], part("w2", c - E)
                for b in range(GB):
                    i = mm(ps[:, 7, b * P:(b + 1) * P], a[:, b * P:(b + 1) * P], m,
                           start=(b == 0 and c in (0, E)), stop=(c in (E - 1, NC - 1)))
                i.then_inc(S["down_ps"], 1)

            def ffn_point(n, what, u):
                f = n - 1
                first = isinstance(n, int) and n == 1
                if what == "vr":
                    pe.wait_ge(S["yt_sb"], at(f, 1, 0))
                    if first:
                        pe.wait_ge(S["late_in"], 3 * 16)
                    else:
                        pe.wait_ge(S["g2_sb"], at(f - 1, NC, NC - 1))
                        pe.wait_ge(S["g1_sb"], at(f - 1, NC, NC - 1))
                    for b in range(GB):
                        i = mm(ps[:, 4 + b // 2, b % 2 * NR:(b % 2 + 1) * NR], yt[:, b * P:(b + 1) * P], w("vr"),
                               start=(b % 2 == 0))
                    i.then_inc(S["vr_ps"], 1)
                elif what == "turn_y":
                    for b in range(GB):
                        i = pe.transpose(ps[:, 6, b * P:(b + 1) * P], yt[:, b * P:(b + 1) * P], ident[:, :])
                    i.then_inc(S["yn_ps"], 1)
                elif what == "q":
                    pe.wait_ge(S["yl_sb"], at(f, 1, 0))
                    if first:
                        pe.wait_ge(S["split_lo"], 2)
                    else:
                        pe.wait_ge(S["fo_sb"], at(f - 1, 1, 0))
                    split3(ps[:, 7, :], 0, yh[:, :], yl[:, :]).then_inc(S["qk_ps"], 1)
                elif what == "k":
                    pe.wait_ge(S["yn_sb"], at(f, 1, 0))
                    split3(ps[:, 6, :], 1, yh[:, :], yl[:, :]).then_inc(S["qk_ps"], 1)
                elif what == "arrange":
                    if u == 1:
                        pe.wait_ge(S["qk_lo"], at(f, 2, 1))
                    for s in range(2):
                        bank = (4, 5)[s] if u % 2 == 0 else (7, 6)[s]
                        if u == 0:
                            pe.wait_ge(S["qk_hi"], at(f, 2, s))
                            pe.wait_ge(S["lg_sb"], at(f, 1, 0))
                            pe.wait_ge(S["va_sb"], at(f, 2, 1))
                            if first:
                                pe.wait_ge(S["split_hi"], 3)
                        elif u >= 2:
                            pe.wait_ge(S["arrk_sb" if s else "arrq_sb"], at(f, 4, u - 2))
                        mm(ps[:, bank, :], arr4[:, 2 * s, u, :], qk_h[:, s, :], stop=False)
                        if u == 0:
                            pe.wait_ge(S["qk_lo"], at(f, 2, s))
                        mm(ps[:, bank, :], arr4[:, 2 * s + 1, u, :], qk_l[:, s, :], start=False).then_inc(S["arr_ps"], 1)
                elif what == "gates":
                    pe.wait_ge(S["g3_sb"], at(f, 1, 0))
                    tile_free(f, "gT")
                    for b in range(GB):
                        i = pe.transpose(ps[0:32, tile_bank("gT"), b * 64:(b + 1) * 64].bitcast(BF16), g3[:, b, :], idb)
                    i.then_inc(S["gT_ps"], 1)
                elif what == "spread":
                    pe.wait_ge(S["gT_sb"], at(f, 1, 0))
                    tile_free(f, ("gate", u))
                    mm(ps[:, tile_bank(("gate", u)), :], sel_exp[:, u, :], gT[:, :]).then_inc(S["spread_ps"], 1)
                elif what == "scores":
                    b, r = divmod(u, 4)
                    if u < 2:
                        pe.wait_ge(S["arrk_sb"], at(f, 4, 3))
                        pe.wait_ge(S["arrq_sb"], at(f, 4, 3))
                    else:
                        pe.wait_ge(S["pa_sb"], at(f, 64, 4 * (u - 2) + 3))
                    mm(ps[:, 4 + u % 2, :], idb, causal, stop=False)
                    for g in range(4):
                        i = mm(ps[:, 4 + u % 2, g * P:(g + 1) * P], qk[32 * r:32 * r + 32, g, 0, b * P:(b + 1) * P],
                               qk[32 * r:32 * r + 32, g, 1, b * P:(b + 1) * P], start=False,
                               tile_position=(32 * r, 0))
                    i.then_inc(S["s_ps"], 1)
                elif what == "values":
                    b, r = divmod(u, 4)
                    pe.wait_ge(S["pat_sb"], at(f, 16, u))
                    pe.wait_ge(S["va_pad_sb"], at(f, 16, u))
                    for g in range(4):
                        h = 4 * g + r
                        i = mm(ps[:, 7, b * P:(b + 1) * P], va_pad[:, h * P:(h + 1) * P], pat[:, u % 2, g, :],
                               start=(u == 0 and g == 0))
                    i.then_inc(S["o_ps"], 1)
                elif what == "turn":
                    pe.wait_ge(S["pa_sb"], at(f, 64, 4 * u + 3))
                    if u:
                        pe.wait_ge(S["pat_sb"], at(f, 16, u - 1))
                    for g in range(4):
                        i = pe.transpose(ps[:, 6, g * P:(g + 1) * P], pa[:, u % 2, g, :], ident[:, :])
                    i.then_inc(S["turned_pa"], 1)
                elif what == "mix":
                    pe.wait_ge(S["inv_sb"], at(f, GB, GB - 1))
                    tile_free(f, "invT")
                    for b in range(GB):
                        i = pe.transpose(ps[:, tile_bank("invT"), b * P:(b + 1) * P],
                                         inv[:, b, :, :].rearrange("p h d -> p (h d)"), ident[:, :])
                    i.then_inc(S["invT_ps"], 1)
                elif what == "out_proj":
                    pe.wait_ge(S["onT_sb"], at(f, 1, 0))
                    for b in range(GB):
                        i = mm(ps[:, 7, b * P:(b + 1) * P], onT[:, b * P:(b + 1) * P], w("wo"), start=(b == 0))
                    i.then_inc(S["wo_ps"], 1)
                elif what == "turn_h":
                    pe.wait_ge(S["hh_sb"], at(f, 1, 0))
                    tile_free(f, "ht")
                    for b in range(GB):
                        i = pe.transpose(ps[:, tile_bank("ht"), b * P:(b + 1) * P], hh[:, b * P:(b + 1) * P], ident[:, :])
                    i.then_inc(S["ht_ps"], 1)
                elif what in ("h1", "h3"):
                    if u == E:
                        pe.wait_ge(S["htl_sb"], at(f, 1, 0))
                    ah, al = (yh, yl) if u < E else (hth, htl)
                    tile_free(f, (what, u))
                    split3(ps[:, tile_bank((what, u)), :], 2 + 2 * u + (what == "h3"), ah[:, :], al[:, :])\
                        .then_inc(S[what + "_ps"], 1)
                elif what == "down":
                    down(f, u)

            iterations(pe, lambda n, cond, ffn, more: [
                (cond_point if k == "c" else ffn_point)(n, what, t) for k, what, t in points(cond, ffn)])

        @block.vector
        def _(dve):
            count = [0]

            def setup(name, ins):
                count[0] += 1
                assert step(name) == count[0]
                ins.then_inc(S["setup_dve"], 1)
                dve.wait_ge(S["setup_dve"], count[0])

            setup("t3", dve.memset(t3[:, :, :], 0.0))
            setup("g3", dve.memset(g3[:, :, :], 0.0))
            setup("va_pad", dve.memset(va_pad[:, :], 0.0))
            dve.wait_ge(S["setup_pe"], 1)
            dve.wait_ge(S["query_in"], 16)
            dve.wait_ge(S["setup_in"], 16)
            setup("qneg", dve.tensor_scalar(qneg[:, :], ps[:, 0, 0:B], col("bqin"), 0.0, ALU.add, ALU.min))
            dve.wait_ge(S["setup_act"], 2)
            setup("qb", dve.scalar_tensor_tensor(out=qb[:, :], in0=qneg[:, :], scalar=-1.0, in1=qb[:, :],
                                                 op0=ALU.add, op1=ALU.add))
            dve.wait_ge(S["setup_pe"], 2)
            setup("cmd", dve.tensor_tensor(cmd[:, :, :], ps[:, 1, 0:T * B].rearrange("p (t b) -> p t b", t=T),
                                           w("bqt").unsqueeze(2).to_broadcast([P, T, B]), ALU.add))
            dve.wait_ge(S["setup_pe"], 3)
            setup("kc", dve.tensor_scalar(kc[:, :, :].rearrange("p t b -> p (t b)"), ps[:, 2, 0:T * B], col("bpk"), None,
                                          ALU.add))
            setup("kw", dve.tensor_tensor(stage[:, 0:W].rearrange("p (b t y) -> p b t y", b=B, t=T),
                                          kc[:, :, :].rearrange("p t b -> p b t").unsqueeze(3).to_broadcast([P, B, T, TY]),
                                          w("wes2").unsqueeze(1).unsqueeze(1).to_broadcast([P, B, T, TY]), ALU.mult))
            setup("vc", dve.tensor_scalar(vc[:, :, :].rearrange("p t b -> p (t b)"), ps[:, 3, 0:T * B], col("bpv"), None,
                                          ALU.add))
            dve.wait_ge(S["setup_pe"], 4)
            setup("qry_w", dve.tensor_copy(qry_w[:, :, :], ps[:, 1, P:P + 3 * TY].rearrange("p (k y) -> p k y", k=3)))
            setup("qry_b", dve.tensor_copy(qry_b[:, :], ps[:, 1, P + 3 * TY:P + 4 * TY]))
            for k in range(2):
                x = rh[:, k, :, :, :].rearrange("p b r c -> p (b r) c")
                setup(f"rh{k}", dve.tensor_copy(x[:, :, 0:P], w(("v2", "v3")[k]).unsqueeze(1).to_broadcast([P, 2 * GB, P])))
                setup(f"rhq{k}", dve.tensor_copy(x[:, :, P:P + TY],
                                                 qry_w[:, 1 + k, :].unsqueeze(1).to_broadcast([P, 2 * GB, TY])))
            setup("rx", dve.tensor_copy(rx[:, :, 0:P], w("v1").unsqueeze(1).to_broadcast([P, GB, P])))
            setup("rxq", dve.tensor_copy(rx[:, :, P:P + TY], qry_w[:, 0, :].unsqueeze(1).to_broadcast([P, GB, TY])))
            dve.wait_ge(S["setup_pe"], 6)
            setup("key_w", dve.tensor_copy(key_w[:, 1, :], ps[:, 5, :]))
            dve.wait_ge(S["setup_pe"], 8)
            setup("key_b", dve.tensor_copy(key_b[:, :], ps[:, 7, :]))
            dve.wait_ge(S["weights_in"], 3 * 16)

            state = {}

            def link(kind, n, per, ins):
                state[kind] += 1
                ins.then_inc(S[kind], 1)
                dve.wait_ge(S[kind], n * per + state[kind])

            def values(lo, hi):
                return ps[:, 0:2, 0:2 * NV].rearrange("p k (b c) -> p k b c", b=2)[:, :, :, lo:hi]

            def cond_point(n, what, t):
                first = isinstance(n, int) and n == 0
                if what == "edges":
                    dve.wait_ge(S["mask_in"], 16 * n + 16)
                    dve.tensor_scalar(xc[:, :], mb[:, :], col("init"), None, ALU.mult).then_inc(S["xc_sb"], 1)
                    dve.wait_ge(S["adj_in"], 16 * n + 16)
                    if not first:
                        dve.wait_ge(S["score_ps"], at(n - 1, 2 * T, 2 * T - 1))
                    for y in range(1, TY):
                        link("cond_dve", n, DVE_COND,
                             dve.tensor_scalar(is_ty[:, y - 1, :], ad[:, :], float(y + 1), None, ALU.is_equal))
                    dve.tensor_scalar(pen[:, :], ad[:, :], 0.0, MASKED, ALU.is_le, ALU.mult).then_inc(S["edges_ready"], 1)
                elif what == "xl":
                    dve.wait_ge(S["pl_ps"], at(n, 1, 0))
                    dve.tensor_scalar(pl[:, :], ps[:, 2, :], col("bpl"), None, ALU.add).then_inc(S["pl_sb"], 1)
                    dve.wait_ge(S["xl_ps"], at(n, 2, 1))
                    for k in range(2):
                        bs = slice(2 * k, 2 * k + 2)
                        x = ps[:, k, 0:2 * NX].rearrange("p (b c) -> p b c", b=2)
                        link("cond_dve", n, DVE_COND, dve.tensor_tensor(
                            xlac[:, bs, :, TY:2 * TY], x[:, :, P + TY:NX].rearrange("p b (t y) -> p b t y", t=T),
                            key_b[:, bass.ds((n * GB + 2 * k) * T * TY, 2 * T * TY)]
                            .rearrange("p (b t y) -> p b t y", b=2, t=T), ALU.add))
                        i = dve.tensor_tensor(xlac[:, bs, :, 0:TY], x[:, :, P:P + TY].unsqueeze(2).to_broadcast([P, 2, T, TY]),
                                              qry_b[:, :].unsqueeze(1).unsqueeze(1).to_broadcast([P, 2, T, TY]), ALU.add)
                        if k == 0:
                            link("cond_dve", n, DVE_COND, i)
                    i.then_inc(S["xlac_sb"], 1)
                elif what == "pr":
                    dve.wait_ge(S["pc_ps"], at(n, T, t))
                    dve.wait_ge(S["pl_sb"], at(n, 1, 0))
                    dve.scalar_tensor_tensor(out=pr[:, :], in0=ps[:, 2, :], scalar=col("bpc"), in1=pl[:, :],
                                             op0=ALU.add, op1=ALU.mult).then_inc(S["prod_sb"], 1)
                elif what == "sc":
                    dve.wait_ge(S["v_ps"], at(n, T, t))
                    if t == 0:
                        dve.wait_ge(S["xlac_sb"], at(n, 1, 0))
                    sc = values(P, NV)
                    xa = xlac[:, :, t, :].rearrange("p (k b) y -> p k b y", k=2)
                    dve.tensor_tensor(ac[:, :, :].rearrange("p (k b) y -> p k b y", k=2), sc, xa, ALU.add)\
                        .then_inc(S["cond_dve"], 1)
                    state["cond_dve"] += 1
                    link("cond_dve", n, DVE_COND, dve.tensor_tensor(
                        t3[:, :, 0:8].rearrange("p (k b) y -> p k b y", k=2), sc, xa, ALU.add))
                    dve.tensor_tensor(ac_r[:, :, :], ac[:, :, :], t3[:, :, 0:8], ALU.subtract).then_inc(S["cond_dve"], 1)
                    state["cond_dve"] += 1
                    link("cond_dve", n, DVE_COND,
                         dve.tensor_tensor(t3[:, :, 8:16], ac[:, :, :], t3[:, :, 0:8], ALU.subtract))
                    dve.tensor_tensor(t3[:, :, 16:24], ac_r[:, :, :], t3[:, :, 8:16], ALU.subtract).then_inc(S["t3_sb"], 1)
                elif what == "vv":
                    dve.wait_ge(S["v_ps"], at(n, T, t))
                    if t == 0:
                        dve.wait_ge(S["xlv_sb"], at(n, 1, 0))
                    dve.tensor_tensor(v[:, :, :].rearrange("p (k b) d -> p k b d", k=2), values(0, P),
                                      xlv[:, :, :].rearrange("p (k b) d -> p k b d", k=2), ALU.add).then_inc(S["v_sb"], 1)
                elif what in ("z0", "z1"):
                    hf = int(what[1])
                    k = 2 * t + hf
                    bs = slice(2 * hf, 2 * hf + 2)
                    dve.wait_ge(S["base_sb"], at(n, 2 * T, k))
                    if t == 0 and hf == 0:
                        dve.wait_ge(S["edges_ready"], at(n, 1, 0))
                    dve.memset(carrier[:, :], 0.0)
                    dve.drain()
                    for y in range(1, TY):
                        i = dve.copy_predicated(z[:, bs, :],
                                                is_ty[:, y - 1, 2 * hf * P:(2 * hf + 2) * P].rearrange("p (b j) -> p b j", b=2),
                                                ps[:, 2 * hf:2 * hf + 2, y * P:(y + 1) * P])
                        if y < TY - 1:
                            dve.drain()
                    i.then_inc(S["z_sb"], 1)
                    dve.wait_ge(S["z_sb"], at(n, 2 * T, k))
                    link("cond_dve", n, DVE_COND, dve.scalar_tensor_tensor(
                        out=lk[:, bs, :], in0=z[:, bs, :], scalar=ALPHA, in1=z[:, bs, :], op0=ALU.mult, op1=ALU.max))
                    dve.tensor_reduce(neg_mx[:, bs], lk[:, bs, :], AX_X, ALU.max, negate=True).then_inc(S["max_sb"], 1)
                elif what in ("n0", "n1"):
                    hf = int(what[1])
                    k = 2 * t + hf
                    bs = slice(2 * hf, 2 * hf + 2)
                    dve.wait_ge(S["exp_sb"], at(n, 4 * T, 2 * k + 1))
                    dve.reciprocal(rden[:, bs], den[:, bs]).then_inc(S["rden_sb"], 1)
                    dve.wait_ge(S["rden_sb"], at(n, 2 * T, k))
                    dve.tensor_tensor(pn[:, bs, :], pe_[:, bs, :], rden[:, bs].unsqueeze(2).to_broadcast([P, 2, P]),
                                      ALU.mult).then_inc(S["probs_sb"], 1)
                elif what == "ms":
                    dve.wait_ge(S["msg_ps"], at(n, T, t))
                    dve.scalar_tensor_tensor(out=ms[:, :].rearrange("p (b i) -> p b i", b=GB),
                                             in0=ps[:, 3, :].rearrange("p (b i) -> p b i", b=GB), scalar=col("bv"),
                                             in1=vc[:, t, bass.ds(n * GB, GB)].unsqueeze(2).to_broadcast([P, GB, P]),
                                             op0=ALU.add, op1=ALU.mult).then_inc(S["msg_sb"], 1)
                elif what == "xc":
                    dve.wait_ge(S["mu_ps"], at(n, T, t))
                    if t < T - 1:
                        dve.scalar_tensor_tensor(out=xc[:, :], in0=ps[:, 1, :], scalar=col("bmu"), in1=mb[:, :],
                                                 op0=ALU.add, op1=ALU.mult).then_inc(S["xc_sb"], 1)
                    else:
                        dve.tensor_scalar(xc[:, :], ps[:, 1, :], col("bmu"), None, ALU.add).then_inc(S["xc_sb"], 1)
                    if first and t == 0:
                        dve.wait_ge(S["late_in"], 3 * 16)
                        setup("w2", dve.tensor_scalar(w("w2"), w("w2"), 0.5, None, ALU.mult))
                elif what == "yt":
                    dve.wait_ge(S["cb_ps"], at(n, 1, 0))
                    if not first:
                        dve.wait_ge(S["yn_ps"], at(n - 1, 1, 0))
                        dve.wait_ge(S["yl_sb"], at(n - 1, 1, 0))
                    dve.tensor_tensor(yt[:, :], ps[:, 2, :], cbx[:, :], ALU.add).then_inc(S["yt_sb"], 1)

            def gates(f):
                def l(ins):
                    link("ffn_dve", f, DVE_FFN, ins)

                def over(x):
                    return x.unsqueeze(2).to_broadcast([P, GB, E])
                dve.wait_ge(S["lge_sb"], at(f, 1, 0))
                l(dve.tensor_reduce(lgs[:, :], lge[:, :, :], AX_X, ALU.add))
                l(dve.reciprocal(lgs[:, :], lgs[:, :]))
                l(dve.tensor_tensor(prb[:, :, :], lge[:, :, :], over(lgs[:, :]), ALU.mult))
                mine = prb[:, :, :].unsqueeze(3).to_broadcast([P, GB, E, E])
                other = prb[:, :, :].unsqueeze(2).to_broadcast([P, GB, E, E])
                l(dve.tensor_tensor(gt[:, :, :, :], other, mine, ALU.is_gt))
                l(dve.tensor_tensor(eq[:, :, :, :], other, mine, ALU.is_equal))
                l(dve.tensor_tensor(eq[:, :, :, :], eq[:, :, :, :],
                                    tri[:, :, :].unsqueeze(1).to_broadcast([P, GB, E, E]), ALU.mult))
                l(dve.tensor_tensor(gt[:, :, :, :], gt[:, :, :, :], eq[:, :, :, :], ALU.add))
                l(dve.tensor_reduce(rank[:, :, :], gt[:, :, :, :], AX_X, ALU.add))
                l(dve.tensor_scalar(rank[:, :, :], rank[:, :, :], 1.5, 0.5, ALU.is_lt, ALU.mult))
                l(dve.tensor_tensor(gate[:, :, :], rank[:, :, :], prb[:, :, :], ALU.mult))
                l(dve.tensor_copy(g3[:, :, 0:E], gate[:, :, :]))
                l(dve.tensor_tensor(gate_r[:, :, :], gate[:, :, :], g3[:, :, 0:E], ALU.subtract))
                l(dve.tensor_copy(g3[:, :, E:2 * E], gate_r[:, :, :]))
                dve.tensor_tensor(g3[:, :, 2 * E:3 * E], gate_r[:, :, :], g3[:, :, E:2 * E], ALU.subtract)\
                    .then_inc(S["g3_sb"], 1)

            def normed(f, k, src, dst):
                dve.wait_ge(S["rstd_sb"], at(f, 3, k))
                for b in range(GB):
                    i = dve.scalar_tensor_tensor(out=dst[:, b * P:(b + 1) * P], in0=src[:, b * P:(b + 1) * P],
                                                 scalar=rstd[:, k, b:b + 1], in1=nrm[:, k, :],
                                                 op0=ALU.mult, op1=ALU.mult)
                    if k == 1:
                        i.then_inc(S["mo_sb"], 1)
                    elif b < GB - 1:
                        i.then_inc(S["ffn_dve"], 1)
                        state["ffn_dve"] += 1
                return i

            def gated(f, c, k):
                if k == 1:
                    dve.wait_ge(S["th_sb"], at(f, NC, c))
                    dve.scalar_tensor_tensor(out=g1[:, c % 2, :], in0=th[:, c % 2, :], scalar=1.0,
                                             in1=ps[:, tile_bank(("h1", c)), :], op0=ALU.add, op1=ALU.mult)\
                        .then_inc(S["g1_sb"], 1)
                    return
                dve.wait_ge(S["h3_ps"], at(f, NC, c))
                dve.wait_ge(S["g1_sb"], at(f, NC, c))
                if 3 <= c < E + 3:
                    dve.wait_ge(S["gw_sb"], at(f, E, c - 3))
                elif c >= E + 3:
                    dve.wait_ge(S["down_ps"], at(f, NC, c - 3))
                dve.tensor_tensor(g2[:, c % 3, :], g1[:, c % 2, :], ps[:, tile_bank(("h3", c)), :], ALU.mult)\
                    .then_inc(S["g2_sb"], 1)

            def ffn_point(n, what, u):
                f = n - 1
                first = isinstance(n, int) and n == 1
                if what == "lg":
                    dve.wait_ge(S["vr_ps"], at(f, 1, 0))
                    dve.tensor_copy(lg[:, :, :].rearrange("p (k b) e -> p k b e", k=2),
                                    ps[:, 4:6, 0:2 * NR].rearrange("p k (b c) -> p k b c", b=2)[:, :, :, P:NR])\
                        .then_inc(S["lg_sb"], 1)
                    dve.wait_ge(S["yh_sb"], at(f, 1, 0))
                    dve.tensor_tensor(yl[:, :], yt[:, :], yh[:, :].bitcast(F32), ALU.subtract).then_inc(S["yl_sb"], 1)
                    dve.wait_ge(S["lg_sb"], at(f, 1, 0))
                    link("ffn_dve", f, DVE_FFN, dve.tensor_reduce(lgm[:, :], lg[:, :, :], AX_X, ALU.max))
                    dve.tensor_tensor(lg[:, :, :], lg[:, :, :], lgm[:, :].unsqueeze(2).to_broadcast([P, GB, E]),
                                      ALU.subtract).then_inc(S["lgneg_sb"], 1)
                elif what == "q_sb":
                    dve.wait_ge(S["qk_hi"], at(f, 2, 0))
                    dve.scalar_tensor_tensor(out=qk_l[:, 0, :], in0=ps[:, 7, :], scalar=HD ** -0.5,
                                             in1=qk_h[:, 0, :].bitcast(F32), op0=ALU.mult, op1=ALU.subtract)\
                        .then_inc(S["qk_lo"], 1)
                elif what == "k_sb":
                    dve.wait_ge(S["qk_hi"], at(f, 2, 1))
                    dve.tensor_tensor(qk_l[:, 1, :], ps[:, 6, :], qk_h[:, 1, :].bitcast(F32), ALU.subtract)\
                        .then_inc(S["qk_lo"], 1)
                elif what == "choose":
                    gates(f)
                elif what == "arr":
                    dve.wait_ge(S["arr_ps"], at(f, 8, 2 * u + 1))
                    dve.tensor_copy(qk[:, u, 1, :], ps[:, 5 if u % 2 == 0 else 6, :]).then_inc(S["arrk_sb"], 1)
                elif what == "max":
                    dve.wait_ge(S["s_ps"], at(f, 16, u))
                    if u >= 2:
                        dve.wait_ge(S["pa_sb"], at(f, 64, 4 * (u - 2) + 3))
                    dve.tensor_reduce(nmx[:, u % 2, :], ps[:, 4 + u % 2, :].rearrange("p (g j) -> p g j", g=4),
                                      AX_X, ALU.max, negate=True).then_inc(S["nmx_sb"], 1)
                elif what == "inv":
                    dve.wait_ge(S["pa_sb"], at(f, 64, 16 * u + 15))
                    dve.reciprocal(inv[:, u, :, :], sums[:, u, :].unsqueeze(2).to_broadcast([P, H, HD]))\
                        .then_inc(S["inv_sb"], 1)
                elif what == "onT":
                    dve.wait_ge(S["o_ps"], at(f, 16, 15))
                    dve.wait_ge(S["invT_sb"], at(f, 1, 0))
                    dve.tensor_tensor(onT[:, :], ps[:, 7, :], onT[:, :], ALU.mult).then_inc(S["onT_sb"], 1)
                elif what == "norm_h":
                    i = normed(f, 0, ps[:, 7, :], nh)
                    link("ffn_dve", f, DVE_FFN, i)
                    dve.wait_ge(S["yn_sb"], at(f, 1, 0))
                    if not first:
                        dve.wait_ge(S["out_stored"], 16 * (n - 1))
                    dve.tensor_tensor(hh[:, :], nh[:, :], yn[:, :, :].rearrange("p b d -> p (b d)"), ALU.add)\
                        .then_inc(S["hh_sb"], 1)
                elif what == "h_parts":
                    dve.wait_ge(S["hth_sb"], at(f, 1, 0))
                    dve.tensor_tensor(htl[:, :], ps[:, tile_bank("ht"), :], hth[:, :].bitcast(F32), ALU.subtract)\
                        .then_inc(S["htl_sb"], 1)
                elif what in ("g1", "g2"):
                    gated(f, u, int(what[1]))
                elif what == "norm_m":
                    normed(f, 1, ps[:, 7, :], mo)
                elif what == "last":
                    i = normed(f, 2, ps[:, 7, :], nh)
                    link("ffn_dve", f, DVE_FFN, i)
                    dve.wait_ge(S["res_sb"], at(f, 1, 0))
                    dve.tensor_tensor(fo[:, :], nh[:, :], res[:, :], ALU.add).then_inc(S["fo_sb"], 1)

            def iteration(n, cond, ffn, more):
                state["cond_dve"] = state["ffn_dve"] = 0
                for k, what, t in points(cond, ffn):
                    (cond_point if k == "c" else ffn_point)(n, what, t)
                assert state["cond_dve"] == (DVE_COND if cond else 0), state
                assert state["ffn_dve"] == (DVE_FFN if ffn else 0), state

            iterations(dve, iteration)

        @block.scalar
        def _(act):
            act.wait_ge(S["setup_dve"], step("qneg"))
            act.activation(qneg[:, :], qneg[:, :], ACT.Exp).then_inc(S["setup_act"], 1)
            act.wait_ge(S["setup_pe"], 1)
            act.activation(qb[:, :], ps[:, 0, 0:B], ACT.Relu, bias=col("bqin")).then_inc(S["setup_act"], 1)
            for k in (0, 2):
                act.wait_ge(S["setup_pe"], 5 + k)
                act.activation(key_w[:, k, :], ps[:, 4 + k, :], ACT.Copy).then_inc(S["setup_act"], 1)

            def cond_point(n, what, t):
                first = isinstance(n, int) and n == 0
                if what == "xl":
                    act.wait_ge(S["cbx_ps"], at(n, 1, 0))
                    if not first:
                        act.wait_ge(S["yt_sb"], at(n - 1, 1, 0))
                    act.activation(cbx[:, :], ps[:, 3, :], ACT.Identity, bias=col("bcb")).then_inc(S["cbx_sb"], 1)
                    act.wait_ge(S["xlac_sb"], at(n, 1, 0))
                    act.activation(xlv[:, :, :].rearrange("p (k b) d -> p k b d", k=2),
                                   ps[:, 0:2, 0:2 * NX].rearrange("p k (b c) -> p k b c", b=2)[:, :, :, 0:P],
                                   ACT.Copy).then_inc(S["xlv_sb"], 1)
                elif what == "tt":
                    act.wait_ge(S["turned_ac"], at(n, T, t))
                    act.activation(tt[:, :], ps[:, 3, 0:P // 2].bitcast(BF16), ACT.Copy).then_inc(S["tt_sb"], 1)
                elif what in ("s0", "s1"):
                    hf = int(what[1])
                    k = 2 * t + hf
                    act.wait_ge(S["score_ps"], at(n, 2 * T, k))
                    act.activation(z[:, 2 * hf:2 * hf + 2, :], ps[:, 2 * hf:2 * hf + 2, 0:P], ACT.Copy).then_inc(S["base_sb"], 1)
                elif what in ("e0", "e1"):
                    hf = int(what[1])
                    k = 2 * t + hf
                    act.wait_ge(S["max_sb"], at(n, 2 * T, k))
                    for b in (2 * hf, 2 * hf + 1):
                        act.activation(pe_[:, b, :], lk[:, b, :], ACT.Exp, bias=neg_mx[:, b:b + 1],
                                       accum_out=den[:, b:b + 1]).then_inc(S["exp_sb"], 1)
                elif what in ("pt0", "pt1"):
                    hf = int(what[2])
                    k = 2 * t + hf
                    act.wait_ge(S["turned_p"], at(n, 2 * T, k))
                    act.activation(pt[:, 2 * hf:2 * hf + 2, :].rearrange("p b i -> p (b i)"), ps[:, 2 * hf, 0:2 * P],
                                   ACT.Copy).then_inc(S["pt_sb"], 1)

                elif what == "xc" and first and t < 3:
                    act.wait_ge(S["splits_in"], 48)
                    if t < 2:
                        sl = slice(t * NS // 2, (t + 1) * NS // 2)
                        i = act.activation(hi_w[:, sl], stage[:, W:W + NS][:, sl], ACT.Copy)
                    else:
                        act.activation(arr[:, 0:8 * P], arr_in[0], ACT.Copy)
                        i = act.activation(arr[:, 8 * P:], arr_in[1], ACT.Copy)
                    i.then_inc(S["split_hi"], 1)

            def squares(f, k, src):
                for b in range(GB):
                    act.activation(sq[:, :], src[:, b * P:(b + 1) * P], ACT.Square, scale=P ** -0.5,
                                   accum_out=ss[:, k, b:b + 1]).then_inc(S["ss_sb"], 1)
                    act.wait_ge(S["ss_sb"], at(f, 3 * GB, k * GB + b))

            def ffn_point(n, what, u):
                f = n - 1
                first = isinstance(n, int) and n == 1
                if what == "lg":
                    act.wait_ge(S["yt_sb"], at(f, 1, 0))
                    act.activation(yh[:, :], yt[:, :], ACT.Copy).then_inc(S["yh_sb"], 1)
                elif what == "va":
                    act.wait_ge(S["lg_sb"], at(f, 1, 0))
                    for k in range(2):
                        act.activation(va[:, 2 * k:2 * k + 2, :, 0:HD],
                                       ps[:, 4 + k, 0:2 * NR].rearrange("p (b c) -> p b c", b=2)[:, :, 0:P]
                                       .rearrange("p b (h d) -> p b h d", h=H), ACT.Copy).then_inc(S["va_sb"], 1)
                elif what == "turn_y":
                    act.wait_ge(S["yn_ps"], at(f, 1, 0))
                    act.activation(yn[:, :, :].rearrange("p b d -> p (b d)"), ps[:, 6, :], ACT.Copy).then_inc(S["yn_sb"], 1)
                elif what in ("q_sb", "k_sb"):
                    s = ("q_sb", "k_sb").index(what)
                    act.wait_ge(S["qk_ps"], at(f, 2, s))
                    act.activation(qk_h[:, s, :], ps[:, (7, 6)[s], :], ACT.Copy,
                                   scale=(HD ** -0.5, 1.0)[s]).then_inc(S["qk_hi"], 1)
                elif what == "choose":
                    act.wait_ge(S["lgneg_sb"], at(f, 1, 0))
                    act.activation(lge[:, :, :], lg[:, :, :], ACT.Exp).then_inc(S["lge_sb"], 1)
                elif what == "arr":
                    act.wait_ge(S["arr_ps"], at(f, 8, 2 * u))
                    act.activation(qk[:, u, 0, :], ps[:, 4 if u % 2 == 0 else 7, :], ACT.Copy).then_inc(S["arrq_sb"], 1)
                elif what == "gates":
                    act.wait_ge(S["gT_ps"], at(f, 1, 0))
                    act.activation(gT[:, :], ps[0:32, tile_bank("gT"), 0:W // 2].bitcast(BF16), ACT.Copy).then_inc(S["gT_sb"], 1)
                elif what == "exps":
                    act.wait_ge(S["nmx_sb"], at(f, 16, u))
                    if u >= 2:
                        act.wait_ge(S["turned_pa"], at(f, 16, u - 2))
                    if u == 0 and not first:
                        act.wait_ge(S["inv_sb"], at(f - 1, GB, GB - 1))
                    for g in range(4):
                        h = 4 * g + u % 4
                        act.activation(pa[:, u % 2, g, :], ps[:, 4 + u % 2, g * P:(g + 1) * P], ACT.Exp,
                                       bias=nmx[:, u % 2, g:g + 1], accum_out=sums[:, u // 4, h:h + 1])\
                            .then_inc(S["pa_sb"], 1)
                elif what == "gate":
                    act.wait_ge(S["spread_ps"], at(f, E, u))
                    act.activation(gate_w[:, u, :], ps[:, tile_bank(("gate", u)), :], ACT.Copy).then_inc(S["gate_sb"], 1)
                elif what == "pat":
                    act.wait_ge(S["turned_pa"], at(f, 16, u))
                    if u >= 2:
                        act.wait_ge(S["o_ps"], at(f, 16, u - 2))
                    act.activation(pat[:, u % 2, :, :].rearrange("p g i -> p (g i)"), ps[:, 6, :], ACT.Copy)\
                        .then_inc(S["pat_sb"], 1)
                elif what == "mix":
                    act.wait_ge(S["invT_ps"], at(f, 1, 0))
                    act.activation(onT[:, :], ps[:, tile_bank("invT"), :], ACT.Copy).then_inc(S["invT_sb"], 1)
                elif what == "sq_a":
                    act.wait_ge(S["wo_ps"], at(f, 1, 0))
                    squares(f, 0, ps[:, 7, :])
                elif what == "h_parts":
                    act.wait_ge(S["ht_ps"], at(f, 1, 0))
                    act.activation(hth[:, :], ps[:, tile_bank("ht"), :], ACT.Copy).then_inc(S["hth_sb"], 1)
                elif what == "th":
                    act.wait_ge(S["h1_ps"], at(f, NC, u))
                    if u >= 2:
                        act.wait_ge(S["g1_sb"], at(f, NC, u - 2))
                    act.activation(th[:, u % 2, :], ps[:, tile_bank(("h1", u)), :], ACT.Tanh, scale=0.5)\
                        .then_inc(S["th_sb"], 1)
                elif what == "sq_m":
                    act.wait_ge(S["down_ps"], at(f, NC, E - 1))
                    squares(f, 1, ps[:, 7, :])
                elif what == "sq_f":
                    act.wait_ge(S["down_ps"], at(f, NC, NC - 1))
                    squares(f, 2, ps[:, 7, :])

            iterations(act, lambda n, cond, ffn, more: [
                (cond_point if k == "c" else ffn_point)(n, what, t) for k, what, t in points(cond, ffn)])

        @block.gpsimd
        def _(pool):
            kw5 = key_w[:, :, :].rearrange("p k (b t y) -> p k b t y", b=B, t=T)

            def keys(n, t):
                for k in range(2):
                    i = pool.tensor_copy(rh[:, k, :, t % 2, P + TY:NV], kw5[:, 1 + k, bass.ds(n * GB, GB), t, :])
                return i

            def keys_x(n):
                x = key_w[:, 0, bass.ds(n * GB * T * TY, GB * T * TY)].rearrange("p (b c) -> p b c", b=GB)
                return pool.tensor_copy(rx[:, :, P + TY:NX], x)

            pool.memset(half_pow[:, :], -0.5)
            pool.memset(eps[:, :], EPS)
            pool.memset(ones[:, :], 1.0)
            pool.wait_ge(S["setup_in"], 16)
            pool.tensor_copy(bias_q, w("bq").to_broadcast([P, P]))
            pool.tensor_copy(bias_k, w("bk").to_broadcast([P, P])).then_inc(S["setup_pool"], 1)
            pool.wait_ge(S["setup_dve"], step("key_w"))
            pool.wait_ge(S["setup_act"], 4)
            keys_x(0)
            for t in range(2):
                i = keys(0, t)
            i.then_inc(S["setup_pool"], 1)
            pool.wait_ge(S["setup_pool"], 2)

            def cond_point(n, what, t, more):
                if what == "pc" and t == 0 and more:
                    pool.wait_ge(S["xl_ps"], at(n, 2, 1))
                    keys_x(n + 1).then_inc(S["rx_next"], 1)
                if what == "tt" and (more or t < 2):
                    pool.wait_ge(S["v_ps"], at(n, T, t))
                    keys(n + (t + 2) // T, (t + 2) % T).then_inc(S["rh_next"], 1)

                if what == "xc" and more and isinstance(n, int) and n == 0 and t < 2:
                    pool.wait_ge(S["split_hi"], t + 1)
                    sl = slice(t * NS // 2, (t + 1) * NS // 2)
                    pool.tensor_tensor(lo_w[:, sl], stage[:, W:W + NS][:, sl], hi_w[:, sl].bitcast(F32), ALU.subtract)\
                        .then_inc(S["split_lo"], 1)

            def rstd_of(f, k):
                pool.wait_ge(S["ss_sb"], at(f, 3 * GB, k * GB + GB - 1))
                pool.tensor_tensor(rs[:, k, :], ss[:, k, :], eps[:, :], ALU.add).then_inc(S["ffn_pool"], 1)
                pool.wait_ge(S["ffn_pool"], at(f, 4, (0, 1, 3)[k]))
                pool.tensor_tensor(rstd[:, k, :], rs[:, k, :], half_pow[:, :], ALU.pow).then_inc(S["rstd_sb"], 1)

            def weighted(f, e):
                pool.wait_ge(S["g2_sb"], at(f, NC, e))
                pool.wait_ge(S["gate_sb"], at(f, E, e))
                if e >= 2:
                    pool.wait_ge(S["down_ps"], at(f, NC, e - 2))
                pool.tensor_tensor(gw[:, e % 2, :], g2[:, e % 3, :], gate_w[:, e, :], ALU.mult).then_inc(S["gw_sb"], 1)

            def pad(f, q):
                b, r = divmod(q, 4)
                x = va[:, b, :, :].rearrange("p (g r) d -> p g r d", g=4)[:, :, r, :]
                pool.tensor_tensor(va_pad[:, :].rearrange("p (g r c) -> p g r c", g=4, r=4)[:, :, r, 0:HD], x,
                                   ones[:, :].unsqueeze(2).to_broadcast([P, 4, HD]), ALU.mult)\
                    .then_inc(S["va_pad_sb"], 1)

            def ffn_point(n, what, u):
                f = n - 1
                first = isinstance(n, int) and n == 1
                if what == "pad":
                    pool.wait_ge(S["va_sb"], at(f, 2, 1))
                    if not first:
                        pool.wait_ge(S["o_ps"], at(f - 1, 16, 12 + u))
                    pad(f, u)
                elif what == "pad_next":
                    pool.wait_ge(S["o_ps"], at(f, 16, u))
                    pad(f, u + 4)
                elif what == "sq_a":
                    rstd_of(f, 0)
                elif what == "gw":
                    weighted(f, u)
                elif what == "sq_m":
                    rstd_of(f, 1)
                elif what == "sq_f":
                    rstd_of(f, 2)
                elif what == "res":
                    pool.wait_ge(S["mo_sb"], at(f, GB, GB - 1))
                    pool.wait_ge(S["hh_sb"], at(f, 1, 0))
                    pool.tensor_tensor(res[:, :], hh[:, :], mo[:, :], ALU.add).then_inc(S["ffn_pool"], 1)
                    pool.wait_ge(S["xn_in"], 16 * n)
                    pool.wait_ge(S["ffn_pool"], at(f, 4, 2))
                    pool.tensor_tensor(res[:, :], res[:, :], xn[:, :, :].rearrange("p b d -> p (b d)"), ALU.add)\
                        .then_inc(S["res_sb"], 1)

            def iteration(n, cond, ffn, more):
                for k, what, t in points(cond, ffn):
                    if k == "f":
                        ffn_point(n, what, t)
                    else:
                        cond_point(n, what, t, more)

            iterations(pool, iteration)


def iterations(eng, body):
    body(0, True, False, True)
    body(1, True, True, True)
    with eng.Fori(2, NG - 1) as n:
        body(n, True, True, True)
    body(NG - 1, True, True, False)
    body(NG, False, True, False)


def _constants():
    import numpy as np
    bf = np.zeros((P, P + 512 + 16 * P + 4 * 512 + E * P), np.float32)
    bf[:, 0:P] = np.eye(P)
    ahead = np.triu(np.ones((P, P), np.float32), 1) * -1e30
    bf[:, P:P + 512] = np.tile(ahead, (1, 4))
    o = P + 512
    key = np.zeros((P, GB, TY, P), np.float32)
    qry = np.zeros((P, GB, TY, P), np.float32)
    for b in range(GB):
        for y in range(TY):
            for part in range(3):
                key[32 * b + 8 * part + TY + y, b, y, :] = 1
                qry[32 * b + 8 * part + y, b, y, :] = 1
    bf[:, o:o + 16 * P] = key.reshape(P, -1)
    o += 16 * P
    bf[:, o:o + 4 * 512] = qry.reshape(P, -1)
    o += 4 * 512
    for e in range(E):
        for part in range(3):
            bf[E * part + e, o + e * P:o + (e + 1) * P] = 1
    arr = np.zeros((P, 4, 4, P), np.float32)
    high = {0: (0, 1), 2: (0, 2)}
    for s in (0, 2):
        for g in range(4):
            for r in range(4):
                for copy in range(4):
                    which = s if copy in high[s] else s + 1
                    for d in range(HD):
                        arr[(4 * g + r) * HD + d, which, g, 32 * r + copy * HD + d] = 1
    tri = np.zeros((P, E, E), np.float32)
    tri[:, :, :] = np.tril(np.ones((E, E)), -1)
    f = np.concatenate([np.eye(P, dtype=np.float32), tri.reshape(P, -1), arr.reshape(P, -1)], 1)
    return bf, f.astype(np.float32)


def kernel(**inputs):
    import numpy as np
    import ml_dtypes
    import concourse.bacc as _bacc
    from concourse.bass_utils import run_bass_kernel_spmd as _run

    a = {k: np.asarray(v) for k, v in inputs.items()}
    c = lambda k: a["L0_cond_" + k]
    f = lambda k: a["L0_ffn_" + k]
    column = lambda v: v.reshape(P, 1)
    wT = {}
    wT["pl"], wT["pc"] = c("w_pl").T, c("w_pc").T
    wT["mu1"], wT["mu2"] = c("w_mu").T[:P], c("w_mu").T[P:]
    wT["cb1"], wT["cb2"] = c("w_cb").T[:P], c("w_cb").T[P:]
    for k in range(3):
        wT[f"v{k + 1}"] = c("w_v").T[k * P:(k + 1) * P]
    wT["wq"], wT["wk"] = c("w_q"), c("w_k")
    wT["qin"], wT["pk"], wT["pv"] = c("w_qin").T, c("w_pk").T, c("w_pv").T
    wT["qt"] = np.concatenate([a["fside_BxSxS_0"][t].T for t in range(T)], 1)
    wT["bqt"] = a["mask_BxS_ff0"][:T].T
    wT["wes1"], wT["wes2"] = a["cond_2048"][:TY, :P].T, a["cond_2048"][:TY, P:].T
    wT["qenc"] = a["fside_BxS_0"].T
    wT["init"] = column(c("init_mem"))
    for k in ("qin", "pl", "pc", "q", "k", "v", "pk", "pv", "mu", "cb"):
        wT["b" + k] = column(c("b_" + k))
    wT["wo"] = f("wo")
    wT["vr"] = np.concatenate([f("wv"), f("router_w")], 1)
    wT["w2"] = np.concatenate([f("w2")[k * P:(k + 1) * P] for k in range(FC)], 1)
    wT["ew2"] = np.concatenate([f("ew2")[e] for e in range(E)], 1)
    for k, (lo, hi) in list(COLS.items()) + list(SETUP_COLS.items()):
        assert wT[k].shape == (P, hi - lo), (k, wT[k].shape)
    sp = [f("wq"), f("wk")]
    for e in range(E):
        sp += [f("ew1")[e], f("ew3")[e]]
    for k in range(FC):
        sp += [f("w1")[:, k * P:(k + 1) * P], f("w3")[:, k * P:(k + 1) * P]]
    splits = np.concatenate(sp, 1)
    bf, cf = _constants()
    arrays = {
        "xT": a["x"].transpose(2, 0, 1).reshape(P, B * P),
        "xN": a["x"].transpose(1, 0, 2),
        "adj": a["itok_BxSxS_0_4"].astype(np.int32).transpose(1, 0, 2),
        "msk": a["mask_BxS_ff1"].reshape(1, B * P),
        "setup_w": np.concatenate([wT[k] for k in SETUP_COLS], 1), "wts": np.concatenate([wT[k] for k in COLS], 1),
        "splits": splits,
        "norms": np.stack([f("attn_norm_w"), f("moe_norm_w"), f("ff_norm_w")]),
        "cst_bf": bf.astype(ml_dtypes.bfloat16), "cst_f": cf,
    }
    arrays = {k + "_dram": np.ascontiguousarray(v) for k, v in arrays.items()}
    nc = _bacc.Bacc("TRN2", target_bir_lowering=False, num_devices=1)
    args = [nc.dram_tensor(k, v.shape, mybir.dt.from_np(v.dtype), kind="ExternalInput").ap() for k, v in arrays.items()]
    out = nc.dram_tensor("out_dram", (P, B, P), F32, kind="ExternalOutput").ap()
    build(nc, *args, out)
    r = _run(nc, [arrays], core_ids=[0])
    return np.ascontiguousarray(r.results[0]["out_dram"].transpose(1, 0, 2))
```
